# Optimizing a Trainium2 kernel written in Bass

```python
import numpy as np
import jax
import jax.numpy as jnp

def _softmax(x, axis=-1):
    return jax.nn.softmax(x, axis=axis)
def _gelu(x):
    return jax.nn.gelu(x, approximate=True)
def _silu(x):
    return jax.nn.silu(x)
def _sigmoid(x):
    return jax.nn.sigmoid(x)
def _layernorm(x, axis=-1, eps=1e-5):
    m = jnp.mean(x, axis=axis, keepdims=True)
    v = jnp.var(x, axis=axis, keepdims=True)
    return (x - m) / jnp.sqrt(v + eps)
def _scatter_add(tgt, idx, src, axis=0):
    return tgt.at[idx].add(src)
def _segment_sum(src, seg, n):
    return jax.ops.segment_sum(src, seg, n)

kernel_name = 'mk_vit_tower_d1_tok_img256_5891bf'

def setup_inputs(seed: int = 0):
    np.random.seed(seed)
    _w = jnp.asarray
    def _rec_inputs():
        import jax
        import jax.numpy as jnp
        _rk = jax.random.key(seed)
        x = (-0.000395706 + 0.999959 * jax.random.normal(jax.random.fold_in(_rk, 1), (8, 1, 224, 224), jnp.float32))
        return x
    x = _rec_inputs()
    def _L0_tok_setup():
        import jax, jax.numpy as jnp
        import numpy as np
        IMAGE_SIZE = 224
        PATCH_SIZE = 7
        EMBED_DIM = 256
        NUM_PATCHES = (IMAGE_SIZE // PATCH_SIZE) ** 2
        PATCH_DIM = PATCH_SIZE ** 2
        key = jax.random.key(seed)
        kx, kw, kb, kp = jax.random.split(key, 4)
        x = jax.random.normal(kx, (256, 1, IMAGE_SIZE, IMAGE_SIZE), dtype=jnp.float32)
        bound = 1.0 / np.sqrt(PATCH_DIM)
        W = jax.random.uniform(kw, (EMBED_DIM, PATCH_DIM), minval=-bound, maxval=bound, dtype=jnp.float32)
        b = jax.random.uniform(kb, (EMBED_DIM,), minval=-bound, maxval=bound, dtype=jnp.float32)
        pos = jax.random.uniform(kp, (1, NUM_PATCHES, EMBED_DIM), dtype=jnp.float32)
        return {'x': x, 'W': W, 'b': b, 'pos': pos}
    _L0_tok_all = _L0_tok_setup()
    _L0_tok_in = {k: v for k, v in _L0_tok_all.items() if k in ('W', 'b', 'pos', )}
    del _L0_tok_all

    def _L0_attn_setup():
        import jax, jax.numpy as jnp
        import numpy as np
        B, N, C, H = (4, 1024, 256, 8)
        HD = C // H
        BN_EPS = 1e-05
        key = jax.random.key(seed)
        ks = jax.random.split(key, 6)

        def w(k, shape, sc=0.02):
            return jax.random.normal(k, shape, jnp.float32) * sc
        return {'x': jax.random.normal(ks[0], (B, N, C), jnp.float32), 'w_qkv': w(ks[1], (3 * C, C)), 'b_qkv': jnp.zeros((3 * C,), jnp.float32), 'w_proj': w(ks[2], (C, C)), 'b_proj': jnp.zeros((C,), jnp.float32), 'scale': jnp.float32(HD ** (-0.5)), 'riem_scale': jnp.float32(HD ** (-0.5)), 'grassman_scale': jnp.float32(HD ** (-0.5)), 'bn_gamma': jnp.ones((3 * H,), jnp.float32), 'bn_beta': jnp.zeros((3 * H,), jnp.float32), 'bn_mean': jnp.zeros((3 * H,), jnp.float32), 'bn_var': jnp.ones((3 * H,), jnp.float32), 'conv_w': w(ks[3], (H, 3 * H)), 'conv_b': jnp.zeros((H,), jnp.float32)}
    _L0_attn_all = _L0_attn_setup()
    _L0_attn_in = {k: v for k, v in _L0_attn_all.items() if k in ('w_qkv', 'b_qkv', 'w_proj', 'b_proj', 'scale', 'riem_scale', 'grassman_scale', 'bn_gamma', 'bn_beta', 'bn_mean', 'bn_var', 'conv_w', 'conv_b', )}
    del _L0_attn_all

    def _L0_ffn_setup():
        import jax, jax.numpy as jnp
        import numpy as np
        E = 8
        K = 2
        D = 256
        H = 512
        DOUT = 256
        EPS = 1e-05
        key = jax.random.key(seed)
        ks = jax.random.split(key, 9)
        s = 0.02
        return {'x': jax.random.normal(ks[0], (4, 8192, D), jnp.float32), 'gamma': 1.0 + 0.05 * jax.random.normal(ks[1], (D,), jnp.float32), 'beta': 0.05 * jax.random.normal(ks[2], (D,), jnp.float32), 'Wr': 0.01 * jax.random.normal(ks[3], (D, E), jnp.float32), 'br': jnp.zeros((E,), jnp.float32), 'W1': s * jax.random.normal(ks[4], (E, D, H), jnp.float32), 'b1': s * jax.random.normal(ks[5], (E, H), jnp.float32), 'W2': s * jax.random.normal(ks[6], (E, H, DOUT), jnp.float32), 'b2': s * jax.random.normal(ks[7], (E, DOUT), jnp.float32)}
    _L0_ffn_all = _L0_ffn_setup()
    _L0_ffn_in = {k: v for k, v in _L0_ffn_all.items() if k in ('gamma', 'beta', 'Wr', 'br', 'W1', 'b1', 'W2', 'b2', )}
    del _L0_ffn_all

    return {
        "x": x,
        "L0_tok_W": _L0_tok_in["W"],
        "L0_tok_b": _L0_tok_in["b"],
        "L0_tok_pos": _L0_tok_in["pos"],
        "L0_attn_w_qkv": _L0_attn_in["w_qkv"],
        "L0_attn_b_qkv": _L0_attn_in["b_qkv"],
        "L0_attn_w_proj": _L0_attn_in["w_proj"],
        "L0_attn_b_proj": _L0_attn_in["b_proj"],
        "L0_attn_scale": _L0_attn_in["scale"],
        "L0_attn_riem_scale": _L0_attn_in["riem_scale"],
        "L0_attn_grassman_scale": _L0_attn_in["grassman_scale"],
        "L0_attn_bn_gamma": _L0_attn_in["bn_gamma"],
        "L0_attn_bn_beta": _L0_attn_in["bn_beta"],
        "L0_attn_bn_mean": _L0_attn_in["bn_mean"],
        "L0_attn_bn_var": _L0_attn_in["bn_var"],
        "L0_attn_conv_w": _L0_attn_in["conv_w"],
        "L0_attn_conv_b": _L0_attn_in["conv_b"],
        "L0_ffn_gamma": _L0_ffn_in["gamma"],
        "L0_ffn_beta": _L0_ffn_in["beta"],
        "L0_ffn_Wr": _L0_ffn_in["Wr"],
        "L0_ffn_br": _L0_ffn_in["br"],
        "L0_ffn_W1": _L0_ffn_in["W1"],
        "L0_ffn_b1": _L0_ffn_in["b1"],
        "L0_ffn_W2": _L0_ffn_in["W2"],
        "L0_ffn_b2": _L0_ffn_in["b2"],
    }

def reference(x, L0_tok_W, L0_tok_b, L0_tok_pos, L0_attn_w_qkv, L0_attn_b_qkv, L0_attn_w_proj, L0_attn_b_proj, L0_attn_scale, L0_attn_riem_scale, L0_attn_grassman_scale, L0_attn_bn_gamma, L0_attn_bn_beta, L0_attn_bn_mean, L0_attn_bn_var, L0_attn_conv_w, L0_attn_conv_b, L0_ffn_gamma, L0_ffn_beta, L0_ffn_Wr, L0_ffn_br, L0_ffn_W1, L0_ffn_b1, L0_ffn_W2, L0_ffn_b2):
    import jax
    import jax.numpy as jnp
    def _L0_tok_ref(x, W, b, pos):
        import jax, jax.numpy as jnp
        import numpy as np
        IMAGE_SIZE = 224
        PATCH_SIZE = 7
        EMBED_DIM = 256
        NUM_PATCHES = (IMAGE_SIZE // PATCH_SIZE) ** 2
        PATCH_DIM = PATCH_SIZE ** 2
        B = x.shape[0]
        p = PATCH_SIZE
        n = IMAGE_SIZE // p
        patches = x.reshape(B, n, p, n, p).transpose(0, 1, 3, 2, 4).reshape(B, n * n, p * p)
        out = jnp.einsum('bnd,ed->bne', patches, W) + b + pos
        return out

    def _L0_attn_ref(x, w_qkv, b_qkv, w_proj, b_proj, scale, riem_scale, grassman_scale, bn_gamma, bn_beta, bn_mean, bn_var, conv_w, conv_b):
        import jax, jax.numpy as jnp
        import numpy as np
        B, N, C, H = (4, 1024, 256, 8)
        HD = C // H
        BN_EPS = 1e-05
        b, n, c = x.shape
        h, hd = (H, c // H)
        qkv = (x @ w_qkv.T + b_qkv).reshape(b, n, 3, h, hd).transpose(2, 0, 3, 1, 4)
        q, k, v = (qkv[0], qkv[1], qkv[2])
        qgr, _ = jnp.linalg.qr(q)
        kgr, _ = jnp.linalg.qr(k)
        attn_grass = jnp.einsum('bhnd,bhmd->bhnm', qgr, kgr) ** 2 * grassman_scale
        dots = jnp.einsum('bhnd,bhmd->bhnm', q, k)
        attn_eucl = dots * scale
        attn_riem = dots ** 2 * riem_scale
        a = jnp.concatenate([attn_eucl, attn_riem, attn_grass], axis=1)
        inv = (bn_gamma * jax.lax.rsqrt(bn_var + BN_EPS))[:, None, None]
        a = (a - bn_mean[:, None, None]) * inv + bn_beta[:, None, None]
        a = jnp.einsum('oc,bcnm->bonm', conv_w, a) + conv_b[None, :, None, None]
        a = jax.nn.softmax(a, axis=-1)
        out = jnp.einsum('bhnm,bhmd->bhnd', a, v)
        out = out.transpose(0, 2, 1, 3).reshape(b, n, c)
        return out @ w_proj.T + b_proj

    def _L0_ffn_ref(x, gamma, beta, Wr, br, W1, b1, W2, b2):
        import jax, jax.numpy as jnp
        import numpy as np
        E = 8
        K = 2
        D = 256
        H = 512
        DOUT = 256
        EPS = 1e-05
        mu = jnp.mean(x, axis=-1, keepdims=True)
        var = jnp.mean(jnp.square(x - mu), axis=-1, keepdims=True)
        xn = (x - mu) * jax.lax.rsqrt(var + EPS) * gamma + beta
        logits = jnp.einsum('bsd,de->bse', xn, Wr) + br
        top_vals, top_idx = jax.lax.top_k(logits, K)
        w = jax.nn.softmax(top_vals, axis=-1)
        w_full = jnp.einsum('bsk,bske->bse', w, jax.nn.one_hot(top_idx, E, dtype=w.dtype))
        y = jnp.zeros(x.shape[:-1] + (DOUT,), x.dtype)
        for e in range(E):
            h = jax.nn.gelu(jnp.einsum('bsd,dh->bsh', xn, W1[e]) + b1[e], approximate=False)
            y_e = jnp.einsum('bsh,hd->bsd', h, W2[e]) + b2[e]
            y = y + y_e * w_full[..., e, None]
        return y

    h = _L0_tok_ref(x, L0_tok_W, L0_tok_b, L0_tok_pos)
    h = h + _L0_attn_ref(_layernorm(h, axis=-1), L0_attn_w_qkv, L0_attn_b_qkv, L0_attn_w_proj, L0_attn_b_proj, L0_attn_scale, L0_attn_riem_scale, L0_attn_grassman_scale, L0_attn_bn_gamma, L0_attn_bn_beta, L0_attn_bn_mean, L0_attn_bn_var, L0_attn_conv_w, L0_attn_conv_b)
    h = h + _L0_ffn_ref(_layernorm(h, axis=-1), L0_ffn_gamma, L0_ffn_beta, L0_ffn_Wr, L0_ffn_br, L0_ffn_W1, L0_ffn_b1, L0_ffn_W2, L0_ffn_b2)
    return h


_drawn_inputs = setup_inputs


def setup_inputs(seed=0):
    import zlib

    import numpy as np

    out = dict(_drawn_inputs(seed))
    spreads = {'L0_attn_b_qkv': (0.0, 0.1),
     'L0_attn_b_proj': (0.0, 0.1),
     'L0_attn_bn_gamma': (1.0, 0.6),
     'L0_attn_bn_beta': (0.0, 0.8),
     'L0_attn_bn_mean': (0.0, 0.8),
     'L0_attn_bn_var': (1.0, 0.6),
     'L0_attn_conv_b': (0.0, 0.8),
     'L0_ffn_br': (0.0, 0.1)}
    factors = {'L0_attn_w_qkv': 3.018,
     'L0_attn_conv_w': 8.0,
     'L0_ffn_gamma': 4.92,
     'L0_ffn_beta': 4.062,
     'L0_ffn_b1': 8.0,
     'L0_ffn_b2': 3.518}
    for name, (base, spread) in spreads.items():
        noise = np.random.default_rng([zlib.crc32(name.encode()), seed]).standard_normal(out[name].shape)
        drawn = base * np.exp(spread * noise) if base else spread * noise
        out[name] = jnp.asarray(drawn.astype(out[name].dtype))
    for name, factor in factors.items():
        out[name] = (out[name] * factor).astype(out[name].dtype)
    return out
```

```python
from contextlib import ExitStack

import concourse.bass as bass
from concourse import mybir

F32 = mybir.dt.float32
F16 = mybir.dt.float16
ALU = mybir.AluOpType
ACT = mybir.ActivationFunctionType
AX_X = mybir.AxisListType.X
ds = bass.ds

P = 128
B = 8
N = 1024
C = 256
H = 8
HD = C // H
NT = N // P
TILES = B * NT
CK = C // P
PD = 49
E = 8
F = 512
EPS = 1e-5
GR = 32.0
GS = 16
NG = P // GS


class Count:

    def __init__(self, sem, per=1, credit=0):
        self.sem, self.per, self.credit = sem, per, credit

    def start(self, eng):
        eng.sem_inc(self.sem, self.per * self.credit)

    def done(self, t):
        return (t + (1 + self.credit)) * self.per

    def freed(self, t, depth):
        assert depth <= self.credit
        return (t + (1 + self.credit - depth)) * self.per


class Maker:

    def __init__(self, nc, ctx, prefix):
        self.nc, self.ctx, self.prefix = nc, ctx, prefix

    def sb(self, name, shape, dt=F32):
        return self.ctx.enter_context(self.nc.sbuf_tensor(f"{self.prefix}_{name}", shape, dt))

    def ps(self, name, shape, dt=F32):
        return self.ctx.enter_context(self.nc.psum_tensor(f"{self.prefix}_{name}", shape, dt))

    def count(self, name, per=1, credit=0):
        return Count(self.ctx.enter_context(self.nc.semaphore(f"{self.prefix}_{name}")), per, credit)


def embed_and_project(nc, a, dr, hs):
    with ExitStack() as ctx:
        m = Maker(nc, ctx, "p1")
        tok_w = m.sb("tok_w", [PD, C])
        pos_b = m.sb("pos_b", [P, NT, C])
        tok_b = m.sb("tok_b", [P, C])
        w_qkv = m.sb("w_qkv", [P, CK, 3 * C])
        b_qkv = m.sb("b_qkv", [P, 3 * C])
        ident = m.sb("ident", [P, P])
        pat = m.sb("pat", [PD, N])
        hc = m.sb("hc", [P, 2, C])
        stats = m.sb("stats", [P, 2, 6])
        mv = m.sb("mv", [P, 2, 2])
        veps = m.sb("veps", [P, 2])
        rstd = m.sb("rstd", [P, 2])
        mhalf = m.sb("mhalf", [P, 1])
        eps = m.sb("eps", [P, 1])
        z = m.sb("z", [P, 2, C])
        zt = m.sb("zt", [P, 2, CK, P])
        qk = m.sb("qk", [P, 2, 2 * C])
        vs = m.sb("vs", [P, 2, C])
        qt = m.sb("qt", [P, 2, 4, P])
        gram = m.sb("gram", [P, 4, HD])

        ps_tok = m.ps("ps_tok", [P, 1, 512])
        ps_zt = m.ps("ps_zt", [P, CK, 256])
        ps_qk = m.ps("ps_qk", [P, 512])
        ps_v = m.ps("ps_v", [P, 512])
        ps_qt = m.ps("ps_qt", [P, 4, P])
        ps_gram = m.ps("ps_gram", [P, 512])

        weights = m.count("weights", 16 * 6)
        pat_in = m.count("pat_in", 16)
        posb_ready = m.count("posb_ready")
        half_ready = m.count("half_ready")
        tok_mm = m.count("tok_mm")
        h_done = m.count("h_done", credit=1)
        st_done = m.count("st_done")
        mv_done = m.count("mv_done")
        ve_done = m.count("ve_done")
        rstd_done = m.count("rstd_done", credit=0)
        z_done = m.count("z_done")
        zt_mm = m.count("zt_mm", credit=2)
        ztc_done = m.count("ztc_done", credit=1)
        qkv_mm = m.count("qkv_mm", credit=2)
        qk_done = m.count("qk_done", credit=1)
        v_done = m.count("v_done", credit=1)
        qt_mm = m.count("qt_mm")
        gram_mm = m.count("gram_mm", credit=2)
        qtc_done = m.count("qtc_done", credit=1)
        gramc_done = m.count("gramc_done", credit=1)
        v_store = [m.count(f"v_store{k}", 16, credit=1) for k in range(2)]
        qt_store = [m.count(f"qt_store{k}", 16, credit=1) for k in range(2)]
        a1_store = m.count("a1_store", 16, credit=1)
        h_store = [m.count(f"h_store{k}", 16, credit=1) for k in range(2)]
        gr_store = m.count("gr_store", 16, credit=1)

        block = ctx.enter_context(nc.Block())

        @block.sync
        def _(sp):
            sp.dma_start(tok_w[:], a["tok_w"]).then_inc(weights.sem, 16)
            sp.dma_start(pos_b[:], a["pos"]).then_inc(weights.sem, 16)
            sp.dma_start(tok_b[:], a["tok_b"]).then_inc(weights.sem, 16)
            sp.dma_start(w_qkv[:], a["w_qkv"]).then_inc(weights.sem, 16)
            sp.dma_start(b_qkv[:], a["b_qkv"]).then_inc(weights.sem, 16)
            sp.dma_start(ident[:], a["ident"]).then_inc(weights.sem, 16)
            for stores in (*v_store, *qt_store, *h_store, a1_store, gr_store):
                stores.start(sp)
            sp.dma_start(pat[:], a["pat"][0]).then_inc(pat_in.sem, 16)
            with sp.Fori(0, B) as b:
                for t in range(NT):
                    T = b * NT + t
                    sp.wait_ge(h_done.sem, h_done.done(T))
                    sp.dma_start(hs[:, ds(T, 1), :], hc[:, t % 2, :]).then_inc(h_store[t % 2].sem, 16)
                    sp.wait_ge(v_done.sem, v_done.done(T))
                    sp.dma_start(dr["v"][ds(b, 1), :, t, :], vs[:, t % 2, :]).then_inc(v_store[t % 2].sem, 16)
                    if t == 0:
                        sp.dma_start(dr["top"][ds(b, 1), :, :], qk[0:HD, 0, :]).then_inc(a1_store.sem, 16)
                    sp.wait_ge(qtc_done.sem, qtc_done.done(T))
                    sp.dma_start(dr["qt"][ds(b, 1), :, :, t * P:(t + 1) * P], qt[:, t % 2]).then_inc(qt_store[t % 2].sem, 16)
                sp.wait_ge(gramc_done.sem, gramc_done.done(b))
                sp.dma_start(dr["gram"][ds(b, 1)], gram[:]).then_inc(gr_store.sem, 16)
            for stores in (*v_store, *qt_store, *h_store):
                sp.wait_ge(stores.sem, stores.done(TILES // 2 - 1))
            sp.wait_ge(a1_store.sem, a1_store.done(B - 1))
            sp.wait_ge(gr_store.sem, gr_store.done(B - 1))

        @block.gpsimd
        def _(pool):
            nc.gpsimd.memset(mhalf[:], -0.5).then_inc(half_ready.sem, 1)
            nc.gpsimd.memset(eps[:], EPS).then_inc(half_ready.sem, 1)
            pool.wait_ge(half_ready.sem, 2)
            with pool.Fori(0, B) as b:
                for t in range(NT):
                    T = b * NT + t
                    pool.wait_ge(mv_done.sem, mv_done.done(T))
                    nc.gpsimd.tensor_tensor(veps[:, t % 2:t % 2 + 1], mv[:, t % 2, 1:2], eps[:],
                                            ALU.add).then_inc(ve_done.sem, 1)
                    pool.wait_ge(ve_done.sem, ve_done.done(T))
                    nc.gpsimd.tensor_tensor(rstd[:, t % 2:t % 2 + 1], veps[:, t % 2:t % 2 + 1], mhalf[:],
                                            ALU.pow).then_inc(rstd_done.sem, 1)

        @block.scalar
        def _(act):
            ztc_done.start(act)
            qtc_done.start(act)
            gramc_done.start(act)
            with act.Fori(0, B) as b:
                for t in range(NT):
                    T = b * NT + t
                    if t == NT - 1:
                        act.wait_ge(tok_mm.sem, tok_mm.done(T))
                        act.dma_start(pat[:], a["pat"][ds(b + 1, 1)]).then_inc(pat_in.sem, 16)
                    act.wait_ge(zt_mm.sem, zt_mm.done(T))
                    act.wait_ge(qkv_mm.sem, qkv_mm.freed(T, 2))
                    nc.scalar.copy(zt[:, t % 2], ps_zt[:, :, 0:P]).then_inc(ztc_done.sem, 1)
                    act.wait_ge(qt_mm.sem, qt_mm.done(T))
                    slot = qt_store[t % 2]
                    act.wait_ge(slot.sem, slot.freed(b * (NT // 2) + t // 2, 1))
                    nc.scalar.copy(qt[:, t % 2], ps_qt[:]).then_inc(qtc_done.sem, 1)
                act.wait_ge(gram_mm.sem, gram_mm.done(b * NT + (NT - 1)))
                act.wait_ge(gr_store.sem, gr_store.freed(b, 1))
                nc.scalar.copy(gram[:], ps_gram[:, 0:4 * HD].rearrange("p (g j) -> p g j", g=4)).then_inc(gramc_done.sem, 1)
            act.wait_ge(pat_in.sem, pat_in.done(B))

        @block.vector
        def _(dve):
            h_done.start(dve)
            qk_done.start(dve)
            v_done.start(dve)
            dve.wait_ge(weights.sem, weights.done(0))
            for t in range(NT):
                last = nc.vector.tensor_tensor(pos_b[:, t], pos_b[:, t], tok_b[:], ALU.add)
            last.then_inc(posb_ready.sem, 1)
            dve.wait_ge(posb_ready.sem, 1)

            def head(T, t):
                dve.wait_ge(tok_mm.sem, tok_mm.done(T))
                slot = h_store[t % 2]
                dve.wait_ge(slot.sem, slot.freed(b * (NT // 2) + t // 2, 1))
                nc.vector.tensor_tensor(hc[:, t % 2, :], ps_tok[:, 0, 0:C], pos_b[:, t, :],
                                        ALU.add).then_inc(h_done.sem, 1)
                dve.wait_ge(h_done.sem, h_done.done(T))
                nc.vector.bn_stats(stats[:, t % 2, :], hc[:, t % 2, :]).then_inc(st_done.sem, 1)
                dve.wait_ge(posb_ready.sem, 1)
                dve.wait_ge(st_done.sem, st_done.done(T))
                nc.vector.bn_aggr(mv[:, t % 2, :], stats[:, t % 2, :]).then_inc(mv_done.sem, 1)

            def tail(T, t):
                dve.wait_ge(qkv_mm.sem, qkv_mm.done(T))
                dve.wait_ge(gram_mm.sem, gram_mm.freed(T, 2))
                if t == 0:
                    dve.wait_ge(a1_store.sem, a1_store.done(b - 1))
                if t == 2:
                    dve.wait_ge(a1_store.sem, a1_store.done(b))
                nc.vector.tensor_tensor(qk[:, t % 2, :], ps_qk[:], b_qkv[:, 0:2 * C], ALU.add).then_inc(qk_done.sem, 1)
                slot = v_store[t % 2]
                dve.wait_ge(slot.sem, slot.freed(b * (NT // 2) + t // 2, 1))
                nc.vector.tensor_tensor(vs[:, t % 2, :], ps_v[:, 0:C], b_qkv[:, 2 * C:3 * C],
                                        ALU.add).then_inc(v_done.sem, 1)

            with dve.Fori(0, B) as b:
                for t in range(NT):
                    T = b * NT + t
                    head(T, t)
                    dve.wait_ge(rstd_done.sem, rstd_done.done(T))
                    dve.wait_ge(zt_mm.sem, zt_mm.freed(T, 2))
                    nc.vector.tensor_scalar(z[:, t % 2, :], hc[:, t % 2, :], mv[:, t % 2, 0:1],
                                            rstd[:, t % 2:t % 2 + 1], ALU.subtract, ALU.mult).then_inc(z_done.sem, 1)
                    tail(T, t)

        @block.tensor
        def _(pe):
            zt_mm.start(pe)
            qkv_mm.start(pe)
            gram_mm.start(pe)
            pe.wait_ge(weights.sem, weights.done(0))

            def tokens(b, t):
                T = b * NT + t
                if t == 0:
                    pe.wait_ge(pat_in.sem, pat_in.done(b))
                pe.wait_ge(h_done.sem, h_done.freed(T, 1))
                pe.matmul(ps_tok[:, 0, 0:C], pat[:, t * P:(t + 1) * P], tok_w[:], start=True,
                          stop=True).then_inc(tok_mm.sem, 1)

            def grams(b, t):
                T = b * NT + t
                pe.wait_ge(qk_done.sem, qk_done.done(T))
                pe.wait_ge(qtc_done.sem, qtc_done.freed(T, 1))
                for g in range(4):
                    last = pe.transpose(ps_qt[:, g, :], qk[:, t % 2, g * P:(g + 1) * P], ident[:])
                last.then_inc(qt_mm.sem, 1)
                if t == 0:
                    pe.wait_ge(gramc_done.sem, gramc_done.freed(b, 1))
                for g in range(4):
                    for j in range(4):
                        w = qk[:, t % 2, g * P + j * HD:g * P + (j + 1) * HD]
                        last = pe.matmul(ps_gram[j * HD:(j + 1) * HD, g * HD:(g + 1) * HD], w, w,
                                         start=(t == 0 and g == 0), stop=(t == NT - 1), skip_group_check=True)
                last.then_inc(gram_mm.sem, 1)

            with pe.Fori(0, B) as b:
                tokens(b, 0)
                for t in range(NT):
                    T = b * NT + t
                    pe.wait_ge(z_done.sem, z_done.done(T))
                    pe.wait_ge(ztc_done.sem, ztc_done.freed(T, 1))
                    for c in range(CK):
                        last = pe.transpose(ps_zt[:, c, 0:P], z[:, t % 2, c * P:(c + 1) * P], ident[:])
                    last.then_inc(zt_mm.sem, 1)
                    if t < NT - 1:
                        tokens(b, t + 1)
                    if t:
                        grams(b, t - 1)
                    pe.wait_ge(ztc_done.sem, ztc_done.done(T))
                    pe.wait_ge(v_done.sem, v_done.freed(T, 1))
                    for c in range(CK):
                        pe.matmul(ps_qk[:], zt[:, t % 2, c, :], w_qkv[:, c, 0:2 * C], start=(c == 0), stop=(c == CK - 1))
                    for c in range(CK):
                        last = pe.matmul(ps_v[:, 0:C], zt[:, t % 2, c, :], w_qkv[:, c, 2 * C:3 * C], start=(c == 0),
                                         stop=(c == CK - 1))
                    last.then_inc(qkv_mm.sem, 1)
                grams(b, NT - 1)


def orthonormal_factors(nc, a, dr):
    with ExitStack() as ctx:
        m = Maker(nc, ctx, "qr")
        g = m.sb("g", [P, HD, HD])
        top = m.sb("top", [P, HD, HD])
        li = m.sb("li", [P, HD, HD])
        lt = m.sb("lt", [P, HD, HD])
        lcol = m.sb("lcol", [P, HD, HD])
        outer = m.sb("outer", [P, HD * HD])
        outer_z = m.sb("outer_z", [P, HD * HD])
        piv = m.sb("piv", [P, HD])
        rpiv = m.sb("rpiv", [P, HD])
        half = m.sb("half", [P, HD])
        root = m.sb("root", [P, HD])
        rroot = m.sb("rroot", [P, HD])
        beta = m.sb("beta", [P, HD])
        rbeta = m.sb("rbeta", [P, HD])
        flip = m.sb("flip", [P, HD])
        den = m.sb("den", [P, HD])
        w = m.sb("w", [P, HD])

        loaded = m.count("loaded", 16 * (1 + B))
        ready = m.count("ready")
        chain = m.ctx.enter_context(nc.semaphore("qr_chain"))
        col_done = m.count("col_done")
        z_done = m.count("z_done")
        zo_done = m.count("zo_done")
        piv_done = m.count("piv_done")
        root_done = m.count("root_done")
        out_done = m.count("out_done")
        stored = m.count("stored", 16)
        block = ctx.enter_context(nc.Block())

        @block.sync
        def _(sp):
            sp.dma_start(g[:], dr["gram_m"]).then_inc(loaded.sem, 16)
            for b in range(B):
                sp.dma_start(top[b * 2 * H:(b + 1) * 2 * H], dr["top_m"][b]).then_inc(loaded.sem, 16)
            sp.wait_ge(out_done.sem, 1)
            sp.dma_start(dr["rt_m"], lt[:]).then_inc(stored.sem, 16)
            sp.wait_ge(stored.sem, 16)

        @block.gpsimd
        def _(pool):
            nc.gpsimd.memset(li[:], 0.0).then_inc(ready.sem, 1)
            pool.wait_ge(ready.sem, 1)
            for j in range(HD):
                last = nc.gpsimd.memset(li[:, j, j:j + 1], 1.0)
            last.then_inc(ready.sem, 1)
            pool.wait_ge(ready.sem, 2)
            nc.gpsimd.memset(half[:], 0.5).then_inc(ready.sem, 1)
            pool.wait_ge(ready.sem, 3)
            for j in range(HD - 1):
                n = HD - 1 - j
                pool.wait_ge(col_done.sem, j + 1)
                if j:
                    pool.wait_ge(z_done.sem, j)
                o = outer_z[:, 0:n * (j + 1)].rearrange("p (i k) -> p i k", i=n)
                nc.gpsimd.tensor_tensor(o, lcol[:, j, j + 1:HD].unsqueeze(2).broadcast_to([P, n, j + 1]),
                                        li[:, j:j + 1, 0:j + 1].broadcast_to([P, n, j + 1]), ALU.mult).then_inc(zo_done.sem, 1)
                pool.wait_ge(zo_done.sem, j + 1)
                nc.gpsimd.tensor_tensor(li[:, j + 1:HD, 0:j + 1], li[:, j + 1:HD, 0:j + 1], o,
                                        ALU.subtract).then_inc(z_done.sem, 1)
            pool.wait_ge(piv_done.sem, 1)
            nc.gpsimd.tensor_tensor(root[:], piv[:], half[:], ALU.pow).then_inc(root_done.sem, 1)

        @block.vector
        def _(dve):
            steps = [0]

            def link(ins):
                steps[0] += 1
                ins.then_inc(chain, 1)
                dve.wait_ge(chain, steps[0])

            dve.wait_ge(loaded.sem, loaded.done(0))
            dve.wait_ge(ready.sem, 3)
            for j in range(HD):
                n = HD - 1 - j
                link(nc.vector.tensor_scalar(piv[:, j:j + 1], g[:, j, j:j + 1], 1e-30, None, ALU.max))
                link(nc.vector.reciprocal(rpiv[:, j:j + 1], piv[:, j:j + 1]))
                if not n:
                    break
                nc.vector.tensor_scalar(lcol[:, j, j + 1:HD], g[:, j, j + 1:HD], rpiv[:, j:j + 1], None,
                                        ALU.mult).then_inc(col_done.sem, 1)
                dve.wait_ge(col_done.sem, j + 1)
                o = outer[:, 0:n * n].rearrange("p (i k) -> p i k", i=n)
                link(nc.vector.tensor_tensor(o, lcol[:, j, j + 1:HD].unsqueeze(2).broadcast_to([P, n, n]),
                                             g[:, j:j + 1, j + 1:HD].broadcast_to([P, n, n]), ALU.mult))
                link(nc.vector.tensor_tensor(g[:, j + 1:HD, j + 1:HD], g[:, j + 1:HD, j + 1:HD], o, ALU.subtract))
            nc.vector.tensor_scalar(flip[:, 0:1], piv[:, 0:1], 0.0, None, ALU.mult).then_inc(piv_done.sem, 1)
            dve.wait_ge(root_done.sem, 1)
            link(nc.vector.reciprocal(rroot[:], root[:]))
            for j in range(HD):
                n = HD - 1 - j
                c = slice(j, j + 1)
                link(nc.vector.tensor_scalar(flip[:, c], top[:, j, c], 0.0, -2.0, ALU.is_ge, ALU.mult))
                link(nc.vector.tensor_scalar(flip[:, c], flip[:, c], 1.0, None, ALU.add))
                nc.vector.tensor_tensor(beta[:, c], flip[:, c], root[:, c], ALU.mult)
                link(nc.vector.tensor_tensor(rbeta[:, c], flip[:, c], rroot[:, c], ALU.mult))
                if not n:
                    break
                link(nc.vector.tensor_tensor(den[:, c], beta[:, c], top[:, j, c], ALU.subtract))
                link(nc.vector.reciprocal(den[:, c], den[:, c]))
                link(nc.vector.scalar_tensor_tensor(w[:, 0:n], g[:, j, j + 1:HD], rbeta[:, c], top[:, j, j + 1:HD],
                                                    ALU.mult, ALU.subtract))
                link(nc.vector.tensor_scalar(w[:, 0:n], w[:, 0:n], den[:, c], None, ALU.mult))
                o = outer[:, 0:n * n].rearrange("p (i k) -> p i k", i=n)
                link(nc.vector.tensor_tensor(o, top[:, j + 1:HD, c].broadcast_to([P, n, n]),
                                             w[:, 0:n].unsqueeze(1).broadcast_to([P, n, n]), ALU.mult))
                link(nc.vector.tensor_tensor(top[:, j + 1:HD, j + 1:HD], top[:, j + 1:HD, j + 1:HD], o, ALU.subtract))
            dve.wait_ge(z_done.sem, HD - 1)
            nc.vector.tensor_tensor(lt[:].rearrange("p k i -> p i k"), li[:], rbeta[:].unsqueeze(2).broadcast_to([P, HD, HD]),
                                    ALU.mult).then_inc(out_done.sem, 1)


def split_operands(nc, a, dr):
    with ExitStack() as ctx:
        m = Maker(nc, ctx, "p2")
        rt = m.sb("rt", [P, 2, 4, P])
        qt = m.sb("qt", [P, 2, 4, N])
        hi = m.sb("hi", [P, 2, 2, 4, N], F16)
        lo = m.sb("lo", [P, 2, 2, 4, N], F16)
        ps = [m.ps(f"ps{k}", [P, 512]) for k in range(4)]
        zeroed = m.count("zeroed")
        qt_in = [m.count(f"qt_in{s}", 16 * 5) for s in range(2)]
        mm = m.count("mm")
        img_mm = m.count("img_mm", credit=2)
        hi_o = m.count("hi_o")
        lo_o = m.count("lo_o", credit=4)
        hi_q = m.count("hi_q", credit=2)
        lo_q = m.count("lo_q", credit=2)
        stores = [m.count(f"stores{s}", 16 * 16, credit=1) for s in range(2)]
        block = ctx.enter_context(nc.Block())

        @block.sync
        def _(sp):
            for s in range(2):
                stores[s].start(sp)
            sp.wait_ge(zeroed.sem, 1)
            with sp.Fori(0, B // 2) as b2:
                for s in range(2):
                    b = b2 * 2 + s
                    sp.wait_ge(img_mm.sem, img_mm.freed(b, 2))
                    sp.wait_ge(lo_q.sem, lo_q.freed(b, 2))
                    sp.dma_start(qt[:, s], dr["qt"][ds(b, 1)]).then_inc(qt_in[s].sem, 16)
                    for j in range(4):
                        sp.dma_start(rt[j * HD:(j + 1) * HD, s, :, j * HD:(j + 1) * HD],
                                     dr["rt"][ds(b, 1), j]).then_inc(qt_in[s].sem, 16)

        @block.gpsimd
        def _(pool):
            lo_q.start(pool)
            nc.gpsimd.memset(rt[:], 0.0).then_inc(zeroed.sem, 1)
            with pool.Fori(0, B // 2) as b2:
                for s in range(2):
                    b = b2 * 2 + s
                    pool.wait_ge(hi_q.sem, hi_q.done(b))
                    nc.gpsimd.tensor_tensor(lo[:, s, 0], qt[:, s], hi[:, s, 0], ALU.subtract).then_inc(lo_q.sem, 1)

        @block.scalar
        def _(act):
            hi_q.start(act)
            with act.Fori(0, B // 2) as b2:
                for s in range(2):
                    b = b2 * 2 + s
                    act.wait_ge(qt_in[s].sem, qt_in[s].done(b2))
                    act.wait_ge(stores[s].sem, stores[s].freed(b2, 1))
                    nc.scalar.copy(hi[:, s, 0], qt[:, s]).then_inc(hi_q.sem, 1)
                    for g in range(4):
                        for n in range(2):
                            u = b * 8 + (2 * g + n)
                            act.wait_ge(mm.sem, mm.done(u))
                            nc.scalar.mul(hi[:, s, 1, g, n * 512:(n + 1) * 512], ps[(2 * g + n) % 4][:], GR).then_inc(hi_o.sem, 1)
                    act.wait_ge(lo_q.sem, lo_q.done(b))
                    act.wait_ge(lo_o.sem, lo_o.done(b * 8 + 7))
                    act.wait_ge(hi_o.sem, hi_o.done(b * 8 + 7))
                    act.wait_ge(hi_q.sem, hi_q.done(b))
                    for y in range(2):
                        for kind in range(2):
                            for part, tile in ((0, hi), (1, lo)):
                                for pr in range(2):
                                    act.dma_start(dr["parts_st"][ds(b, 1), y, :, kind, part, pr],
                                                  tile[pr * 64:(pr + 1) * 64, s, kind, 2 * y:2 * y + 2, :]
                                                  ).then_inc(stores[s].sem, 16)
            for s in range(2):
                act.wait_ge(stores[s].sem, stores[s].done(B // 2 - 1))

        @block.vector
        def _(dve):
            lo_o.start(dve)
            with dve.Fori(0, B // 2) as b2:
                for s in range(2):
                    b = b2 * 2 + s
                    for g in range(4):
                        for n in range(2):
                            u = b * 8 + (2 * g + n)
                            dve.wait_ge(hi_o.sem, hi_o.done(u))
                            c = slice(n * 512, (n + 1) * 512)
                            nc.vector.scalar_tensor_tensor(lo[:, s, 1, g, c], ps[(2 * g + n) % 4][:], GR, hi[:, s, 1, g, c],
                                                           ALU.mult, ALU.subtract).then_inc(lo_o.sem, 1)

        @block.tensor
        def _(pe):
            img_mm.start(pe)
            with pe.Fori(0, B // 2) as b2:
                for s in range(2):
                    b = b2 * 2 + s
                    pe.wait_ge(qt_in[s].sem, qt_in[s].done(b2))
                    for g in range(4):
                        for n in range(2):
                            u = b * 8 + (2 * g + n)
                            pe.wait_ge(lo_o.sem, lo_o.freed(u, 4))
                            last = pe.matmul(ps[(2 * g + n) % 4][:], rt[:, s, g, :], qt[:, s, g, n * 512:(n + 1) * 512],
                                             start=True, stop=True).then_inc(mm.sem, 1)
                    pe.wait_ge(mm.sem, mm.done(b * 8 + 7))
                    pe.sem_inc(img_mm.sem, 1)


def attention(nc, a, dr, hs):
    with ExitStack() as ctx:
        m = Maker(nc, ctx, "p3")
        NB = B * NT
        ident = m.sb("ident", [P, P])
        w_proj = m.sb("w_proj", [P, CK, C])
        b_proj = m.sb("b_proj", [P, 1, C])
        mix_w = m.sb("mix_w", [P, 3, H])
        bn = m.sb("bn", [P, 5, 3])
        mask = m.sb("mask", [P, GS])
        conv_b = m.sb("conv_b", [P, 1])
        half = m.sb("half", [P, 3])
        eps = m.sb("eps", [P, 3])
        ones = m.sb("ones", [P, 1])
        one = m.sb("one", [P, 1], F16)
        coef = m.sb("coef", [P, 4, 3])
        cw = m.sb("cw", [P, 2, 3, H])
        mixer = m.sb("mixer", [P, 3, H, GS])
        shifter = m.sb("shifter", [P, 3, H, GS])
        const = m.sb("const", [P, 1])
        keys = m.sb("keys", [P, 2, 4, N], F16)
        v = m.sb("v", [P, NT, C])
        q_in = m.sb("q_in", [P, 16, P], F16)
        q_bd = m.sb("q_bd", [P, 16, NG, 2 * GS], F16)
        s_d = m.sb("s_d", [P, 4, 512])
        s_dd = m.sb("s_dd", [P, 4, 512])
        s_gg = m.sb("s_gg", [P, 4, 512])
        mx = m.sb("mx", [P, 2, 2])
        mxc = m.sb("mxc", [P, 2])
        bias = m.sb("bias", [P, 2])
        p = m.sb("p", [P, 2, N])
        pt = m.sb("pt", [P, NT, H, P])
        sums = m.sb("sums", [P, 2, 2])
        total = m.sb("total", [P, 2])
        rden = m.sb("rden", [P, 2])
        ot = m.sb("ot", [P, CK, P])
        delta = m.sb("delta", [P, 1, C])

        ps_d = m.ps("ps_d", [P, 2, 512])
        ps_g = m.ps("ps_g", [P, 512])
        ps_a = m.ps("ps_a", [P, 2, 512])
        ps_t = m.ps("ps_t", [P, NT, P])
        ps_m = m.ps("ps_m", [P, 1, 512])

        consts = m.count("consts", 16 * 7)
        set_up = m.count("set_up")
        pool_set = m.count("pool_set")
        fold = m.ctx.enter_context(nc.semaphore("p3_fold"))
        powed = m.count("powed")
        k_in = {(kind, mh): m.count(f"k_in_{kind}{mh}", 64) for kind in range(2) for mh in range(2)}
        v_in = m.count("v_in", 16)
        qn_in = m.count("qn_in", 64)
        qb_done = m.count("qb_done", credit=2)
        d_mm = m.count("d_mm", credit=2 * NG)
        g_mm = m.count("g_mm", credit=2 * NG)
        mix_mm = m.count("mix_mm", credit=4)
        tr_mm = m.count("tr_mm", credit=2)
        pv_mm = m.count("pv_mm", credit=2)
        pj_mm = m.count("pj_mm")
        dc_done = m.count("dc_done", credit=2)
        gg_done = m.count("gg_done", credit=1)
        dd_done = m.count("dd_done")
        mx_done = m.count("mx_done")
        mxc_done = m.count("mxc_done")
        bias_done = m.count("bias_done")
        p_done = m.count("p_done", credit=2)
        total_done = m.count("total_done")
        pt_done = m.count("pt_done", credit=1)
        rden_done = m.count("rden_done")
        pn_done = m.count("pn_done")
        otc_done = m.count("otc_done")
        delta_done = m.count("delta_done", credit=1)
        h_done = m.count("h_done")

        block = ctx.enter_context(nc.Block())

        def blocks(eng, body):
            body(0, True, False)
            with eng.Fori(1, NB - 1) as blk:
                body(blk, False, False)
            body(NB - 1, False, True)

        @block.sync
        def _(sp):
            for tile, name in ((ident, "ident"), (w_proj, "w_proj"), (b_proj, "b_proj"), (mix_w, "mix_w"), (bn, "bn"),
                               (mask, "mask"), (conv_b, "conv_b")):
                sp.dma_start(tile[:], a[name]).then_inc(consts.sem, 16)

            def queries(b, nb, blk):
                col = sp.snap(nb * P) if not isinstance(nb, int) else nb * P
                if blk is not None:
                    sp.wait_ge(qb_done.sem, qb_done.done(2 * blk - 1))
                for hp in range(2):
                    for dup in range(2):
                        r = hp * 64 + dup * HD
                        sp.dma_start(q_in[r:r + HD], dr["parts"][ds(b, 1), 0, hp * HD:(hp + 1) * HD, :, ds(col, P)]
                                     ).then_inc(qn_in.sem, 16)

            with sp.Fori(0, B) as b:
                sp.wait_ge(qb_done.sem, qb_done.done(2 * NT * b - 1))
                queries(b, 0, None)
                for mh in range(2):
                    for kind, sem in ((0, d_mm), (1, g_mm)):
                        sp.wait_ge(sem.sem, sem.done(b * (2 * NG * NT) - 2 + mh))
                        for hp in range(2):
                            for part in range(2):
                                r = hp * 64 + part * HD
                                sp.dma_start(keys[r:r + HD, kind, :, mh * 512:(mh + 1) * 512],
                                             dr["keys"][ds(b, 1), hp * HD:(hp + 1) * HD, kind, part, :, mh * 512:(mh + 1) * 512]
                                             ).then_inc(k_in[kind, mh].sem, 16)
                sp.wait_ge(pv_mm.sem, pv_mm.done(b * NT - 1))
                sp.dma_start(v[:], dr["v"][ds(b, 1)]).then_inc(v_in.sem, 16)
                with sp.Fori(1, NT) as nb:
                    queries(b, nb, b * NT + nb)

        @block.gpsimd
        def _(pool):
            qb_done.start(pool)
            nc.gpsimd.memset(q_bd[:], 0.0).then_inc(pool_set.sem, 1)
            nc.gpsimd.memset(half[:], -0.5).then_inc(pool_set.sem, 1)
            nc.gpsimd.memset(eps[:], EPS).then_inc(pool_set.sem, 1)
            nc.gpsimd.memset(ones[:], 1.0).then_inc(pool_set.sem, 1)
            nc.gpsimd.memset(one[:], 1.0).then_inc(pool_set.sem, 1)
            pool.wait_ge(pool_set.sem, 5)
            pool.wait_ge(consts.sem, consts.done(0))
            nc.gpsimd.tensor_tensor(coef[:, 0], bn[:, 3], eps[:], ALU.add).then_inc(powed.sem, 1)
            pool.wait_ge(powed.sem, 1)
            nc.gpsimd.tensor_tensor(coef[:, 1], coef[:, 0], half[:], ALU.pow).then_inc(powed.sem, 1)
            pool.wait_ge(powed.sem, 2)
            with pool.Fori(0, NB) as blk:
                for hf in range(2):
                    pool.wait_ge(qn_in.sem, qn_in.done(blk))
                    pool.wait_ge(g_mm.sem, g_mm.freed(blk * (2 * NG) + (8 * hf + 7), 2 * NG))
                    for hp in range(2):
                        r = slice(hp * 64, hp * 64 + 64)
                        src = q_in[r, :, hf * 64:hf * 64 + 64].rearrange("p x (g n) -> p x g n", g=4)
                        last = nc.gpsimd.tensor_tensor(q_bd[r, :, 4 * hf:4 * hf + 4, hp * GS:(hp + 1) * GS], src, one[r].unsqueeze(2).unsqueeze(3).broadcast_to([64, 16, 4, GS]), ALU.mult)
                    last.then_inc(qb_done.sem, 1)

        @block.scalar
        def _(act):
            dc_done.start(act)
            gg_done.start(act)
            p_done.start(act)

            def plain(u, k):
                act.wait_ge(d_mm.sem, d_mm.done(u))
                act.wait_ge(mix_mm.sem, mix_mm.freed(u, 4))
                nc.scalar.copy(s_d[:, k, :], ps_d[:, k % 2, :]).then_inc(dc_done.sem, 1)

            def grass(u, k):
                act.wait_ge(g_mm.sem, g_mm.done(u))
                act.wait_ge(mix_mm.sem, mix_mm.freed(u, 4))
                nc.scalar.activation(s_gg[:, k, :], ps_g[:], ACT.Square).then_inc(gg_done.sem, 1)

            def weights(s, g, mh):
                if mh == 0:
                    act.wait_ge(bias_done.sem, bias_done.done(s))
                    act.wait_ge(tr_mm.sem, tr_mm.freed(s, 2))
                nc.scalar.activation(p[:, g % 2, mh * 512:(mh + 1) * 512], ps_a[:, mh, :], ACT.Exp,
                                     bias=bias[:, g % 2:g % 2 + 1], accum_out=sums[:, g % 2, mh:mh + 1]
                                     ).then_inc(p_done.sem, 1)

            def body(blk, first, last):
                for g in range(NG):
                    s = blk * NG + g
                    more = not (last and g == NG - 1)
                    k = 2 * ((g + 1) % 2)
                    if more:
                        plain(2 * s + 2, k)
                        grass(2 * s + 2, k)
                    weights(s, g, 0)
                    weights(s, g, 1)
                    if more:
                        plain(2 * s + 3, k + 1)
                        grass(2 * s + 3, k + 1)
                    if g == 2 and not first:
                        outputs_t(blk - 1)

            def outputs_t(blk):
                act.wait_ge(pv_mm.sem, pv_mm.done(blk))
                nc.scalar.copy(ot[:].rearrange("p c n -> p (c n)"), ps_m[:, 0, 0:CK * P]).then_inc(otc_done.sem, 1)

            plain(0, 0)
            grass(0, 0)
            plain(1, 1)
            grass(1, 1)
            blocks(act, body)
            outputs_t(NB - 1)

        @block.vector
        def _(dve):
            pt_done.start(dve)
            delta_done.start(dve)
            steps = [0]

            def link(ins):
                steps[0] += 1
                ins.then_inc(fold, 1)
                dve.wait_ge(fold, steps[0])

            dve.wait_ge(consts.sem, consts.done(0))
            dve.wait_ge(powed.sem, 2)
            link(nc.vector.tensor_tensor(coef[:, 0], bn[:, 0], coef[:, 1], ALU.mult))
            link(nc.vector.tensor_tensor(coef[:, 2], coef[:, 0], bn[:, 4], ALU.mult))
            link(nc.vector.tensor_scalar(coef[:, 2, 2:3], coef[:, 2, 2:3], GR ** -4, None, ALU.mult))
            link(nc.vector.tensor_tensor(coef[:, 3], bn[:, 2], coef[:, 0], ALU.mult))
            link(nc.vector.tensor_tensor(coef[:, 3], bn[:, 1], coef[:, 3], ALU.subtract))
            for n, w in ((2, 0), (3, 1)):
                link(nc.vector.tensor_tensor(cw[:, w], mix_w[:], coef[:, n].unsqueeze(2).broadcast_to([P, 3, H]), ALU.mult))
                for kind in range(3):
                    link(nc.vector.tensor_tensor((mixer, shifter)[w][:, kind], cw[:, w, kind].unsqueeze(2).broadcast_to([P, H, GS]),
                                                 mask[:].unsqueeze(1).broadcast_to([P, H, GS]), ALU.mult))
            nc.vector.tensor_copy(bias[:, 0:1], conv_b[:]).then_inc(set_up.sem, 1)
            dve.wait_ge(pv_mm.sem, 2)
            link(nc.vector.tensor_tensor(const[:], ps_m[:, 0, 0:1], conv_b[:], ALU.add))

            def squares(u, k):
                dve.wait_ge(dc_done.sem, dc_done.done(u))
                nc.vector.tensor_tensor(s_dd[:, k, :], s_d[:, k, :], s_d[:, k, :], ALU.mult).then_inc(dd_done.sem, 1)

            def maximum(s, g, mh):
                dve.wait_ge(mix_mm.sem, mix_mm.done(2 * s + mh))
                nc.vector.tensor_reduce(mx[:, g % 2, mh:mh + 1], ps_a[:, mh, :], AX_X, ALU.max).then_inc(mx_done.sem, 1)

            def shift(s, g):
                c = slice(g % 2, g % 2 + 1)
                dve.wait_ge(mx_done.sem, mx_done.done(2 * s + 1))
                nc.vector.tensor_scalar(mxc[:, c], mx[:, g % 2, 0:1], mx[:, g % 2, 1:2], const[:], ALU.max, ALU.add
                                        ).then_inc(mxc_done.sem, 1)
                dve.wait_ge(mxc_done.sem, mxc_done.done(s))
                nc.vector.tensor_scalar(bias[:, c], mxc[:, c], -1.0, const[:], ALU.mult, ALU.add).then_inc(bias_done.sem, 1)

            def normalised(s, g):
                c = slice(g % 2, g % 2 + 1)
                dve.wait_ge(p_done.sem, p_done.done(2 * s + 1))
                nc.vector.tensor_tensor(total[:, c], sums[:, g % 2, 0:1], sums[:, g % 2, 1:2], ALU.add).then_inc(total_done.sem, 1)
                dve.wait_ge(total_done.sem, total_done.done(s))
                nc.vector.reciprocal(rden[:, c], total[:, c]).then_inc(rden_done.sem, 1)
                dve.wait_ge(rden_done.sem, rden_done.done(s))
                nc.vector.tensor_scalar(p[:, g % 2, :], p[:, g % 2, :], rden[:, c], None, ALU.mult).then_inc(pn_done.sem, 1)

            def weights_t(s, g, blk, first):
                dve.wait_ge(tr_mm.sem, tr_mm.done(s))
                if g == 0 and not first:
                    dve.wait_ge(pv_mm.sem, pv_mm.done(blk - 1))
                nc.vector.tensor_copy(pt[:, :, :, g * GS:(g + 1) * GS], ps_t[:].rearrange("p t (o n) -> p t o n", o=H)
                                      ).then_inc(pt_done.sem, 1)

            def residual(blk):
                dve.wait_ge(pj_mm.sem, pj_mm.done(blk))
                nc.vector.tensor_tensor(delta[:], ps_m[:, :, 0:C], b_proj[:], ALU.add).then_inc(delta_done.sem, 1)
                dve.wait_ge(delta_done.sem, delta_done.done(blk))
                nc.vector.tensor_tensor(hs[:, ds(blk, 1), :], hs[:, ds(blk, 1), :], delta[:], ALU.add).then_inc(h_done.sem, 1)

            def body(blk, first, last):
                for g in range(NG):
                    s = blk * NG + g
                    more = not (last and g == NG - 1)
                    k = 2 * ((g + 1) % 2)
                    if g >= 2 or not first:
                        weights_t(s - 2, (g - 2) % NG, blk, first)
                    if g or not first:
                        normalised(s - 1, (g - 1) % NG)
                    maximum(s, g, 0)
                    if more:
                        squares(2 * s + 2, k)
                    maximum(s, g, 1)
                    shift(s, g)
                    if more:
                        squares(2 * s + 3, k + 1)
                    if g == 4 and not first:
                        residual(blk - 1)

            squares(0, 0)
            squares(1, 1)
            blocks(dve, body)
            weights_t(NB * NG - 2, NG - 2, NB - 1, False)
            normalised(NB * NG - 1, NG - 1)
            weights_t(NB * NG - 1, NG - 1, NB - 1, False)
            residual(NB - 1)
            dve.wait_ge(h_done.sem, h_done.done(NB - 1))

        @block.tensor
        def _(pe):
            d_mm.start(pe)
            g_mm.start(pe)
            mix_mm.start(pe)
            tr_mm.start(pe)
            pe.sem_inc(pv_mm.sem, 1)
            pe.wait_ge(pool_set.sem, 5)
            pe.wait_ge(set_up.sem, 1)
            for kind in range(3):
                last_mm = pe.matmul(ps_m[:, 0, 0:1], shifter[:, kind].rearrange("p o n -> p (o n)"), ones[:], start=(kind == 0),
                                    stop=(kind == 2))
            last_mm.then_inc(pv_mm.sem, 1)

            def scores(blk, g, mh):
                u = 2 * (blk * NG + g) + mh
                if g % 4 == 0 and mh == 0:
                    pe.wait_ge(qb_done.sem, qb_done.done(2 * blk + g // 4))
                for kind, ps, sem in ((0, ps_d[:, mh, :], d_mm), (1, ps_g[:], g_mm)):
                    if g == 0:
                        pe.wait_ge(k_in[kind, mh].sem, k_in[kind, mh].done(blk // NT))
                    if kind:
                        pe.wait_ge(gg_done.sem, gg_done.freed(u, 1))
                    else:
                        pe.wait_ge(dc_done.sem, dc_done.freed(u, 2))
                    for part in range(2):
                        for pair in range(4):
                            last_mm = pe.matmul(ps[pair * 32:(pair + 1) * 32], q_bd[:, kind * 8 + part * 4 + pair, g, :],
                                                keys[:, kind, pair, mh * 512:(mh + 1) * 512], start=(part == 0),
                                                stop=(part == 1))
                    last_mm.then_inc(sem.sem, 1)

            def mixed(s, g, mh):
                u = 2 * s + mh
                k = 2 * (g % 2) + mh
                pe.wait_ge(p_done.sem, p_done.freed(u, 2))
                pe.wait_ge(dd_done.sem, dd_done.done(u))
                pe.wait_ge(gg_done.sem, gg_done.done(u))
                for kind, tile in ((0, s_d), (1, s_dd), (2, s_gg)):
                    last_mm = pe.matmul(ps_a[:, mh, :], mixer[:, kind].rearrange("p o n -> p (o n)"), tile[:, k, :],
                                        start=(kind == 0), stop=(kind == 2))
                last_mm.then_inc(mix_mm.sem, 1)

            def transposed(s, g):
                pe.wait_ge(pn_done.sem, pn_done.done(s))
                pe.wait_ge(pt_done.sem, pt_done.freed(s, 1))
                for t in range(NT):
                    last_mm = pe.transpose(ps_t[:, t, :], p[:, g % 2, t * P:(t + 1) * P], ident[:])
                last_mm.then_inc(tr_mm.sem, 1)

            def weighted(blk):
                pe.wait_ge(pt_done.sem, pt_done.done(blk * NG + NG - 1))
                pe.wait_ge(v_in.sem, v_in.done(blk // NT))
                pe.wait_ge(delta_done.sem, delta_done.freed(blk, 1))
                for t in range(NT):
                    for c in range(CK):
                        for o in range(4 * c, 4 * c + 4):
                            r = o % 4 * HD
                            last_mm = pe.matmul(ps_m[r:r + HD, 0, c * P:(c + 1) * P], v[:, t, o * HD:(o + 1) * HD], pt[:, t, o, :],
                                                start=(t == 0 and c == 0), stop=(t == NT - 1), skip_group_check=True)
                last_mm.then_inc(pv_mm.sem, 1)

            def projected(blk):
                pe.wait_ge(otc_done.sem, otc_done.done(blk))
                for c in range(CK):
                    last_mm = pe.matmul(ps_m[:, 0, 0:C], ot[:, c, :], w_proj[:, c, :], start=(c == 0), stop=(c == CK - 1))
                last_mm.then_inc(pj_mm.sem, 1)

            def body(blk, first, last):
                for g in range(NG):
                    s = blk * NG + g
                    ahead = (blk, g + 1) if g < NG - 1 else (blk + 1, 0)
                    more = not (last and g == NG - 1)
                    mixed(s, g, 0)
                    if g == 1 and not first:
                        weighted(blk - 1)
                    if more:
                        scores(*ahead, 0)
                    mixed(s, g, 1)
                    if more:
                        scores(*ahead, 1)
                    if g or not first:
                        transposed(s - 1, (g - 1) % NG)
                    if g == 3 and not first:
                        projected(blk - 1)

            scores(0, 0, 0)
            scores(0, 0, 1)
            blocks(pe, body)
            transposed(NB * NG - 1, NG - 1)
            weighted(NB - 1)
            projected(NB - 1)


def experts(nc, a, hs, out):
    with ExitStack() as ctx:
        m = Maker(nc, ctx, "p4")
        NB = B * N // 512
        TB = 512 // P
        HT = F // P
        ident = m.sb("ident", [P, P])
        norm = m.sb("norm", [P, 2, CK])
        w_r = m.sb("w_r", [P, CK, E])
        b_r = m.sb("b_r", [P, E])
        b1 = m.sb("b1", [P, E, HT])
        b2 = m.sb("b2", [E, C])
        iota = m.sb("iota", [P, E])
        half = m.sb("half", [P, TB])
        eps = m.sb("eps", [P, TB])
        carrier = m.sb("carrier", [P, 128])
        stage = m.sb("stage", [P, 2, 2, 1024])
        w1 = m.sb("w1", [P, 2, E, CK, F], F16)
        w2 = m.sb("w2", [P, 2, E, HT, C], F16)
        hc = m.sb("hc", [P, TB, C])
        stats = m.sb("stats", [P, TB, 6])
        mv = m.sb("mv", [P, TB, 2])
        veps = m.sb("veps", [P, TB])
        rstd = m.sb("rstd", [P, TB])
        z = m.sb("z", [P, TB, C])
        xh = m.sb("xh", [P, TB, C])
        xf = m.sb("xf", [P, CK, 512])
        x_hi = m.sb("x_hi", [P, CK, 512], F16)
        x_lo = m.sb("x_lo", [P, CK, 512], F16)
        logit = m.sb("logit", [P, TB, E])
        top = m.sb("top", [P, TB, 8])
        idx = m.sb("idx", [P, TB, 8], mybir.dt.uint32)
        idxf = m.sb("idxf", [P, TB, 2])
        gap = m.sb("gap", [P, TB])
        th = m.sb("th", [P, TB])
        wt = m.sb("wt", [P, 2, TB])
        hot = m.sb("hot", [P, 2, TB, E])
        gate_next = m.sb("gate_next", [P, TB, E])
        gate = m.sb("gate", [P, TB, E])
        gate_t = m.sb("gate_t", [E, 512])
        g32 = m.sb("g32", [P, HT, 512])
        g_hi = m.sb("g_hi", [P, 2, HT, 512], F16)
        g_lo = m.sb("g_lo", [P, 2, HT, 512], F16)
        y = m.sb("y", [P, TB, C])
        o = m.sb("o", [P, TB, C])

        ps_h = [m.ps(f"ps_h{k}", [P, 512]) for k in range(4)]
        ps_y = [m.ps(f"ps_y{k}", [P, 512]) for k in range(2)]
        ps_x = m.ps("ps_x", [P, 512])
        ps_r = m.ps("ps_r", [P, 512])

        consts = m.count("consts", 16 * 7)
        w_in = [m.count(f"w_in{k}", 32) for k in range(2)]
        w_hi_done = m.count("w_hi_done")
        w_done = m.count("w_done", credit=2)
        pool_set = m.count("pool_set")
        hc_in = m.count("hc_in", 16)
        st_done = m.count("st_done")
        mv_done = m.count("mv_done")
        ve_done = m.count("ve_done")
        rstd_done = m.count("rstd_done")
        z_done = m.count("z_done")
        xh_done = m.count("xh_done", credit=1)
        xt_mm = m.count("xt_mm", credit=2)
        xf_done = m.count("xf_done")
        x_hi_done = m.count("x_hi_done")
        x_lo_done = m.count("x_lo_done", credit=1)
        r_mm = m.count("r_mm")
        logit_done = m.count("logit_done")
        top_done = m.count("top_done")
        idx_done = m.count("idx_done")
        gap_done = m.count("gap_done")
        th_done = m.count("th_done")
        g_step = m.count("g_step", 1)
        gate_done = m.count("gate_done")
        gt_mm = m.count("gt_mm")
        gt_done = m.count("gt_done", credit=1)
        gate_set = m.count("gate_set", credit=1)
        h_mm = m.count("h_mm", credit=1)
        g32_done = m.count("g32_done")
        gh_done = m.count("gh_done", credit=4)
        gl_done = m.count("gl_done", credit=4)
        y_mm = m.count("y_mm", credit=8)
        acc_done = m.count("acc_done", credit=2)
        stored = m.count("stored", 16, credit=1)

        YU = TB * (E + 1)

        block = ctx.enter_context(nc.Block())

        def blocks(eng, body):
            with eng.Fori(0, NB - 1) as blk:
                body(blk, False)
            body(NB - 1, True)

        @block.sync
        def _(sp):
            stored.start(sp)
            for tile, name in ((ident, "ident"), (norm, "norm"), (w_r, "w_r"), (b_r, "b_r"), (b1, "b1"), (b2, "b2"),
                               (iota, "iota")):
                sp.dma_start(tile[:], a[name]).then_inc(consts.sem, 16)
            sp.dma_start(hc[:], hs[:, 0:TB, :]).then_inc(hc_in.sem, 16)
            for e in range(E):
                sp.wait_ge(w_done.sem, w_done.freed(e, 2))
                sp.dma_start(stage[:, e % 2, 0], a["w1"][:, e]).then_inc(w_in[e % 2].sem, 16)
                sp.dma_start(stage[:, e % 2, 1], a["w2"][:, e]).then_inc(w_in[e % 2].sem, 16)

            def body(blk, last):
                if not last:
                    sp.wait_ge(acc_done.sem, acc_done.done(blk * YU + (TB - 1)))
                    sp.dma_start(hc[:], hs[:, ds(blk * TB + TB, TB), :]).then_inc(hc_in.sem, 16)
                sp.wait_ge(acc_done.sem, acc_done.done(blk * YU + (YU - 1)))
                sp.dma_start(out[ds(blk * TB, TB)].rearrange("t p c -> p t c"), o[:]).then_inc(stored.sem, 16)

            blocks(sp, body)
            sp.wait_ge(stored.sem, stored.done(NB - 1))

        @block.gpsimd
        def _(pool):
            nc.gpsimd.memset(half[:], -0.5).then_inc(pool_set.sem, 1)
            nc.gpsimd.memset(eps[:], EPS).then_inc(pool_set.sem, 1)
            nc.gpsimd.memset(carrier[:], 1.0).then_inc(pool_set.sem, 1)
            pool.wait_ge(pool_set.sem, 3)

            with pool.Fori(0, 2 * NB) as n:
                pool.wait_ge(mv_done.sem, mv_done.done(n))
                nc.gpsimd.tensor_tensor(veps[:], mv[:, :, 1], eps[:], ALU.add).then_inc(ve_done.sem, 1)
                pool.wait_ge(ve_done.sem, ve_done.done(n))
                nc.gpsimd.tensor_tensor(rstd[:], veps[:], half[:], ALU.pow).then_inc(rstd_done.sem, 1)

        @block.scalar
        def _(act):
            gt_done.start(act)
            gh_done.start(act)

            def scaled(blk, c):
                act.wait_ge(xt_mm.sem, xt_mm.done(2 * blk + c))
                if c == 0:
                    act.wait_ge(x_lo_done.sem, x_lo_done.freed(blk, 1))
                nc.scalar.activation(xf[:, c, :], ps_x[:], ACT.Identity, bias=norm[:, 1, c:c + 1],
                                     scale=norm[:, 0, c:c + 1]).then_inc(xf_done.sem, 1)

            def tanh(blk):
                act.wait_ge(gap_done.sem, gap_done.done(blk))
                nc.scalar.activation(th[:], gap[:], ACT.Tanh, scale=0.5).then_inc(th_done.sem, 1)

            def gates_t(blk):
                act.wait_ge(gt_mm.sem, gt_mm.done(blk))
                nc.scalar.copy(gate_t[:], ps_x[0:E, :]).then_inc(gt_done.sem, 1)

            steps = {3: lambda blk: scaled(blk, 0), 4: lambda blk: scaled(blk, 1), 5: tanh, 6: gates_t}

            def hidden(blk, e):
                for t in range(HT):
                    u = blk * (4 * E) + (4 * e + t)
                    act.wait_ge(h_mm.sem, h_mm.done(u))
                    act.wait_ge(gl_done.sem, gl_done.freed(u, 4))
                    nc.scalar.activation(g32[:, t, :], ps_h[t][:], ACT.Gelu, bias=b1[:, e, t:t + 1]).then_inc(g32_done.sem, 1)
                    act.wait_ge(y_mm.sem, y_mm.done(blk * YU + (4 * e - 1 if e > 1 else 4 * e - 5)))
                    nc.scalar.activation(g_hi[:, e % 2, t, :], ps_h[t][:], ACT.Gelu, bias=b1[:, e, t:t + 1]
                                         ).then_inc(gh_done.sem, 1)

            for e in range(E):
                act.wait_ge(w_in[e % 2].sem, w_in[e % 2].done(e // 2))
                nc.scalar.copy(w1[:, 0, e].rearrange("p c n -> p (c n)"), stage[:, e % 2, 0])
                nc.scalar.copy(w2[:, 0, e].rearrange("p c n -> p (c n)"), stage[:, e % 2, 1]).then_inc(w_hi_done.sem, 1)
            act.wait_ge(consts.sem, consts.done(0))
            for k in sorted(steps):
                steps[k](0)

            def body(blk, last):
                act.wait_ge(xf_done.sem, xf_done.done(2 * blk + 1))
                act.wait_ge(h_mm.sem, h_mm.freed(blk * (4 * E), 1))
                nc.scalar.copy(x_hi[:], xf[:]).then_inc(x_hi_done.sem, 1)
                hidden(blk, 0)
                for e in range(E):
                    if e < E - 1:
                        hidden(blk, e + 1)
                    if not last and e in steps:
                        steps[e](blk + 1)

            blocks(act, body)

        @block.vector
        def _(dve):
            for k in (xh_done, x_lo_done, w_done, gate_set, gl_done, acc_done):
                k.start(dve)

            held = [0]

            def hold(k, value):
                dve.wait_ge(k.sem, value)
                held[0] += 1
                nc.vector.tensor_tensor(carrier[:, held[0]:held[0] + 1], carrier[:, 0:1], carrier[:, 0:1], ALU.mult)

            def moments(n, src):
                for t in range(TB):
                    last = nc.vector.bn_stats(stats[:, t, :], src[:, t, :])
                last.then_inc(st_done.sem, 1)
                hold(st_done, st_done.done(n))
                for t in range(TB):
                    last = nc.vector.bn_aggr(mv[:, t, :], stats[:, t, :])
                last.then_inc(mv_done.sem, 1)

            def centred(n, src, dst, done):
                hold(rstd_done, rstd_done.done(n))
                for t in range(TB):
                    last = nc.vector.tensor_scalar(dst[:, t, :], src[:, t, :], mv[:, t, 0:1], rstd[:, t:t + 1],
                                                   ALU.subtract, ALU.mult)
                last.then_inc(done.sem, 1)

            def first_moments(blk):
                hold(hc_in, hc_in.done(blk))
                hold(xh_done, xh_done.freed(blk, 1))
                moments(2 * blk, hc)

            def second_moments(blk):
                centred(2 * blk, hc, z, z_done)
                hold(z_done, z_done.done(blk))
                moments(2 * blk + 1, z)

            def normalised(blk):
                hold(xt_mm, xt_mm.freed(2 * blk + 1, 2))
                centred(2 * blk + 1, z, xh, xh_done)

            def best(blk):
                hold(r_mm, r_mm.done(blk))
                nc.vector.tensor_tensor(logit[:], ps_r[:, 0:TB * E].rearrange("p (t e) -> p t e", t=TB),
                                        b_r[:].unsqueeze(1).broadcast_to([P, TB, E]), ALU.add).then_inc(logit_done.sem, 1)
                hold(logit_done, logit_done.done(blk))
                for t in range(TB):
                    last = nc.vector.max(top[:, t, :], logit[:, t, :])
                last.then_inc(top_done.sem, 1)
                hold(top_done, top_done.done(blk))
                for t in range(TB):
                    last = nc.vector.max_index(idx[:, t, :], top[:, t, :], logit[:, t, :])
                last.then_inc(idx_done.sem, 1)
                nc.vector.tensor_tensor(gap[:], top[:, :, 1], top[:, :, 0], ALU.subtract).then_inc(gap_done.sem, 1)
                hold(idx_done, idx_done.done(blk))
                nc.vector.tensor_copy(idxf[:], idx[:, :, 0:2]).then_inc(g_step.sem, 1)

            def gates(blk):
                hold(th_done, th_done.done(blk))
                nc.vector.tensor_scalar(wt[:, 0], th[:], -0.5, 0.5, ALU.mult, ALU.add)
                nc.vector.tensor_scalar(wt[:, 1], th[:], 0.5, 0.5, ALU.mult, ALU.add).then_inc(g_step.sem, 1)
                hold(g_step, g_step.done(4 * blk + 1))
                for k in range(2):
                    last = nc.vector.tensor_tensor(hot[:, k], iota[:].unsqueeze(1).broadcast_to([P, TB, E]),
                                                   idxf[:, :, k:k + 1].broadcast_to([P, TB, E]), ALU.is_equal)
                last.then_inc(g_step.sem, 1)
                hold(g_step, g_step.done(4 * blk + 2))
                for k in range(2):
                    last = nc.vector.tensor_tensor(hot[:, k], hot[:, k], wt[:, k].unsqueeze(2).broadcast_to([P, TB, E]), ALU.mult)
                last.then_inc(g_step.sem, 1)
                hold(g_step, g_step.done(4 * blk + 3))
                hold(gate_set, gate_set.freed(blk, 1))
                nc.vector.tensor_tensor(gate_next[:], hot[:, 0], hot[:, 1], ALU.add).then_inc(gate_done.sem, 1)

            steps = {0: first_moments, 1: second_moments, 2: normalised, 5: best, 6: gates}

            def low(blk, e):
                for t in range(HT):
                    u = blk * (4 * E) + (4 * e + t)
                    dve.wait_ge(gh_done.sem, gh_done.done(u))
                    nc.vector.tensor_tensor(g_lo[:, e % 2, t, :], g32[:, t, :], g_hi[:, e % 2, t, :],
                                            ALU.subtract).then_inc(gl_done.sem, 1)

            def summed(blk, e):
                for t in range(TB):
                    u = blk * YU + (4 * (e + 1) + t)
                    dve.wait_ge(y_mm.sem, y_mm.done(u))
                    if e < 0:
                        nc.vector.tensor_tensor(y[:, t, :], ps_y[t % 2][:, 0:C], hc[:, t, :], ALU.add).then_inc(acc_done.sem, 1)
                        continue
                    if e == E - 1 and t == 0:
                        dve.wait_ge(stored.sem, stored.freed(blk, 1))
                    nc.vector.scalar_tensor_tensor((y, o)[e == E - 1][:, t, :], ps_y[t % 2][:, 0:C], gate[:, t, e:e + 1], y[:, t, :],
                                                   ALU.mult, ALU.add).then_inc(acc_done.sem, 1)

            dve.wait_ge(consts.sem, consts.done(0))
            dve.wait_ge(pool_set.sem, 3)
            for e in range(E):
                if e == 1:
                    for k in (0, 1, 2):
                        steps[k](0)
                dve.wait_ge(w_hi_done.sem, e + 1)
                nc.vector.tensor_tensor(w1[:, 1, e].rearrange("p c n -> p (c n)"), stage[:, e % 2, 0],
                                        w1[:, 0, e].rearrange("p c n -> p (c n)"), ALU.subtract)
                nc.vector.tensor_tensor(w2[:, 1, e].rearrange("p c n -> p (c n)"), stage[:, e % 2, 1],
                                        w2[:, 0, e].rearrange("p c n -> p (c n)"), ALU.subtract).then_inc(w_done.sem, 1)
            best(0)
            gates(0)

            def body(blk, last):
                hold(gate_done, gate_done.done(blk))
                hold(acc_done, acc_done.done(blk * YU - 1))
                nc.vector.tensor_copy(gate[:], gate_next[:]).then_inc(gate_set.sem, 1)
                dve.wait_ge(x_hi_done.sem, x_hi_done.done(blk))
                nc.vector.tensor_tensor(x_lo[:], xf[:], x_hi[:], ALU.subtract).then_inc(x_lo_done.sem, 1)
                hold(gate_set, gate_set.done(blk))
                summed(blk, -1)
                low(blk, 0)
                for e in range(E):
                    if e < E - 1:
                        low(blk, e + 1)
                    summed(blk, e)
                    if not last and e in steps:
                        steps[e](blk + 1)

            blocks(dve, body)

        @block.tensor
        def _(pe):
            h_mm.start(pe)
            xt_mm.start(pe)
            y_mm.start(pe)

            def turned(blk, c):
                pe.wait_ge(xh_done.sem, xh_done.done(blk))
                if c == 0:
                    pe.wait_ge(gt_done.sem, gt_done.freed(blk, 1))
                else:
                    pe.wait_ge(xf_done.sem, xf_done.done(2 * blk))
                for t in range(TB):
                    last = pe.transpose(ps_x[:, t * P:(t + 1) * P], xh[:, t, c * P:(c + 1) * P], ident[:])
                last.then_inc(xt_mm.sem, 1)

            def routed(blk):
                pe.wait_ge(xf_done.sem, xf_done.done(2 * blk + 1))
                for t in range(TB):
                    for c in range(CK):
                        last = pe.matmul(ps_r[:, t * E:(t + 1) * E], xf[:, c, t * P:(t + 1) * P], w_r[:, c, :],
                                         start=(t == 0 and c == 0), stop=(c == CK - 1), skip_group_check=True)
                last.then_inc(r_mm.sem, 1)

            def gates_t(blk):
                pe.wait_ge(gate_done.sem, gate_done.done(blk))
                for t in range(TB):
                    last = pe.transpose(ps_x[0:E, t * P:(t + 1) * P], gate_next[:, t, :], ident[:])
                last.then_inc(gt_mm.sem, 1)

            steps = {3: lambda blk: turned(blk, 0), 4: lambda blk: turned(blk, 1), 5: routed, 6: gates_t}

            def hidden(blk, e):
                if not isinstance(blk, int) or blk == 0:
                    pe.wait_ge(w_done.sem, w_done.done(e))
                for t in range(HT):
                    u = blk * (4 * E) + (4 * e + t)
                    pe.wait_ge(gh_done.sem, gh_done.freed(u, 4))
                    n = 0
                    for c in range(CK):
                        for wp, x in ((0, x_hi), (0, x_lo), (1, x_hi)):
                            last = pe.matmul(ps_h[t][:], w1[:, wp, e, c, t * P:(t + 1) * P], x[:, c, :], start=(n == 0),
                                             stop=(n == 3 * CK - 1))
                            n += 1
                    last.then_inc(h_mm.sem, 1)

            def outputs(blk, e):
                for t in range(TB):
                    u = blk * YU + (4 * (e + 1) + t)
                    pe.wait_ge(acc_done.sem, acc_done.freed(u, 2))
                    if e < 0:
                        pe.matmul(ps_y[t % 2][:, 0:C], gate_t[:, t * P:(t + 1) * P], b2[:], start=True, stop=True
                                  ).then_inc(y_mm.sem, 1)
                        continue
                    if t == 0:
                        pe.wait_ge(gl_done.sem, gl_done.done(blk * (4 * E) + (4 * e + 3)))
                    n = 0
                    for k in range(HT):
                        for g, wp in ((g_hi, 0), (g_hi, 1), (g_lo, 0)):
                            last = pe.matmul(ps_y[t % 2][:, 0:C], g[:, e % 2, k, t * P:(t + 1) * P], w2[:, wp, e, k, :],
                                             start=(n == 0), stop=(n == 3 * HT - 1))
                            n += 1
                    last.then_inc(y_mm.sem, 1)

            pe.wait_ge(consts.sem, consts.done(0))
            for k in sorted(steps):
                steps[k](0)

            def body(blk, last):
                pe.wait_ge(gt_done.sem, gt_done.done(blk))
                outputs(blk, -1)
                pe.wait_ge(x_lo_done.sem, x_lo_done.done(blk))
                hidden(blk, 0)
                for e in range(E):
                    if e < E - 1:
                        hidden(blk, e + 1)
                    outputs(blk, e)
                    if not last and e in steps:
                        steps[e](blk + 1)

            blocks(pe, body)


def program(nc, a, out):
    with ExitStack() as ctx:
        m = Maker(nc, ctx, "all")
        hs = m.sb("h", [P, TILES, C])

        def dram(name, shape, dt=F32):
            return nc.dram_tensor(name, shape, dt, kind=KINDS.get(name, "Internal")).ap()

        v_d = dram("v_d", [B, P, NT, C])
        qt_d = dram("qt_d", [B, P, 4, N])
        top_d = dram("top_d", [B, HD, 2 * C])
        gram_d = dram("gram_d", [B * 4 * P, HD])
        rt_d = dram("rt_d", [P * HD, HD])
        parts_d = dram("parts_d", [B, 2, 2 * HD, 2, 2, 2, 2, N], F16)
        dr = {
            "v": v_d, "qt": qt_d, "top": top_d,
            "gram": gram_d.rearrange("(b g p) j -> b p g j", b=B, g=4),
            "gram_m": gram_d.rearrange("(m i) j -> m i j", m=P),
            "top_m": top_d.rearrange("b n (m d) -> b m n d", d=HD),
            "rt_m": rt_d.rearrange("(m i) j -> m i j", m=P),
            "rt": rt_d.rearrange("(b g h k) i -> b h k g i", b=B, g=4, h=4),
            "parts_st": parts_d,
            "parts": parts_d[:, 0:1].rearrange("b y x k p r g n -> b y x (k p r g) n"),
            "keys": parts_d[:, 1].rearrange("b x k p r g n -> b x k p (r g) n"),
        }
        embed_and_project(nc, a, dr, hs)
        orthonormal_factors(nc, a, dr)
        split_operands(nc, a, dr)
        attention(nc, a, dr, hs)
        experts(nc, a, hs, out.rearrange("b (t p) c -> (b t) p c", p=P))


KINDS = {}


def kernel(**inputs):
    import numpy as np
    import concourse.bacc as bacc
    from concourse.bass_utils import run_bass_kernel_spmd as run

    def rows(v, n=P):
        return np.broadcast_to(v.reshape(1, -1), (n, v.size))

    i = {k.replace("L0_", ""): np.asarray(v) for k, v in inputs.items()}
    x = i["x"].reshape(B, 32, 7, 32, 7).transpose(0, 2, 4, 1, 3).reshape(B, PD, N)
    laid = {
        "pat": np.concatenate([x, x[:1]]),
        "tok_w": i["tok_W"].T,
        "pos": i["tok_pos"].reshape(NT, P, C).transpose(1, 0, 2),
        "tok_b": rows(i["tok_b"]),
        "w_qkv": i["attn_w_qkv"].T.reshape(CK, P, 3 * C).transpose(1, 0, 2),
        "b_qkv": rows(i["attn_b_qkv"]),
        "ident": np.eye(P, dtype=np.float32),
    }
    heads = [g * 4 + pr * 2 + hp for pr in range(2) for g in range(2) for hp in range(2)]
    kinds = lambda v: np.repeat(v.reshape(3, H)[:, heads].T, GS, axis=0)
    laid |= {
        "w_proj": i["attn_w_proj"].T.reshape(CK, P, C).transpose(1, 0, 2),
        "b_proj": rows(i["attn_b_proj"]).reshape(P, 1, C),
        "mix_w": np.repeat(i["attn_conv_w"].reshape(H, 3, H)[:, :, heads].transpose(2, 1, 0), GS, axis=0),
        "bn": np.stack([kinds(i["attn_bn_" + k]) for k in ("gamma", "beta", "mean", "var")]
                       + [rows(np.stack([i["attn_scale"], i["attn_riem_scale"], i["attn_grassman_scale"]]))], axis=1),
        "mask": np.tile(np.eye(GS, dtype=np.float32), (H, 1)),
        "conv_b": np.repeat(i["attn_conv_b"], GS).reshape(P, 1),
    }
    laid |= {
        "norm": np.stack([i["ffn_gamma"].reshape(CK, P).T, i["ffn_beta"].reshape(CK, P).T], axis=1),
        "w_r": i["ffn_Wr"].reshape(CK, P, E).transpose(1, 0, 2),
        "b_r": rows(i["ffn_br"]),
        "b1": i["ffn_b1"].reshape(E, F // P, P).transpose(2, 0, 1),
        "b2": i["ffn_b2"],
        "iota": rows(np.arange(E, dtype=np.float32)),
        "w1": i["ffn_W1"].reshape(E, CK, P, F).transpose(2, 0, 1, 3).reshape(P, E, CK * F),
        "w2": i["ffn_W2"].reshape(E, F // P, P, C).transpose(2, 0, 1, 3).reshape(P, E, F // P * C),
    }
    nc = bacc.Bacc("TRN2", target_bir_lowering=False, num_devices=1)
    arrays, aps = {}, {}
    for name, v in laid.items():
        arrays[f"in_{name}"] = np.ascontiguousarray(v)
        aps[name] = nc.dram_tensor(f"in_{name}", v.shape, mybir.dt.from_np(v.dtype), kind="ExternalInput").ap()
    out = nc.dram_tensor("out_0", (B, N, C), F32, kind="ExternalOutput").ap()
    program(nc, aps, out)
    r = run(nc, [arrays], core_ids=[0])
    return r.results[0]["out_0"]
```

```python
from contextlib import ExitStack

import concourse.bass as bass
from concourse import mybir

F32 = mybir.dt.float32
F16 = mybir.dt.float16
ALU = mybir.AluOpType
ACT = mybir.ActivationFunctionType
AX_X = mybir.AxisListType.X
ds = bass.ds

P = 128
B = 8
N = 1024
C = 256
H = 8
HD = C // H
NT = N // P
TILES = B * NT
CK = C // P
PD = 49
E = 8
F = 512
EPS = 1e-5
GR = 32.0
MX = 16.0
DX = 1 / 8
GS = 16
NG = P // GS


class Count:

    def __init__(self, sem, per=1, credit=0):
        self.sem, self.per, self.credit = sem, per, credit

    def start(self, eng):
        eng.sem_inc(self.sem, self.per * self.credit)

    def done(self, t):
        return (t + (1 + self.credit)) * self.per

    def freed(self, t, depth):
        assert depth <= self.credit
        return (t + (1 + self.credit - depth)) * self.per


class Maker:

    def __init__(self, nc, ctx, prefix):
        self.nc, self.ctx, self.prefix = nc, ctx, prefix

    def sb(self, name, shape, dt=F32):
        return self.ctx.enter_context(self.nc.sbuf_tensor(f"{self.prefix}_{name}", shape, dt))

    def ps(self, name, shape, dt=F32):
        return self.ctx.enter_context(self.nc.psum_tensor(f"{self.prefix}_{name}", shape, dt))

    def count(self, name, per=1, credit=0):
        return Count(self.ctx.enter_context(self.nc.semaphore(f"{self.prefix}_{name}")), per, credit)


def embed_and_project(nc, a, dr, hs):
    with ExitStack() as ctx:
        m = Maker(nc, ctx, "p1")
        tok_w = m.sb("tok_w", [PD, C])
        pos_b = m.sb("pos_b", [P, NT, C])
        tok_b = m.sb("tok_b", [P, C])
        w_qkv = m.sb("w_qkv", [P, CK, 3 * C])
        b_qkv = m.sb("b_qkv", [P, 3 * C])
        ident = m.sb("ident", [P, P])
        pat = m.sb("pat", [PD, N])
        hc = m.sb("hc", [P, 4, C])
        stats = m.sb("stats", [P, 4, 6])
        mv = m.sb("mv", [P, 4, 2])
        veps = m.sb("veps", [P, 4])
        rstd = m.sb("rstd", [P, 4])
        mhalf = m.sb("mhalf", [P, 1])
        eps = m.sb("eps", [P, 1])
        z = m.sb("z", [P, 2, C])
        zt = m.sb("zt", [P, 2, CK, P])
        qk = m.sb("qk", [P, 2, 2 * C])
        vs = m.sb("vs", [P, 2, C])
        qt = m.sb("qt", [P, 2, 4, P])
        gram = m.sb("gram", [P, 4, HD])

        ps_tok = m.ps("ps_tok", [P, 2, 512])
        ps_zt = m.ps("ps_zt", [P, CK, 256])
        ps_qk = m.ps("ps_qk", [P, 512])
        ps_v = m.ps("ps_v", [P, 512])
        ps_qt = m.ps("ps_qt", [P, 4, P])
        ps_gram = m.ps("ps_gram", [P, 512])

        weights = m.count("weights", 16 * 6)
        pat_in = [m.count(f"pat_in{k}", 16) for k in range(2)]
        posb_ready = m.count("posb_ready")
        half_ready = m.count("half_ready")
        tok_mm = m.count("tok_mm")
        h_done = m.count("h_done", credit=2)
        st_done = m.count("st_done")
        mv_done = m.count("mv_done")
        ve_done = m.count("ve_done")
        rstd_done = m.count("rstd_done", credit=0)
        z_done = m.count("z_done")
        zt_mm = m.count("zt_mm", credit=2)
        ztc_done = m.count("ztc_done", credit=1)
        qkv_mm = m.count("qkv_mm", credit=2)
        qk_done = m.count("qk_done", credit=1)
        v_done = m.count("v_done", credit=1)
        qt_mm = m.count("qt_mm")
        gram_mm = m.count("gram_mm", credit=2)
        qtc_done = m.count("qtc_done", credit=1)
        gramc_done = m.count("gramc_done", credit=1)
        v_store = [m.count(f"v_store{k}", 16, credit=1) for k in range(2)]
        qt_store = [m.count(f"qt_store{k}", 16, credit=1) for k in range(2)]
        a1_store = m.count("a1_store", 16, credit=1)
        h_store = [m.count(f"h_store{k}", 16, credit=1) for k in range(4)]
        gr_store = m.count("gr_store", 16, credit=1)

        block = ctx.enter_context(nc.Block())

        def images(eng, body):
            body(0, True, False)
            with eng.Fori(1, B - 1) as b:
                body(b, False, False)
            body(B - 1, False, True)

        def at(b, t):
            return b + t // NT, t % NT, b * NT + t

        def load_patches(eng, b, half):
            c = slice(half * N // 2, (half + 1) * N // 2)
            eng.dma_start(pat[:, c], a["pat"][b if isinstance(b, int) else ds(b, 1), :, c]).then_inc(pat_in[half].sem, 16)

        @block.sync
        def _(sp):
            load_patches(sp, 0, 0)
            load_patches(sp, 0, 1)
            sp.dma_start(tok_w[:], a["tok_w"]).then_inc(weights.sem, 16)
            sp.dma_start(pos_b[:], a["pos"]).then_inc(weights.sem, 16)
            sp.dma_start(tok_b[:], a["tok_b"]).then_inc(weights.sem, 16)
            sp.dma_start(w_qkv[:], a["w_qkv"]).then_inc(weights.sem, 16)
            sp.dma_start(b_qkv[:], a["b_qkv"]).then_inc(weights.sem, 16)
            sp.dma_start(ident[:], a["ident"]).then_inc(weights.sem, 16)
            for stores in (*v_store, *qt_store, *h_store, a1_store, gr_store):
                stores.start(sp)
            with sp.Fori(0, B) as b:
                for t in range(NT):
                    T = b * NT + t
                    sp.wait_ge(h_done.sem, h_done.done(T))
                    sp.dma_start(hs[:, ds(T, 1), :], hc[:, t % 4, :]).then_inc(h_store[t % 4].sem, 16)
                    sp.wait_ge(v_done.sem, v_done.done(T))
                    sp.dma_start(dr["v"][ds(b, 1), :, t, :], vs[:, t % 2, :]).then_inc(v_store[t % 2].sem, 16)
                    if t == 0:
                        sp.dma_start(dr["top"][ds(b, 1), :, :], qk[0:HD, 0, :]).then_inc(a1_store.sem, 16)
                    sp.wait_ge(qtc_done.sem, qtc_done.done(T))
                    sp.dma_start(dr["qt"][ds(b, 1), :, :, t * P:(t + 1) * P], qt[:, t % 2]).then_inc(qt_store[t % 2].sem, 16)
                sp.wait_ge(gramc_done.sem, gramc_done.done(b))
                sp.dma_start(dr["gram"][ds(b, 1)], gram[:]).then_inc(gr_store.sem, 16)
            for stores in (*v_store, *qt_store):
                sp.wait_ge(stores.sem, stores.done(TILES // 2 - 1))
            for stores in h_store:
                sp.wait_ge(stores.sem, stores.done(TILES // 4 - 1))
            sp.wait_ge(a1_store.sem, a1_store.done(B - 1))
            sp.wait_ge(gr_store.sem, gr_store.done(B - 1))

        @block.gpsimd
        def _(pool):
            nc.gpsimd.memset(mhalf[:], -0.5).then_inc(half_ready.sem, 1)
            nc.gpsimd.memset(eps[:], EPS).then_inc(half_ready.sem, 1)
            pool.wait_ge(half_ready.sem, 2)
            with pool.Fori(0, TILES // 4) as quad:
                for t in range(4):
                    T = quad * 4 + t
                    pool.wait_ge(mv_done.sem, mv_done.done(T))
                    nc.gpsimd.tensor_tensor(veps[:, t:t + 1], mv[:, t, 1:2], eps[:], ALU.add).then_inc(ve_done.sem, 1)
                    pool.wait_ge(ve_done.sem, ve_done.done(T))
                    nc.gpsimd.tensor_tensor(rstd[:, t:t + 1], veps[:, t:t + 1], mhalf[:], ALU.pow).then_inc(rstd_done.sem, 1)

        @block.scalar
        def _(act):
            ztc_done.start(act)
            qtc_done.start(act)
            gramc_done.start(act)

            def z_t(b, t, T):
                act.wait_ge(zt_mm.sem, zt_mm.done(T))
                act.wait_ge(qkv_mm.sem, qkv_mm.freed(T, 2))
                nc.scalar.copy(zt[:, t % 2], ps_zt[:, :, 0:P]).then_inc(ztc_done.sem, 1)

            def qk_t(b, t, T):
                act.wait_ge(qt_mm.sem, qt_mm.done(T))
                slot = qt_store[t % 2]
                act.wait_ge(slot.sem, slot.freed(b * (NT // 2) + t // 2, 1))
                nc.scalar.copy(qt[:, t % 2], ps_qt[:]).then_inc(qtc_done.sem, 1)
                if t == NT - 1:
                    act.wait_ge(gram_mm.sem, gram_mm.done(T))
                    act.wait_ge(gr_store.sem, gr_store.freed(b, 1))
                    nc.scalar.copy(gram[:], ps_gram[:, 0:4 * HD].rearrange("p (g j) -> p g j", g=4)).then_inc(gramc_done.sem, 1)

            def body(b, first, last):
                for t in range(NT):
                    if t in (0, 4) and not last:
                        act.wait_ge(tok_mm.sem, tok_mm.done(b * NT + t + 3))
                        load_patches(act, b + 1, t // 4)
                    if t < NT - 1 or not last:
                        z_t(*at(b, t + 1))
                    if t or not first:
                        qk_t(*at(b, t - 1))

            z_t(0, 0, 0)
            images(act, body)
            qk_t(*at(B, -1))

        @block.vector
        def _(dve):
            h_done.start(dve)
            qk_done.start(dve)
            v_done.start(dve)
            dve.wait_ge(weights.sem, weights.done(0))
            for t in range(NT):
                last = nc.vector.tensor_tensor(pos_b[:, t], pos_b[:, t], tok_b[:], ALU.add)
            last.then_inc(posb_ready.sem, 1)
            dve.wait_ge(posb_ready.sem, 1)

            def head(b, t, T):
                k = t % 4
                dve.wait_ge(tok_mm.sem, tok_mm.done(T))
                dve.wait_ge(h_store[k].sem, h_store[k].freed(b * (NT // 4) + t // 4, 1))
                nc.vector.tensor_tensor(hc[:, k, :], ps_tok[:, t % 2, 0:C], pos_b[:, t, :], ALU.add).then_inc(h_done.sem, 1)
                dve.wait_ge(h_done.sem, h_done.done(T))
                nc.vector.bn_stats(stats[:, k, :], hc[:, k, :]).then_inc(st_done.sem, 1)
                dve.wait_ge(posb_ready.sem, 1)
                dve.wait_ge(st_done.sem, st_done.done(T))
                nc.vector.bn_aggr(mv[:, k, :], stats[:, k, :]).then_inc(mv_done.sem, 1)

            def normed(b, t, T):
                k = t % 4
                dve.wait_ge(rstd_done.sem, rstd_done.done(T))
                dve.wait_ge(zt_mm.sem, zt_mm.freed(T, 2))
                nc.vector.tensor_scalar(z[:, t % 2, :], hc[:, k, :], mv[:, k, 0:1], rstd[:, k:k + 1], ALU.subtract, ALU.mult
                                        ).then_inc(z_done.sem, 1)

            def tail(b, t, T):
                dve.wait_ge(qkv_mm.sem, qkv_mm.done(T))
                dve.wait_ge(gram_mm.sem, gram_mm.freed(T, 2))
                if t == 0:
                    dve.wait_ge(a1_store.sem, a1_store.done(b - 1))
                if t == 2:
                    dve.wait_ge(a1_store.sem, a1_store.done(b))
                nc.vector.tensor_tensor(qk[:, t % 2, :], ps_qk[:], b_qkv[:, 0:2 * C], ALU.add).then_inc(qk_done.sem, 1)
                slot = v_store[t % 2]
                dve.wait_ge(slot.sem, slot.freed(b * (NT // 2) + t // 2, 1))
                nc.vector.tensor_tensor(vs[:, t % 2, :], ps_v[:, 0:C], b_qkv[:, 2 * C:3 * C],
                                        ALU.add).then_inc(v_done.sem, 1)

            def body(b, first, last):
                for t in range(NT):
                    tail(*at(b, t))
                    if t < NT - 2 or not last:
                        normed(*at(b, t + 2))
                    if t < NT - 3 or not last:
                        head(*at(b, t + 3))

            for t in range(3):
                head(0, t, t)
            for t in range(2):
                normed(0, t, t)
            images(dve, body)

        @block.tensor
        def _(pe):
            zt_mm.start(pe)
            qkv_mm.start(pe)
            gram_mm.start(pe)
            pe.wait_ge(weights.sem, weights.done(0))

            def tokens(b, t, T):
                if t % 4 == 0:
                    pe.wait_ge(pat_in[t // 4].sem, pat_in[t // 4].done(b))
                pe.wait_ge(h_done.sem, h_done.freed(T, 2))
                pe.matmul(ps_tok[:, t % 2, 0:C], pat[:, t * P:(t + 1) * P], tok_w[:], start=True,
                          stop=True).then_inc(tok_mm.sem, 1)

            def z_t(b, t, T):
                pe.wait_ge(z_done.sem, z_done.done(T))
                pe.wait_ge(ztc_done.sem, ztc_done.freed(T, 1))
                for c in range(CK):
                    last = pe.transpose(ps_zt[:, c, 0:P], z[:, t % 2, c * P:(c + 1) * P], ident[:])
                last.then_inc(zt_mm.sem, 1)

            def qkv(b, t, T):
                pe.wait_ge(ztc_done.sem, ztc_done.done(T))
                pe.wait_ge(v_done.sem, v_done.freed(T, 1))
                for c in range(CK):
                    pe.matmul(ps_qk[:], zt[:, t % 2, c, :], w_qkv[:, c, 0:2 * C], start=(c == 0), stop=(c == CK - 1))
                for c in range(CK):
                    last = pe.matmul(ps_v[:, 0:C], zt[:, t % 2, c, :], w_qkv[:, c, 2 * C:3 * C], start=(c == 0),
                                     stop=(c == CK - 1))
                last.then_inc(qkv_mm.sem, 1)

            def grams(b, t, T):
                pe.wait_ge(qk_done.sem, qk_done.done(T))
                pe.wait_ge(qtc_done.sem, qtc_done.freed(T, 1))
                for g in range(4):
                    last = pe.transpose(ps_qt[:, g, :], qk[:, t % 2, g * P:(g + 1) * P], ident[:])
                last.then_inc(qt_mm.sem, 1)
                if t == 0:
                    pe.wait_ge(gramc_done.sem, gramc_done.freed(b, 1))
                for g in range(4):
                    for j in range(4):
                        w = qk[:, t % 2, g * P + j * HD:g * P + (j + 1) * HD]
                        last = pe.matmul(ps_gram[j * HD:(j + 1) * HD, g * HD:(g + 1) * HD], w, w,
                                         start=(t == 0 and g == 0), stop=(t == NT - 1), skip_group_check=True)
                last.then_inc(gram_mm.sem, 1)

            def body(b, first, last):
                for t in range(NT):
                    qkv(*at(b, t))
                    if t < NT - 1 or not last:
                        z_t(*at(b, t + 1))
                    if t or not first:
                        grams(*at(b, t - 1))
                    if t < NT - 4 or not last:
                        tokens(*at(b, t + 4))

            for t in range(4):
                tokens(0, t, t)
            z_t(0, 0, 0)
            images(pe, body)
            grams(*at(B, -1))


def orthonormal_factors(nc, a, dr):
    with ExitStack() as ctx:
        m = Maker(nc, ctx, "qr")
        g = m.sb("g", [P, HD, HD])
        top = m.sb("top", [P, HD, HD])
        li = m.sb("li", [P, HD, HD])
        lt = m.sb("lt", [P, HD, HD])
        lcol = m.sb("lcol", [P, HD, HD])
        outer = m.sb("outer", [P, HD * HD])
        outer_z = m.sb("outer_z", [P, HD * HD])
        piv = m.sb("piv", [P, HD])
        rpiv = m.sb("rpiv", [P, HD])
        half = m.sb("half", [P, HD])
        root = m.sb("root", [P, HD])
        rroot = m.sb("rroot", [P, HD])
        beta = m.sb("beta", [P, HD])
        rbeta = m.sb("rbeta", [P, HD])
        flip = m.sb("flip", [P, HD])
        den = m.sb("den", [P, HD])
        w = m.sb("w", [P, HD])

        loaded = m.count("loaded", 16 * (1 + B))
        ready = m.count("ready")
        chain = m.ctx.enter_context(nc.semaphore("qr_chain"))
        col_done = m.count("col_done")
        z_done = m.count("z_done")
        zo_done = m.count("zo_done")
        piv_done = m.count("piv_done")
        root_done = m.count("root_done")
        out_done = m.count("out_done")
        stored = m.count("stored", 16)
        block = ctx.enter_context(nc.Block())

        @block.sync
        def _(sp):
            sp.dma_start(g[:], dr["gram_m"]).then_inc(loaded.sem, 16)
            for b in range(B):
                sp.dma_start(top[b * 2 * H:(b + 1) * 2 * H], dr["top_m"][b]).then_inc(loaded.sem, 16)
            sp.wait_ge(out_done.sem, 1)
            sp.dma_start(dr["rt_m"], lt[:]).then_inc(stored.sem, 16)
            sp.wait_ge(stored.sem, 16)

        @block.gpsimd
        def _(pool):
            nc.gpsimd.memset(li[:], 0.0).then_inc(ready.sem, 1)
            pool.wait_ge(ready.sem, 1)
            for j in range(HD):
                last = nc.gpsimd.memset(li[:, j, j:j + 1], 1.0)
            last.then_inc(ready.sem, 1)
            pool.wait_ge(ready.sem, 2)
            nc.gpsimd.memset(half[:], 0.5).then_inc(ready.sem, 1)
            pool.wait_ge(ready.sem, 3)
            for j in range(HD - 1):
                n = HD - 1 - j
                pool.wait_ge(col_done.sem, j + 1)
                if j:
                    pool.wait_ge(z_done.sem, j)
                o = outer_z[:, 0:n * (j + 1)].rearrange("p (i k) -> p i k", i=n)
                nc.gpsimd.tensor_tensor(o, lcol[:, j, j + 1:HD].unsqueeze(2).broadcast_to([P, n, j + 1]),
                                        li[:, j:j + 1, 0:j + 1].broadcast_to([P, n, j + 1]), ALU.mult).then_inc(zo_done.sem, 1)
                pool.wait_ge(zo_done.sem, j + 1)
                nc.gpsimd.tensor_tensor(li[:, j + 1:HD, 0:j + 1], li[:, j + 1:HD, 0:j + 1], o,
                                        ALU.subtract).then_inc(z_done.sem, 1)
            pool.wait_ge(piv_done.sem, 1)
            nc.gpsimd.tensor_tensor(root[:], piv[:], half[:], ALU.pow).then_inc(root_done.sem, 1)

        @block.vector
        def _(dve):
            steps = [0]

            def link(ins):
                steps[0] += 1
                ins.then_inc(chain, 1)
                dve.wait_ge(chain, steps[0])

            dve.wait_ge(loaded.sem, loaded.done(0))
            dve.wait_ge(ready.sem, 3)
            for j in range(HD):
                n = HD - 1 - j
                link(nc.vector.tensor_scalar(piv[:, j:j + 1], g[:, j, j:j + 1], 1e-30, None, ALU.max))
                link(nc.vector.reciprocal(rpiv[:, j:j + 1], piv[:, j:j + 1]))
                if not n:
                    break
                nc.vector.tensor_scalar(lcol[:, j, j + 1:HD], g[:, j, j + 1:HD], rpiv[:, j:j + 1], None,
                                        ALU.mult).then_inc(col_done.sem, 1)
                dve.wait_ge(col_done.sem, j + 1)
                o = outer[:, 0:n * n].rearrange("p (i k) -> p i k", i=n)
                link(nc.vector.tensor_tensor(o, lcol[:, j, j + 1:HD].unsqueeze(2).broadcast_to([P, n, n]),
                                             g[:, j:j + 1, j + 1:HD].broadcast_to([P, n, n]), ALU.mult))
                link(nc.vector.tensor_tensor(g[:, j + 1:HD, j + 1:HD], g[:, j + 1:HD, j + 1:HD], o, ALU.subtract))
            nc.vector.tensor_scalar(flip[:, 0:1], piv[:, 0:1], 0.0, None, ALU.mult).then_inc(piv_done.sem, 1)
            dve.wait_ge(root_done.sem, 1)
            link(nc.vector.reciprocal(rroot[:], root[:]))
            for j in range(HD):
                n = HD - 1 - j
                c = slice(j, j + 1)
                link(nc.vector.tensor_scalar(flip[:, c], top[:, j, c], 0.0, -2.0, ALU.is_ge, ALU.mult))
                link(nc.vector.tensor_scalar(flip[:, c], flip[:, c], 1.0, None, ALU.add))
                nc.vector.tensor_tensor(beta[:, c], flip[:, c], root[:, c], ALU.mult)
                link(nc.vector.tensor_tensor(rbeta[:, c], flip[:, c], rroot[:, c], ALU.mult))
                if not n:
                    break
                link(nc.vector.tensor_tensor(den[:, c], beta[:, c], top[:, j, c], ALU.subtract))
                link(nc.vector.reciprocal(den[:, c], den[:, c]))
                link(nc.vector.scalar_tensor_tensor(w[:, 0:n], g[:, j, j + 1:HD], rbeta[:, c], top[:, j, j + 1:HD],
                                                    ALU.mult, ALU.subtract))
                link(nc.vector.tensor_scalar(w[:, 0:n], w[:, 0:n], den[:, c], None, ALU.mult))
                o = outer[:, 0:n * n].rearrange("p (i k) -> p i k", i=n)
                link(nc.vector.tensor_tensor(o, top[:, j + 1:HD, c].broadcast_to([P, n, n]),
                                             w[:, 0:n].unsqueeze(1).broadcast_to([P, n, n]), ALU.mult))
                link(nc.vector.tensor_tensor(top[:, j + 1:HD, j + 1:HD], top[:, j + 1:HD, j + 1:HD], o, ALU.subtract))
            dve.wait_ge(z_done.sem, HD - 1)
            nc.vector.tensor_tensor(lt[:].rearrange("p k i -> p i k"), li[:], rbeta[:].unsqueeze(2).broadcast_to([P, HD, HD]),
                                    ALU.mult).then_inc(out_done.sem, 1)


def split_operands(nc, a, dr):
    with ExitStack() as ctx:
        m = Maker(nc, ctx, "p2")
        rt = m.sb("rt", [P, 2, 4, P])
        qt = m.sb("qt", [P, 2, 4, N])
        hi = m.sb("hi", [P, 2, 2, 4, N], F16)
        lo = m.sb("lo", [P, 2, 2, 4, N], F16)
        ps = [m.ps(f"ps{k}", [P, 512]) for k in range(4)]
        zeroed = m.count("zeroed")
        qt_in = [m.count(f"qt_in{s}", 16 * 5) for s in range(2)]
        mm = m.count("mm")
        img_mm = m.count("img_mm", credit=2)
        hi_o = m.count("hi_o")
        lo_o = m.count("lo_o", credit=4)
        hi_q = m.count("hi_q", credit=2)
        lo_q = m.count("lo_q", credit=2)
        stores = [m.count(f"stores{s}", 16 * 16, credit=1) for s in range(2)]
        block = ctx.enter_context(nc.Block())

        @block.sync
        def _(sp):
            for s in range(2):
                stores[s].start(sp)
            sp.wait_ge(zeroed.sem, 1)
            with sp.Fori(0, B // 2) as b2:
                for s in range(2):
                    b = b2 * 2 + s
                    sp.wait_ge(img_mm.sem, img_mm.freed(b, 2))
                    sp.wait_ge(lo_q.sem, lo_q.freed(b, 2))
                    sp.dma_start(qt[:, s], dr["qt"][ds(b, 1)]).then_inc(qt_in[s].sem, 16)
                    for j in range(4):
                        sp.dma_start(rt[j * HD:(j + 1) * HD, s, :, j * HD:(j + 1) * HD],
                                     dr["rt"][ds(b, 1), j]).then_inc(qt_in[s].sem, 16)

        @block.gpsimd
        def _(pool):
            lo_q.start(pool)
            nc.gpsimd.memset(rt[:], 0.0).then_inc(zeroed.sem, 1)
            with pool.Fori(0, B // 2) as b2:
                for s in range(2):
                    b = b2 * 2 + s
                    pool.wait_ge(hi_q.sem, hi_q.done(b))
                    nc.gpsimd.tensor_tensor(lo[:, s, 0], qt[:, s], hi[:, s, 0], ALU.subtract).then_inc(lo_q.sem, 1)

        @block.scalar
        def _(act):
            hi_q.start(act)
            with act.Fori(0, B // 2) as b2:
                for s in range(2):
                    b = b2 * 2 + s
                    act.wait_ge(qt_in[s].sem, qt_in[s].done(b2))
                    act.wait_ge(stores[s].sem, stores[s].freed(b2, 1))
                    nc.scalar.copy(hi[:, s, 0], qt[:, s]).then_inc(hi_q.sem, 1)
                    for g in range(4):
                        for n in range(2):
                            u = b * 8 + (2 * g + n)
                            act.wait_ge(mm.sem, mm.done(u))
                            nc.scalar.mul(hi[:, s, 1, g, n * 512:(n + 1) * 512], ps[(2 * g + n) % 4][:], GR).then_inc(hi_o.sem, 1)
                    act.wait_ge(lo_q.sem, lo_q.done(b))
                    act.wait_ge(lo_o.sem, lo_o.done(b * 8 + 7))
                    act.wait_ge(hi_o.sem, hi_o.done(b * 8 + 7))
                    act.wait_ge(hi_q.sem, hi_q.done(b))
                    for y in range(2):
                        for kind in range(2):
                            for part, tile in ((0, hi), (1, lo)):
                                for pr in range(2):
                                    act.dma_start(dr["parts_st"][ds(b, 1), y, :, kind, part, pr],
                                                  tile[pr * 64:(pr + 1) * 64, s, kind, 2 * y:2 * y + 2, :]
                                                  ).then_inc(stores[s].sem, 16)
            for s in range(2):
                act.wait_ge(stores[s].sem, stores[s].done(B // 2 - 1))

        @block.vector
        def _(dve):
            lo_o.start(dve)
            with dve.Fori(0, B // 2) as b2:
                for s in range(2):
                    b = b2 * 2 + s
                    for g in range(4):
                        for n in range(2):
                            u = b * 8 + (2 * g + n)
                            dve.wait_ge(hi_o.sem, hi_o.done(u))
                            c = slice(n * 512, (n + 1) * 512)
                            nc.vector.scalar_tensor_tensor(lo[:, s, 1, g, c], ps[(2 * g + n) % 4][:], GR, hi[:, s, 1, g, c],
                                                           ALU.mult, ALU.subtract).then_inc(lo_o.sem, 1)

        @block.tensor
        def _(pe):
            img_mm.start(pe)
            with pe.Fori(0, B // 2) as b2:
                for s in range(2):
                    b = b2 * 2 + s
                    pe.wait_ge(qt_in[s].sem, qt_in[s].done(b2))
                    for g in range(4):
                        for n in range(2):
                            u = b * 8 + (2 * g + n)
                            pe.wait_ge(lo_o.sem, lo_o.freed(u, 4))
                            last = pe.matmul(ps[(2 * g + n) % 4][:], rt[:, s, g, :], qt[:, s, g, n * 512:(n + 1) * 512],
                                             start=True, stop=True).then_inc(mm.sem, 1)
                    pe.wait_ge(mm.sem, mm.done(b * 8 + 7))
                    pe.sem_inc(img_mm.sem, 1)


def attention(nc, a, dr, hs):
    with ExitStack() as ctx:
        m = Maker(nc, ctx, "p3")
        NB = B * NT
        ident = m.sb("ident", [P, P])
        w_proj = m.sb("w_proj", [P, CK, C])
        b_proj = m.sb("b_proj", [P, 1, C])
        mix_w = m.sb("mix_w", [P, 3, H])
        bn = m.sb("bn", [P, 5, 3])
        mask = m.sb("mask", [P, GS])
        conv_b = m.sb("conv_b", [P, 1])
        half = m.sb("half", [P, 3])
        eps = m.sb("eps", [P, 3])
        ones = m.sb("ones", [P, 1])
        one = m.sb("one", [P, 1], F16)
        coef = m.sb("coef", [P, 4, 3])
        cw = m.sb("cw", [P, 2, 3, H])
        mixer = m.sb("mixer", [P, 3, H, GS])
        shifter = m.sb("shifter", [P, 3, H, GS])
        const = m.sb("const", [P, 1])
        keys = m.sb("keys", [P, 2, 4, N], F16)
        v = m.sb("v", [P, NT, C])
        q_in = m.sb("q_in", [P, 16, P], F16)
        q_bd = m.sb("q_bd", [P, 16, NG, 2 * GS], F16)
        mix_h = m.sb("mix_h", [P, 2, P], F16)
        mix_l = m.sb("mix_l", [P, 2, P], F16)
        const_x = m.sb("const_x", [P, 1])
        s_h = m.sb("s_h", [P, 4, 2, 512], F16)
        s_l = m.sb("s_l", [P, 4, 2, 512], F16)
        s_dd = m.sb("s_dd", [P, 2, 512])
        s_gg = m.sb("s_gg", [P, 4, 512])
        mx = m.sb("mx", [P, 2, 2])
        mxc = m.sb("mxc", [P, 2])
        bias = m.sb("bias", [P, 2])
        p = m.sb("p", [P, 2, N])
        pt = m.sb("pt", [P, NT, H, P])
        sums = m.sb("sums", [P, 2, 2])
        total = m.sb("total", [P, 2])
        rden = m.sb("rden", [P, 2])
        ot = m.sb("ot", [P, CK, P])
        delta = m.sb("delta", [P, 1, C])

        ps_d = m.ps("ps_d", [P, 2, 512])
        ps_g = m.ps("ps_g", [P, 512])
        ps_a = m.ps("ps_a", [P, 2, 512])
        ps_t = m.ps("ps_t", [P, NT, P])
        ps_m = m.ps("ps_m", [P, 1, 512])

        consts = m.count("consts", 16 * 7)
        set_up = m.count("set_up")
        pool_set = m.count("pool_set")
        fold = m.ctx.enter_context(nc.semaphore("p3_fold"))
        powed = m.count("powed")
        k_in = {(kind, mh): m.count(f"k_in_{kind}{mh}", 64) for kind in range(2) for mh in range(2)}
        v_in = m.count("v_in", 16)
        qn_in = m.count("qn_in", 64)
        qb_done = m.count("qb_done", credit=2)
        d_mm = m.count("d_mm", credit=2 * NG)
        g_mm = m.count("g_mm", credit=2 * NG)
        mix_mm = m.count("mix_mm", credit=4)
        tr_mm = m.count("tr_mm", credit=2)
        pv_mm = m.count("pv_mm", credit=2)
        pj_mm = m.count("pj_mm")
        dh_done = m.count("dh_done", 3)
        dl_done = m.count("dl_done", credit=2)
        gg_done = m.count("gg_done", credit=1)
        dd_done = m.count("dd_done", credit=2)
        mx_done = m.count("mx_done")
        mxc_done = m.count("mxc_done")
        bias_done = m.count("bias_done")
        p_done = m.count("p_done", credit=2)
        total_done = m.count("total_done")
        pt_done = m.count("pt_done", credit=1)
        rden_done = m.count("rden_done")
        pn_done = m.count("pn_done")
        otc_done = m.count("otc_done")
        delta_done = m.count("delta_done", credit=1)
        h_done = m.count("h_done")

        block = ctx.enter_context(nc.Block())

        def blocks(eng, body):
            body(0, True, False)
            with eng.Fori(1, NB - 1) as blk:
                body(blk, False, False)
            body(NB - 1, False, True)

        @block.sync
        def _(sp):
            for tile, name in ((ident, "ident"), (w_proj, "w_proj"), (b_proj, "b_proj"), (mix_w, "mix_w"), (bn, "bn"),
                               (mask, "mask"), (conv_b, "conv_b")):
                sp.dma_start(tile[:], a[name]).then_inc(consts.sem, 16)

            def queries(b, nb, blk):
                col = sp.snap(nb * P) if not isinstance(nb, int) else nb * P
                if blk is not None:
                    sp.wait_ge(qb_done.sem, qb_done.done(2 * blk - 1))
                for hp in range(2):
                    for dup in range(2):
                        r = hp * 64 + dup * HD
                        sp.dma_start(q_in[r:r + HD], dr["parts"][ds(b, 1), 0, hp * HD:(hp + 1) * HD, :, ds(col, P)]
                                     ).then_inc(qn_in.sem, 16)

            with sp.Fori(0, B) as b:
                sp.wait_ge(qb_done.sem, qb_done.done(2 * NT * b - 1))
                queries(b, 0, None)
                for mh in range(2):
                    for kind, sem in ((0, d_mm), (1, g_mm)):
                        sp.wait_ge(sem.sem, sem.done(b * (2 * NG * NT) - 2 + mh))
                        for hp in range(2):
                            for part in range(2):
                                r = hp * 64 + part * HD
                                sp.dma_start(keys[r:r + HD, kind, :, mh * 512:(mh + 1) * 512],
                                             dr["keys"][ds(b, 1), hp * HD:(hp + 1) * HD, kind, part, :, mh * 512:(mh + 1) * 512]
                                             ).then_inc(k_in[kind, mh].sem, 16)
                sp.wait_ge(pv_mm.sem, pv_mm.done(b * NT - 1))
                sp.dma_start(v[:], dr["v"][ds(b, 1)]).then_inc(v_in.sem, 16)
                with sp.Fori(1, NT) as nb:
                    queries(b, nb, b * NT + nb)

        @block.gpsimd
        def _(pool):
            qb_done.start(pool)
            nc.gpsimd.memset(q_bd[:], 0.0).then_inc(pool_set.sem, 1)
            nc.gpsimd.memset(half[:], -0.5).then_inc(pool_set.sem, 1)
            nc.gpsimd.memset(eps[:], EPS).then_inc(pool_set.sem, 1)
            nc.gpsimd.memset(ones[:], 1.0).then_inc(pool_set.sem, 1)
            nc.gpsimd.memset(one[:], 1.0).then_inc(pool_set.sem, 1)
            pool.wait_ge(pool_set.sem, 5)
            pool.wait_ge(consts.sem, consts.done(0))
            nc.gpsimd.tensor_tensor(coef[:, 0], bn[:, 3], eps[:], ALU.add).then_inc(powed.sem, 1)
            pool.wait_ge(powed.sem, 1)
            nc.gpsimd.tensor_tensor(coef[:, 1], coef[:, 0], half[:], ALU.pow).then_inc(powed.sem, 1)
            pool.wait_ge(powed.sem, 2)
            with pool.Fori(0, NB) as blk:
                for hf in range(2):
                    pool.wait_ge(qn_in.sem, qn_in.done(blk))
                    pool.wait_ge(g_mm.sem, g_mm.freed(blk * (2 * NG) + (8 * hf + 7), 2 * NG))
                    for hp in range(2):
                        r = slice(hp * 64, hp * 64 + 64)
                        src = q_in[r, :, hf * 64:hf * 64 + 64].rearrange("p x (g n) -> p x g n", g=4)
                        last = nc.gpsimd.tensor_tensor(q_bd[r, :, 4 * hf:4 * hf + 4, hp * GS:(hp + 1) * GS], src, one[r].unsqueeze(2).unsqueeze(3).broadcast_to([64, 16, 4, GS]), ALU.mult)
                    last.then_inc(qb_done.sem, 1)

        @block.scalar
        def _(act):
            gg_done.start(act)
            p_done.start(act)

            def high_part(u, k):
                act.wait_ge(d_mm.sem, d_mm.done(u))
                act.wait_ge(mix_mm.sem, mix_mm.freed(u, 4))
                nc.scalar.copy(s_h[:, k, 0, :], ps_d[:, k % 2, :]).then_inc(dh_done.sem, 1)

            def squares(u, k):
                act.wait_ge(dd_done.sem, dd_done.freed(u, 2))
                nc.scalar.activation(s_dd[:, k % 2, :], ps_d[:, k % 2, :], ACT.Square, scale=DX).then_inc(dh_done.sem, 1)
                nc.scalar.activation(s_h[:, k, 1, :], ps_d[:, k % 2, :], ACT.Square, scale=DX).then_inc(dh_done.sem, 1)

            def grass(u, k):
                act.wait_ge(g_mm.sem, g_mm.done(u))
                act.wait_ge(mix_mm.sem, mix_mm.freed(u, 4))
                nc.scalar.activation(s_gg[:, k, :], ps_g[:], ACT.Square).then_inc(gg_done.sem, 1)

            def weights(s, g, mh):
                if mh == 0:
                    act.wait_ge(bias_done.sem, bias_done.done(s))
                    act.wait_ge(tr_mm.sem, tr_mm.freed(s, 2))
                nc.scalar.activation(p[:, g % 2, mh * 512:(mh + 1) * 512], ps_a[:, mh, :], ACT.Exp,
                                     scale=1 / MX, bias=bias[:, g % 2:g % 2 + 1], accum_out=sums[:, g % 2, mh:mh + 1]
                                     ).then_inc(p_done.sem, 1)

            def body(blk, first, last):
                for g in range(NG):
                    s = blk * NG + g
                    more = not (last and g == NG - 1)
                    k = 2 * ((g + 1) % 2)
                    if more:
                        high_part(2 * s + 2, k)
                        squares(2 * s + 2, k)
                        grass(2 * s + 2, k)
                        high_part(2 * s + 3, k + 1)
                    weights(s, g, 0)
                    weights(s, g, 1)
                    if more:
                        squares(2 * s + 3, k + 1)
                        grass(2 * s + 3, k + 1)
                    if g == 2 and not first:
                        outputs_t(blk - 1)

            def outputs_t(blk):
                act.wait_ge(pv_mm.sem, pv_mm.done(blk))
                nc.scalar.copy(ot[:].rearrange("p c n -> p (c n)"), ps_m[:, 0, 0:CK * P]).then_inc(otc_done.sem, 1)

            for u in range(2):
                high_part(u, u)
                squares(u, u)
                grass(u, u)
            blocks(act, body)
            outputs_t(NB - 1)

        @block.vector
        def _(dve):
            pt_done.start(dve)
            delta_done.start(dve)
            dl_done.start(dve)
            dd_done.start(dve)
            steps = [0]

            def link(ins):
                steps[0] += 1
                ins.then_inc(fold, 1)
                dve.wait_ge(fold, steps[0])

            dve.wait_ge(consts.sem, consts.done(0))
            dve.wait_ge(powed.sem, 2)
            link(nc.vector.tensor_tensor(coef[:, 0], bn[:, 0], coef[:, 1], ALU.mult))
            link(nc.vector.tensor_tensor(coef[:, 2], coef[:, 0], bn[:, 4], ALU.mult))
            for kind, by in enumerate((MX, MX / DX ** 2, MX / GR ** 4)):
                link(nc.vector.tensor_scalar(coef[:, 2, kind:kind + 1], coef[:, 2, kind:kind + 1], by, None, ALU.mult))
            link(nc.vector.tensor_tensor(coef[:, 3], bn[:, 2], coef[:, 0], ALU.mult))
            link(nc.vector.tensor_tensor(coef[:, 3], bn[:, 1], coef[:, 3], ALU.subtract))
            for n, w in ((2, 0), (3, 1)):
                link(nc.vector.tensor_tensor(cw[:, w], mix_w[:], coef[:, n].unsqueeze(2).broadcast_to([P, 3, H]), ALU.mult))
                for kind in range(3):
                    link(nc.vector.tensor_tensor((mixer, shifter)[w][:, kind], cw[:, w, kind].unsqueeze(2).broadcast_to([P, H, GS]),
                                                 mask[:].unsqueeze(1).broadcast_to([P, H, GS]), ALU.mult))
            link(nc.vector.tensor_copy(mix_h[:], mixer[:, 0:2].rearrange("p k o n -> p k (o n)")))
            nc.vector.tensor_tensor(mix_l[:], mixer[:, 0:2].rearrange("p k o n -> p k (o n)"), mix_h[:], ALU.subtract
                                    ).then_inc(set_up.sem, 1)
            dve.wait_ge(pv_mm.sem, 2)
            link(nc.vector.tensor_tensor(const[:], ps_m[:, 0, 0:1], conv_b[:], ALU.add))
            link(nc.vector.tensor_scalar(const_x[:], const[:], MX, None, ALU.mult))

            def low_dots(u, k):
                dve.wait_ge(dh_done.sem, dh_done.done(u))
                nc.vector.tensor_tensor(s_l[:, k, 0, :], ps_d[:, k % 2, :], s_h[:, k, 0, :], ALU.subtract).then_inc(dl_done.sem, 1)

            def low_squares(k):
                nc.vector.tensor_tensor(s_l[:, k, 1, :], s_dd[:, k % 2, :], s_h[:, k, 1, :], ALU.subtract).then_inc(dd_done.sem, 1)

            def maximum(s, g, mh):
                dve.wait_ge(mix_mm.sem, mix_mm.done(2 * s + mh))
                nc.vector.tensor_reduce(mx[:, g % 2, mh:mh + 1], ps_a[:, mh, :], AX_X, ALU.max).then_inc(mx_done.sem, 1)

            def shift(s, g):
                c = slice(g % 2, g % 2 + 1)
                dve.wait_ge(mx_done.sem, mx_done.done(2 * s + 1))
                nc.vector.tensor_scalar(mxc[:, c], mx[:, g % 2, 0:1], mx[:, g % 2, 1:2], const_x[:], ALU.max, ALU.add
                                        ).then_inc(mxc_done.sem, 1)
                dve.wait_ge(mxc_done.sem, mxc_done.done(s))
                nc.vector.tensor_scalar(bias[:, c], mxc[:, c], -1 / MX, const[:], ALU.mult, ALU.add).then_inc(bias_done.sem, 1)

            def normalised(s, g):
                c = slice(g % 2, g % 2 + 1)
                dve.wait_ge(p_done.sem, p_done.done(2 * s + 1))
                nc.vector.tensor_tensor(total[:, c], sums[:, g % 2, 0:1], sums[:, g % 2, 1:2], ALU.add).then_inc(total_done.sem, 1)
                dve.wait_ge(total_done.sem, total_done.done(s))
                nc.vector.reciprocal(rden[:, c], total[:, c]).then_inc(rden_done.sem, 1)
                dve.wait_ge(rden_done.sem, rden_done.done(s))
                nc.vector.tensor_scalar(p[:, g % 2, :], p[:, g % 2, :], rden[:, c], None, ALU.mult).then_inc(pn_done.sem, 1)

            def weights_t(s, g, blk, first):
                dve.wait_ge(tr_mm.sem, tr_mm.done(s))
                if g == 0 and not first:
                    dve.wait_ge(pv_mm.sem, pv_mm.done(blk - 1))
                nc.vector.tensor_copy(pt[:, :, :, g * GS:(g + 1) * GS], ps_t[:].rearrange("p t (o n) -> p t o n", o=H)
                                      ).then_inc(pt_done.sem, 1)

            def residual(blk):
                dve.wait_ge(pj_mm.sem, pj_mm.done(blk))
                nc.vector.tensor_tensor(delta[:], ps_m[:, :, 0:C], b_proj[:], ALU.add).then_inc(delta_done.sem, 1)
                dve.wait_ge(delta_done.sem, delta_done.done(blk))
                nc.vector.tensor_tensor(hs[:, ds(blk, 1), :], hs[:, ds(blk, 1), :], delta[:], ALU.add).then_inc(h_done.sem, 1)

            def body(blk, first, last):
                for g in range(NG):
                    s = blk * NG + g
                    more = not (last and g == NG - 1)
                    k = 2 * ((g + 1) % 2)
                    maximum(s, g, 0)
                    if g or not first:
                        normalised(s - 1, (g - 1) % NG)
                    if more:
                        low_dots(2 * s + 2, k)
                    maximum(s, g, 1)
                    shift(s, g)
                    if more:
                        low_squares(k)
                    if g or not first:
                        weights_t(s - 1, (g - 1) % NG, blk, first)
                    if more:
                        low_dots(2 * s + 3, k + 1)
                        low_squares(k + 1)
                    if g == 4 and not first:
                        residual(blk - 1)

            for u in range(2):
                low_dots(u, u)
                low_squares(u)
            blocks(dve, body)
            normalised(NB * NG - 1, NG - 1)
            weights_t(NB * NG - 1, NG - 1, NB - 1, False)
            residual(NB - 1)
            dve.wait_ge(h_done.sem, h_done.done(NB - 1))

        @block.tensor
        def _(pe):
            d_mm.start(pe)
            g_mm.start(pe)
            mix_mm.start(pe)
            tr_mm.start(pe)
            pe.sem_inc(pv_mm.sem, 1)
            pe.wait_ge(pool_set.sem, 5)
            pe.wait_ge(set_up.sem, 1)
            for kind in range(3):
                last_mm = pe.matmul(ps_m[:, 0, 0:1], shifter[:, kind].rearrange("p o n -> p (o n)"), ones[:], start=(kind == 0),
                                    stop=(kind == 2))
            last_mm.then_inc(pv_mm.sem, 1)

            def scores(blk, g, mh, kind):
                u = 2 * (blk * NG + g) + mh
                if g % 4 == 0:
                    pe.wait_ge(qb_done.sem, qb_done.done(2 * blk + g // 4))
                if g == 0:
                    pe.wait_ge(k_in[kind, mh].sem, k_in[kind, mh].done(blk // NT))
                if kind:
                    pe.wait_ge(gg_done.sem, gg_done.freed(u, 1))
                else:
                    pe.wait_ge(dl_done.sem, dl_done.freed(u, 2))
                ps = ps_g[:] if kind else ps_d[:, mh, :]
                for part in range(2):
                    for pair in range(4):
                        last_mm = pe.matmul(ps[pair * 32:(pair + 1) * 32], q_bd[:, kind * 8 + part * 4 + pair, g, :],
                                            keys[:, kind, pair, mh * 512:(mh + 1) * 512], start=(part == 0),
                                            stop=(part == 1))
                last_mm.then_inc((g_mm if kind else d_mm).sem, 1)

            def mixed(s, g, mh):
                u = 2 * s + mh
                k = 2 * (g % 2) + mh
                pe.wait_ge(p_done.sem, p_done.freed(u, 2))
                for kind, low in enumerate((dl_done, dd_done)):
                    pe.wait_ge(low.sem, low.done(u))
                    pe.matmul(ps_a[:, mh, :], mix_h[:, kind], s_h[:, k, kind, :], start=(kind == 0), stop=False)
                    pe.matmul(ps_a[:, mh, :], mix_h[:, kind], s_l[:, k, kind, :], start=False, stop=False)
                    pe.matmul(ps_a[:, mh, :], mix_l[:, kind], s_h[:, k, kind, :], start=False, stop=False)
                pe.wait_ge(gg_done.sem, gg_done.done(u))
                pe.matmul(ps_a[:, mh, :], mixer[:, 2].rearrange("p o n -> p (o n)"), s_gg[:, k, :], start=False, stop=True
                          ).then_inc(mix_mm.sem, 1)

            def transposed(s, g):
                pe.wait_ge(pn_done.sem, pn_done.done(s))
                pe.wait_ge(pt_done.sem, pt_done.freed(s, 1))
                for t in range(NT):
                    last_mm = pe.transpose(ps_t[:, t, :], p[:, g % 2, t * P:(t + 1) * P], ident[:])
                last_mm.then_inc(tr_mm.sem, 1)

            def weighted(blk):
                pe.wait_ge(pt_done.sem, pt_done.done(blk * NG + NG - 1))
                pe.wait_ge(v_in.sem, v_in.done(blk // NT))
                pe.wait_ge(delta_done.sem, delta_done.freed(blk, 1))
                for t in range(NT):
                    for c in range(CK):
                        for o in range(4 * c, 4 * c + 4):
                            r = o % 4 * HD
                            last_mm = pe.matmul(ps_m[r:r + HD, 0, c * P:(c + 1) * P], v[:, t, o * HD:(o + 1) * HD], pt[:, t, o, :],
                                                start=(t == 0 and c == 0), stop=(t == NT - 1), skip_group_check=True)
                last_mm.then_inc(pv_mm.sem, 1)

            def projected(blk):
                pe.wait_ge(otc_done.sem, otc_done.done(blk))
                for c in range(CK):
                    last_mm = pe.matmul(ps_m[:, 0, 0:C], ot[:, c, :], w_proj[:, c, :], start=(c == 0), stop=(c == CK - 1))
                last_mm.then_inc(pj_mm.sem, 1)

            def body(blk, first, last):
                for g in range(NG):
                    s = blk * NG + g
                    ahead = (blk, g + 1) if g < NG - 1 else (blk + 1, 0)
                    more = not (last and g == NG - 1)
                    mixed(s, g, 0)
                    if g == 1 and not first:
                        weighted(blk - 1)
                    if more:
                        scores(*ahead, 0, 0)
                    mixed(s, g, 1)
                    if more:
                        scores(*ahead, 0, 1)
                        scores(*ahead, 1, 0)
                    if g or not first:
                        transposed(s - 1, (g - 1) % NG)
                    if more:
                        scores(*ahead, 1, 1)
                    if g == 3 and not first:
                        projected(blk - 1)

            for mh in range(2):
                for kind in range(2):
                    scores(0, 0, mh, kind)
            blocks(pe, body)
            transposed(NB * NG - 1, NG - 1)
            weighted(NB - 1)
            projected(NB - 1)


def experts(nc, a, hs, out):
    with ExitStack() as ctx:
        m = Maker(nc, ctx, "p4")
        NB = B * N // 512
        TB = 512 // P
        HT = F // P
        ident = m.sb("ident", [P, P])
        norm = m.sb("norm", [P, 2, CK])
        w_r = m.sb("w_r", [P, CK, E])
        b_r = m.sb("b_r", [P, E])
        b1 = m.sb("b1", [P, E, HT])
        b2 = m.sb("b2", [E, C])
        iota = m.sb("iota", [P, E])
        half = m.sb("half", [P, TB])
        eps = m.sb("eps", [P, TB])
        carrier = m.sb("carrier", [P, 128])
        stage = m.sb("stage", [P, 2, 2, 1024])
        w1 = m.sb("w1", [P, 2, E, CK, F], F16)
        w2 = m.sb("w2", [P, 2, E, HT, C], F16)
        hc = m.sb("hc", [P, TB, C])
        stats = m.sb("stats", [P, TB, 6])
        mv = m.sb("mv", [P, TB, 2])
        veps = m.sb("veps", [P, TB])
        rstd = m.sb("rstd", [P, TB])
        z = m.sb("z", [P, TB, C])
        xh = m.sb("xh", [P, TB, C])
        xf = m.sb("xf", [P, CK, 512])
        x_hi = m.sb("x_hi", [P, CK, 512], F16)
        x_lo = m.sb("x_lo", [P, CK, 512], F16)
        logit = m.sb("logit", [P, TB, E])
        top = m.sb("top", [P, TB, 8])
        idx = m.sb("idx", [P, TB, 8], mybir.dt.uint32)
        idxf = m.sb("idxf", [P, TB, 2])
        gap = m.sb("gap", [P, TB])
        th = m.sb("th", [P, TB])
        wt = m.sb("wt", [P, 2, TB])
        hot = m.sb("hot", [P, 2, TB, E])
        gate_next = m.sb("gate_next", [P, TB, E])
        gate = m.sb("gate", [P, TB, E])
        gate_t = m.sb("gate_t", [E, 512])
        g32 = m.sb("g32", [P, HT, 512])
        g_hi = m.sb("g_hi", [P, 2, HT, 512], F16)
        g_lo = m.sb("g_lo", [P, 2, HT, 512], F16)
        y = m.sb("y", [P, TB, C])
        o = m.sb("o", [P, TB, C])

        ps_h = [m.ps(f"ps_h{k}", [P, 512]) for k in range(4)]
        ps_y = [m.ps(f"ps_y{k}", [P, 512]) for k in range(2)]
        ps_x = m.ps("ps_x", [P, 512])
        ps_r = m.ps("ps_r", [P, 512])

        consts = m.count("consts", 16 * 7)
        w_in = [m.count(f"w_in{k}", 32) for k in range(2)]
        w_hi_done = m.count("w_hi_done")
        w_done = m.count("w_done", credit=2)
        pool_set = m.count("pool_set")
        hc_in = m.count("hc_in", 16)
        st_done = m.count("st_done")
        mv_done = m.count("mv_done")
        ve_done = m.count("ve_done")
        rstd_done = m.count("rstd_done")
        z_done = m.count("z_done")
        xh_done = m.count("xh_done", credit=1)
        xt_mm = m.count("xt_mm", credit=2)
        xf_done = m.count("xf_done")
        x_hi_done = m.count("x_hi_done")
        x_lo_done = m.count("x_lo_done", credit=1)
        r_mm = m.count("r_mm")
        logit_done = m.count("logit_done")
        top_done = m.count("top_done")
        idx_done = m.count("idx_done")
        gap_done = m.count("gap_done")
        th_done = m.count("th_done")
        g_step = m.count("g_step", 1)
        gate_done = m.count("gate_done")
        gt_mm = m.count("gt_mm")
        gt_done = m.count("gt_done", credit=1)
        gate_set = m.count("gate_set", credit=1)
        h_mm = m.count("h_mm", credit=1)
        g32_done = m.count("g32_done")
        gh_done = m.count("gh_done", credit=4)
        gl_done = m.count("gl_done", credit=4)
        y_mm = m.count("y_mm", credit=8)
        acc_done = m.count("acc_done", credit=2)
        stored = m.count("stored", 16, credit=1)

        YU = TB * (E + 1)

        block = ctx.enter_context(nc.Block())

        def blocks(eng, body):
            with eng.Fori(0, NB - 1) as blk:
                body(blk, False)
            body(NB - 1, True)

        @block.sync
        def _(sp):
            stored.start(sp)
            for tile, name in ((ident, "ident"), (norm, "norm"), (w_r, "w_r"), (b_r, "b_r"), (b1, "b1"), (b2, "b2"),
                               (iota, "iota")):
                sp.dma_start(tile[:], a[name]).then_inc(consts.sem, 16)
            sp.dma_start(hc[:], hs[:, 0:TB, :]).then_inc(hc_in.sem, 16)
            for e in range(E):
                sp.wait_ge(w_done.sem, w_done.freed(e, 2))
                sp.dma_start(stage[:, e % 2, 0], a["w1"][:, e]).then_inc(w_in[e % 2].sem, 16)
                sp.dma_start(stage[:, e % 2, 1], a["w2"][:, e]).then_inc(w_in[e % 2].sem, 16)

            def body(blk, last):
                if not last:
                    sp.wait_ge(acc_done.sem, acc_done.done(blk * YU + (TB - 1)))
                    sp.dma_start(hc[:], hs[:, ds(blk * TB + TB, TB), :]).then_inc(hc_in.sem, 16)
                sp.wait_ge(acc_done.sem, acc_done.done(blk * YU + (YU - 1)))
                sp.dma_start(out[ds(blk * TB, TB)].rearrange("t p c -> p t c"), o[:]).then_inc(stored.sem, 16)

            blocks(sp, body)
            sp.wait_ge(stored.sem, stored.done(NB - 1))

        @block.gpsimd
        def _(pool):
            nc.gpsimd.memset(half[:], -0.5).then_inc(pool_set.sem, 1)
            nc.gpsimd.memset(eps[:], EPS).then_inc(pool_set.sem, 1)
            nc.gpsimd.memset(carrier[:], 1.0).then_inc(pool_set.sem, 1)
            pool.wait_ge(pool_set.sem, 3)

            with pool.Fori(0, 2 * NB) as n:
                pool.wait_ge(mv_done.sem, mv_done.done(n))
                nc.gpsimd.tensor_tensor(veps[:], mv[:, :, 1], eps[:], ALU.add).then_inc(ve_done.sem, 1)
                pool.wait_ge(ve_done.sem, ve_done.done(n))
                nc.gpsimd.tensor_tensor(rstd[:], veps[:], half[:], ALU.pow).then_inc(rstd_done.sem, 1)

        @block.scalar
        def _(act):
            gt_done.start(act)
            gh_done.start(act)

            def scaled(blk, c):
                act.wait_ge(xt_mm.sem, xt_mm.done(2 * blk + c))
                if c == 0:
                    act.wait_ge(x_lo_done.sem, x_lo_done.freed(blk, 1))
                nc.scalar.activation(xf[:, c, :], ps_x[:], ACT.Identity, bias=norm[:, 1, c:c + 1],
                                     scale=norm[:, 0, c:c + 1]).then_inc(xf_done.sem, 1)

            def tanh(blk):
                act.wait_ge(gap_done.sem, gap_done.done(blk))
                nc.scalar.activation(th[:], gap[:], ACT.Tanh, scale=0.5).then_inc(th_done.sem, 1)

            def gates_t(blk):
                act.wait_ge(gt_mm.sem, gt_mm.done(blk))
                nc.scalar.copy(gate_t[:], ps_x[0:E, :]).then_inc(gt_done.sem, 1)

            def high_part(blk):
                act.wait_ge(xf_done.sem, xf_done.done(2 * blk + 1))
                act.wait_ge(h_mm.sem, h_mm.freed(blk * (4 * E), 1))
                nc.scalar.copy(x_hi[:], xf[:]).then_inc(x_hi_done.sem, 1)

            steps = {3: lambda blk: scaled(blk, 0), 4: lambda blk: scaled(blk, 1), 5: tanh, 7: lambda blk: (high_part(blk), gates_t(blk))}

            def hidden(blk, e):
                for t in range(HT):
                    u = blk * (4 * E) + (4 * e + t)
                    act.wait_ge(h_mm.sem, h_mm.done(u))
                    act.wait_ge(gl_done.sem, gl_done.freed(u, 4))
                    nc.scalar.activation(g32[:, t, :], ps_h[t][:], ACT.Gelu, bias=b1[:, e, t:t + 1]).then_inc(g32_done.sem, 1)
                    act.wait_ge(y_mm.sem, y_mm.done(blk * YU + (4 * e - 1 if e > 1 else 4 * e - 5)))
                    nc.scalar.activation(g_hi[:, e % 2, t, :], ps_h[t][:], ACT.Gelu, bias=b1[:, e, t:t + 1]
                                         ).then_inc(gh_done.sem, 1)

            for e in range(E):
                act.wait_ge(w_in[e % 2].sem, w_in[e % 2].done(e // 2))
                nc.scalar.copy(w1[:, 0, e].rearrange("p c n -> p (c n)"), stage[:, e % 2, 0])
                nc.scalar.copy(w2[:, 0, e].rearrange("p c n -> p (c n)"), stage[:, e % 2, 1]).then_inc(w_hi_done.sem, 1)
            act.wait_ge(consts.sem, consts.done(0))
            for k in sorted(steps):
                steps[k](0)

            def body(blk, last):
                hidden(blk, 0)
                for e in range(E):
                    if e < E - 1:
                        hidden(blk, e + 1)
                    if not last and e in steps:
                        steps[e](blk + 1)

            blocks(act, body)

        @block.vector
        def _(dve):
            for k in (xh_done, x_lo_done, w_done, gate_set, gl_done, acc_done):
                k.start(dve)

            held = [0]

            def hold(k, value):
                dve.wait_ge(k.sem, value)
                held[0] += 1
                nc.vector.tensor_tensor(carrier[:, held[0]:held[0] + 1], carrier[:, 0:1], carrier[:, 0:1], ALU.mult)

            def moments(n, src):
                for t in range(TB):
                    last = nc.vector.bn_stats(stats[:, t, :], src[:, t, :])
                last.then_inc(st_done.sem, 1)
                hold(st_done, st_done.done(n))
                for t in range(TB):
                    last = nc.vector.bn_aggr(mv[:, t, :], stats[:, t, :])
                last.then_inc(mv_done.sem, 1)

            def centred(n, src, dst, done):
                hold(rstd_done, rstd_done.done(n))
                for t in range(TB):
                    last = nc.vector.tensor_scalar(dst[:, t, :], src[:, t, :], mv[:, t, 0:1], rstd[:, t:t + 1],
                                                   ALU.subtract, ALU.mult)
                last.then_inc(done.sem, 1)

            def first_moments(blk):
                hold(hc_in, hc_in.done(blk))
                hold(xh_done, xh_done.freed(blk, 1))
                moments(2 * blk, hc)

            def second_moments(blk):
                centred(2 * blk, hc, z, z_done)
                hold(z_done, z_done.done(blk))
                moments(2 * blk + 1, z)

            def normalised(blk):
                hold(xt_mm, xt_mm.freed(2 * blk + 1, 2))
                centred(2 * blk + 1, z, xh, xh_done)

            def best(blk):
                hold(r_mm, r_mm.done(blk))
                nc.vector.tensor_tensor(logit[:], ps_r[:, 0:TB * E].rearrange("p (t e) -> p t e", t=TB),
                                        b_r[:].unsqueeze(1).broadcast_to([P, TB, E]), ALU.add).then_inc(logit_done.sem, 1)
                hold(logit_done, logit_done.done(blk))
                for t in range(TB):
                    last = nc.vector.max(top[:, t, :], logit[:, t, :])
                last.then_inc(top_done.sem, 1)
                hold(top_done, top_done.done(blk))
                for t in range(TB):
                    last = nc.vector.max_index(idx[:, t, :], top[:, t, :], logit[:, t, :])
                last.then_inc(idx_done.sem, 1)
                nc.vector.tensor_tensor(gap[:], top[:, :, 1], top[:, :, 0], ALU.subtract).then_inc(gap_done.sem, 1)
                hold(idx_done, idx_done.done(blk))
                nc.vector.tensor_copy(idxf[:], idx[:, :, 0:2]).then_inc(g_step.sem, 1)

            def gates(blk):
                hold(th_done, th_done.done(blk))
                nc.vector.tensor_scalar(wt[:, 0], th[:], -0.5, 0.5, ALU.mult, ALU.add)
                nc.vector.tensor_scalar(wt[:, 1], th[:], 0.5, 0.5, ALU.mult, ALU.add).then_inc(g_step.sem, 1)
                hold(g_step, g_step.done(4 * blk + 1))
                for k in range(2):
                    last = nc.vector.tensor_tensor(hot[:, k], iota[:].unsqueeze(1).broadcast_to([P, TB, E]),
                                                   idxf[:, :, k:k + 1].broadcast_to([P, TB, E]), ALU.is_equal)
                last.then_inc(g_step.sem, 1)
                hold(g_step, g_step.done(4 * blk + 2))
                for k in range(2):
                    last = nc.vector.tensor_tensor(hot[:, k], hot[:, k], wt[:, k].unsqueeze(2).broadcast_to([P, TB, E]), ALU.mult)
                last.then_inc(g_step.sem, 1)
                hold(g_step, g_step.done(4 * blk + 3))
                hold(gate_set, gate_set.freed(blk, 1))
                nc.vector.tensor_tensor(gate_next[:], hot[:, 0], hot[:, 1], ALU.add).then_inc(gate_done.sem, 1)

            def low_part(blk):
                dve.wait_ge(x_hi_done.sem, x_hi_done.done(blk))
                nc.vector.tensor_tensor(x_lo[:], xf[:], x_hi[:], ALU.subtract).then_inc(x_lo_done.sem, 1)

            steps = {0: first_moments, 1: second_moments, 2: normalised, 5: best, 6: gates}

            def low(blk, e):
                for t in range(HT):
                    u = blk * (4 * E) + (4 * e + t)
                    dve.wait_ge(gh_done.sem, gh_done.done(u))
                    nc.vector.tensor_tensor(g_lo[:, e % 2, t, :], g32[:, t, :], g_hi[:, e % 2, t, :],
                                            ALU.subtract).then_inc(gl_done.sem, 1)

            def summed(blk, e):
                for t in range(TB):
                    u = blk * YU + (4 * (e + 1) + t)
                    dve.wait_ge(y_mm.sem, y_mm.done(u))
                    if e < 0:
                        nc.vector.tensor_tensor(y[:, t, :], ps_y[t % 2][:, 0:C], hc[:, t, :], ALU.add).then_inc(acc_done.sem, 1)
                        continue
                    if e == E - 1 and t == 0:
                        dve.wait_ge(stored.sem, stored.freed(blk, 1))
                    nc.vector.scalar_tensor_tensor((y, o)[e == E - 1][:, t, :], ps_y[t % 2][:, 0:C], gate[:, t, e:e + 1], y[:, t, :],
                                                   ALU.mult, ALU.add).then_inc(acc_done.sem, 1)

            dve.wait_ge(consts.sem, consts.done(0))
            dve.wait_ge(pool_set.sem, 3)
            for e in range(E):
                if e == 1:
                    for k in (0, 1, 2):
                        steps[k](0)
                dve.wait_ge(w_hi_done.sem, e + 1)
                nc.vector.tensor_tensor(w1[:, 1, e].rearrange("p c n -> p (c n)"), stage[:, e % 2, 0],
                                        w1[:, 0, e].rearrange("p c n -> p (c n)"), ALU.subtract)
                nc.vector.tensor_tensor(w2[:, 1, e].rearrange("p c n -> p (c n)"), stage[:, e % 2, 1],
                                        w2[:, 0, e].rearrange("p c n -> p (c n)"), ALU.subtract).then_inc(w_done.sem, 1)
            best(0)
            gates(0)
            low_part(0)

            def body(blk, last):
                hold(gate_done, gate_done.done(blk))
                hold(acc_done, acc_done.done(blk * YU - 1))
                nc.vector.tensor_copy(gate[:], gate_next[:]).then_inc(gate_set.sem, 1)
                hold(gate_set, gate_set.done(blk))
                summed(blk, -1)
                low(blk, 0)
                for e in range(E):
                    if e < E - 1:
                        low(blk, e + 1)
                    elif not last:
                        low_part(blk + 1)
                    summed(blk, e)
                    if not last and e in steps:
                        steps[e](blk + 1)

            blocks(dve, body)

        @block.tensor
        def _(pe):
            h_mm.start(pe)
            xt_mm.start(pe)
            y_mm.start(pe)

            def turned(blk, c):
                pe.wait_ge(xh_done.sem, xh_done.done(blk))
                if c == 0:
                    pe.wait_ge(gt_done.sem, gt_done.freed(blk, 1))
                else:
                    pe.wait_ge(xf_done.sem, xf_done.done(2 * blk))
                for t in range(TB):
                    last = pe.transpose(ps_x[:, t * P:(t + 1) * P], xh[:, t, c * P:(c + 1) * P], ident[:])
                last.then_inc(xt_mm.sem, 1)

            def routed(blk):
                pe.wait_ge(xf_done.sem, xf_done.done(2 * blk + 1))
                for t in range(TB):
                    for c in range(CK):
                        last = pe.matmul(ps_r[:, t * E:(t + 1) * E], xf[:, c, t * P:(t + 1) * P], w_r[:, c, :],
                                         start=(t == 0 and c == 0), stop=(c == CK - 1), skip_group_check=True)
                last.then_inc(r_mm.sem, 1)

            def gates_t(blk):
                pe.wait_ge(gate_done.sem, gate_done.done(blk))
                for t in range(TB):
                    last = pe.transpose(ps_x[0:E, t * P:(t + 1) * P], gate_next[:, t, :], ident[:])
                last.then_inc(gt_mm.sem, 1)

            steps = {3: lambda blk: turned(blk, 0), 4: lambda blk: turned(blk, 1), 5: routed, 7: gates_t}

            def hidden(blk, e):
                if not isinstance(blk, int) or blk == 0:
                    pe.wait_ge(w_done.sem, w_done.done(e))
                for t in range(HT):
                    u = blk * (4 * E) + (4 * e + t)
                    pe.wait_ge(gh_done.sem, gh_done.freed(u, 4))
                    n = 0
                    for c in range(CK):
                        for wp, x in ((0, x_hi), (0, x_lo), (1, x_hi)):
                            last = pe.matmul(ps_h[t][:], w1[:, wp, e, c, t * P:(t + 1) * P], x[:, c, :], start=(n == 0),
                                             stop=(n == 3 * CK - 1))
                            n += 1
                    last.then_inc(h_mm.sem, 1)

            def outputs(blk, e):
                for t in range(TB):
                    u = blk * YU + (4 * (e + 1) + t)
                    pe.wait_ge(acc_done.sem, acc_done.freed(u, 2))
                    if e < 0:
                        pe.matmul(ps_y[t % 2][:, 0:C], gate_t[:, t * P:(t + 1) * P], b2[:], start=True, stop=True
                                  ).then_inc(y_mm.sem, 1)
                        continue
                    if t == 0:
                        pe.wait_ge(gl_done.sem, gl_done.done(blk * (4 * E) + (4 * e + 3)))
                    n = 0
                    for k in range(HT):
                        for g, wp in ((g_hi, 0), (g_hi, 1), (g_lo, 0)):
                            last = pe.matmul(ps_y[t % 2][:, 0:C], g[:, e % 2, k, t * P:(t + 1) * P], w2[:, wp, e, k, :],
                                             start=(n == 0), stop=(n == 3 * HT - 1))
                            n += 1
                    last.then_inc(y_mm.sem, 1)

            pe.wait_ge(consts.sem, consts.done(0))
            for k in sorted(steps):
                steps[k](0)

            def body(blk, last):
                pe.wait_ge(x_lo_done.sem, x_lo_done.done(blk))
                hidden(blk, 0)
                pe.wait_ge(gt_done.sem, gt_done.done(blk))
                outputs(blk, -1)
                for e in range(E):
                    if e < E - 1:
                        hidden(blk, e + 1)
                    outputs(blk, e)
                    if not last and e in steps:
                        steps[e](blk + 1)

            blocks(pe, body)


def program(nc, a, out):
    with ExitStack() as ctx:
        m = Maker(nc, ctx, "all")
        hs = m.sb("h", [P, TILES, C])

        def dram(name, shape, dt=F32):
            return nc.dram_tensor(name, shape, dt, kind=KINDS.get(name, "Internal")).ap()

        v_d = dram("v_d", [B, P, NT, C])
        qt_d = dram("qt_d", [B, P, 4, N])
        top_d = dram("top_d", [B, HD, 2 * C])
        gram_d = dram("gram_d", [B * 4 * P, HD])
        rt_d = dram("rt_d", [P * HD, HD])
        parts_d = dram("parts_d", [B, 2, 2 * HD, 2, 2, 2, 2, N], F16)
        dr = {
            "v": v_d, "qt": qt_d, "top": top_d,
            "gram": gram_d.rearrange("(b g p) j -> b p g j", b=B, g=4),
            "gram_m": gram_d.rearrange("(m i) j -> m i j", m=P),
            "top_m": top_d.rearrange("b n (m d) -> b m n d", d=HD),
            "rt_m": rt_d.rearrange("(m i) j -> m i j", m=P),
            "rt": rt_d.rearrange("(b g h k) i -> b h k g i", b=B, g=4, h=4),
            "parts_st": parts_d,
            "parts": parts_d[:, 0:1].rearrange("b y x k p r g n -> b y x (k p r g) n"),
            "keys": parts_d[:, 1].rearrange("b x k p r g n -> b x k p (r g) n"),
        }
        embed_and_project(nc, a, dr, hs)
        orthonormal_factors(nc, a, dr)
        split_operands(nc, a, dr)
        attention(nc, a, dr, hs)
        experts(nc, a, hs, out.rearrange("b (t p) c -> (b t) p c", p=P))


KINDS = {}


def kernel(**inputs):
    import numpy as np
    import concourse.bacc as bacc
    from concourse.bass_utils import run_bass_kernel_spmd as run

    def rows(v, n=P):
        return np.broadcast_to(v.reshape(1, -1), (n, v.size))

    i = {k.replace("L0_", ""): np.asarray(v) for k, v in inputs.items()}
    x = i["x"].reshape(B, 32, 7, 32, 7).transpose(0, 2, 4, 1, 3).reshape(B, PD, N)
    laid = {
        "pat": x,
        "tok_w": i["tok_W"].T,
        "pos": i["tok_pos"].reshape(NT, P, C).transpose(1, 0, 2),
        "tok_b": rows(i["tok_b"]),
        "w_qkv": i["attn_w_qkv"].T.reshape(CK, P, 3 * C).transpose(1, 0, 2),
        "b_qkv": rows(i["attn_b_qkv"]),
        "ident": np.eye(P, dtype=np.float32),
    }
    heads = [g * 4 + pr * 2 + hp for pr in range(2) for g in range(2) for hp in range(2)]
    kinds = lambda v: np.repeat(v.reshape(3, H)[:, heads].T, GS, axis=0)
    laid |= {
        "w_proj": i["attn_w_proj"].T.reshape(CK, P, C).transpose(1, 0, 2),
        "b_proj": rows(i["attn_b_proj"]).reshape(P, 1, C),
        "mix_w": np.repeat(i["attn_conv_w"].reshape(H, 3, H)[:, :, heads].transpose(2, 1, 0), GS, axis=0),
        "bn": np.stack([kinds(i["attn_bn_" + k]) for k in ("gamma", "beta", "mean", "var")]
                       + [rows(np.stack([i["attn_scale"], i["attn_riem_scale"], i["attn_grassman_scale"]]))], axis=1),
        "mask": np.tile(np.eye(GS, dtype=np.float32), (H, 1)),
        "conv_b": np.repeat(i["attn_conv_b"], GS).reshape(P, 1),
    }
    laid |= {
        "norm": np.stack([i["ffn_gamma"].reshape(CK, P).T, i["ffn_beta"].reshape(CK, P).T], axis=1),
        "w_r": i["ffn_Wr"].reshape(CK, P, E).transpose(1, 0, 2),
        "b_r": rows(i["ffn_br"]),
        "b1": i["ffn_b1"].reshape(E, F // P, P).transpose(2, 0, 1),
        "b2": i["ffn_b2"],
        "iota": rows(np.arange(E, dtype=np.float32)),
        "w1": i["ffn_W1"].reshape(E, CK, P, F).transpose(2, 0, 1, 3).reshape(P, E, CK * F),
        "w2": i["ffn_W2"].reshape(E, F // P, P, C).transpose(2, 0, 1, 3).reshape(P, E, F // P * C),
    }
    nc = bacc.Bacc("TRN2", target_bir_lowering=False, num_devices=1)
    arrays, aps = {}, {}
    for name, v in laid.items():
        arrays[f"in_{name}"] = np.ascontiguousarray(v)
        aps[name] = nc.dram_tensor(f"in_{name}", v.shape, mybir.dt.from_np(v.dtype), kind="ExternalInput").ap()
    out = nc.dram_tensor("out_0", (B, N, C), F32, kind="ExternalOutput").ap()
    program(nc, aps, out)
    r = run(nc, [arrays], core_ids=[0])
    return r.results[0]["out_0"]
```

```python
from contextlib import ExitStack

import concourse.bass as bass
from concourse import mybir

F32 = mybir.dt.float32
F16 = mybir.dt.float16
ALU = mybir.AluOpType
ACT = mybir.ActivationFunctionType
AX_X = mybir.AxisListType.X
ds = bass.ds

P = 128
B = 8
N = 1024
C = 256
H = 8
HD = C // H
NT = N // P
TILES = B * NT
CK = C // P
PD = 49
E = 8
F = 512
EPS = 1e-5
WX = 64.0
GR = 32.0
MX = 16.0
DX = 1 / 8
GS = 16
NG = P // GS


class Count:

    def __init__(self, sem, per=1, credit=0):
        self.sem, self.per, self.credit = sem, per, credit

    def start(self, eng):
        eng.sem_inc(self.sem, self.per * self.credit)

    def done(self, t):
        return (t + (1 + self.credit)) * self.per

    def freed(self, t, depth):
        assert depth <= self.credit
        return (t + (1 + self.credit - depth)) * self.per


class Maker:

    def __init__(self, nc, ctx, prefix):
        self.nc, self.ctx, self.prefix = nc, ctx, prefix

    def sb(self, name, shape, dt=F32):
        return self.ctx.enter_context(self.nc.sbuf_tensor(f"{self.prefix}_{name}", shape, dt))

    def ps(self, name, shape, dt=F32):
        return self.ctx.enter_context(self.nc.psum_tensor(f"{self.prefix}_{name}", shape, dt))

    def count(self, name, per=1, credit=0):
        return Count(self.ctx.enter_context(self.nc.semaphore(f"{self.prefix}_{name}")), per, credit)


def embed_and_project(nc, a, dr, hs):
    with ExitStack() as ctx:
        m = Maker(nc, ctx, "p1")
        tok_w = m.sb("tok_w", [PD, C])
        pos_b = m.sb("pos_b", [P, NT, C])
        tok_b = m.sb("tok_b", [P, C])
        w_qkv = m.sb("w_qkv", [P, CK, 3 * C])
        b_qkv = m.sb("b_qkv", [P, 3 * C])
        ident = m.sb("ident", [P, P])
        pat = m.sb("pat", [PD, N])
        hc = m.sb("hc", [P, NT, C])
        stats = m.sb("stats", [P, 4, 6])
        mv = m.sb("mv", [P, 4, 2])
        veps = m.sb("veps", [P, 4])
        rstd = m.sb("rstd", [P, 4])
        mhalf = m.sb("mhalf", [P, 1])
        eps = m.sb("eps", [P, 1])
        z = m.sb("z", [P, 2, C])
        w_hi = m.sb("w_hi", [P, CK, 3 * C], F16)
        w_lo = m.sb("w_lo", [P, CK, 3 * C], F16)
        z_hi = m.sb("z_hi", [P, 2, CK, P], F16)
        z_lo = m.sb("z_lo", [P, 2, CK, P], F16)
        qk = m.sb("qk", [P, 2, 2 * C])
        vs = m.sb("vs", [P, 4, C])
        qt_hi = m.sb("qt_hi", [P, 2, 4, N // 2], F16)
        qt_lo = m.sb("qt_lo", [P, 2, 4, N // 2], F16)
        gram = m.sb("gram", [P, 4, HD])
        top = m.sb("top", [HD, 2 * C])

        ps_tok = m.ps("ps_tok", [P, 2, 512])
        ps_zt = m.ps("ps_zt", [P, CK, 256])
        ps_qk = m.ps("ps_qk", [P, 512])
        ps_v = m.ps("ps_v", [P, 512])
        ps_qt = m.ps("ps_qt", [P, 4, P])
        ps_gram = m.ps("ps_gram", [P, 512])

        weights = m.count("weights", 16 * 6)
        pat_in = [m.count(f"pat_in{k}", 16) for k in range(2)]
        posb_ready = m.count("posb_ready")
        half_ready = m.count("half_ready")
        tok_mm = m.count("tok_mm")
        h_done = m.count("h_done", credit=2)
        st_done = m.count("st_done")
        mv_done = m.count("mv_done")
        ve_done = m.count("ve_done")
        rstd_done = m.count("rstd_done", credit=0)
        z_done = m.count("z_done")
        zt_mm = m.count("zt_mm", credit=2)
        wh_done = m.count("wh_done")
        wl_done = m.count("wl_done")
        zh_done = m.count("zh_done")
        zl_done = m.count("zl_done", credit=1)
        qkv_mm = m.count("qkv_mm", credit=2)
        qk_done = m.count("qk_done", credit=1)
        v_done = m.count("v_done", credit=1)
        qt_mm = m.count("qt_mm")
        gram_mm = m.count("gram_mm", credit=2)
        qth_done = m.count("qth_done")
        qtl_done = m.count("qtl_done", credit=1)
        gramc_done = m.count("gramc_done", credit=1)
        v_store = [m.count(f"v_store{k}", 16, credit=1) for k in range(4)]
        qt_store = [m.count(f"qt_store{k}", 16 * 4, credit=1) for k in range(2)]
        top_done = m.count("top_done")
        top_store = m.count("top_store", 16, credit=1)
        h_store = [m.count(f"h_store{k}", 16, credit=1) for k in range(NT)]
        gr_store = m.count("gr_store", 16, credit=1)

        block = ctx.enter_context(nc.Block())

        def images(eng, body):
            body(0, True, False)
            with eng.Fori(1, B - 1) as b:
                body(b, False, False)
            body(B - 1, False, True)

        def at(b, t):
            return b + t // NT, t % NT, b * NT + t

        def load_patches(eng, b, half):
            c = slice(half * N // 2, (half + 1) * N // 2)
            eng.dma_start(pat[:, c], a["pat"][b if isinstance(b, int) else ds(b, 1), :, c]).then_inc(pat_in[half].sem, 16)

        @block.sync
        def _(sp):
            load_patches(sp, 0, 0)
            load_patches(sp, 0, 1)
            sp.dma_start(tok_w[:], a["tok_w"]).then_inc(weights.sem, 16)
            sp.dma_start(pos_b[:], a["pos"]).then_inc(weights.sem, 16)
            sp.dma_start(tok_b[:], a["tok_b"]).then_inc(weights.sem, 16)
            sp.dma_start(w_qkv[:], a["w_qkv"]).then_inc(weights.sem, 16)
            sp.dma_start(b_qkv[:], a["b_qkv"]).then_inc(weights.sem, 16)
            sp.dma_start(ident[:], a["ident"]).then_inc(weights.sem, 16)
            for stores in (*v_store, *qt_store, *h_store, top_store, gr_store):
                stores.start(sp)
            with sp.Fori(0, B) as b:
                for t in range(NT):
                    T = b * NT + t
                    sp.wait_ge(h_done.sem, h_done.done(T))
                    sp.dma_start(hs[:, ds(T, 1), :], hc[:, t, :]).then_inc(h_store[t].sem, 16)
                    sp.wait_ge(v_done.sem, v_done.done(T))
                    sp.dma_start(dr["v"][ds(b, 1), :, t, :], vs[:, t % 4, :]).then_inc(v_store[t % 4].sem, 16)
                    if t == 0:
                        sp.wait_ge(top_done.sem, top_done.done(b))
                        sp.dma_start(dr["top"][ds(b, 1), :, :], top[:]).then_inc(top_store.sem, 16)
                    if t % 4 == 3:
                        half = t // 4
                        sp.wait_ge(qtl_done.sem, qtl_done.done(T))
                        for part, tile in ((0, qt_hi), (1, qt_lo)):
                            for pr in range(2):
                                sp.dma_start(dr["parts_st"][ds(b, 1), :, 0, part, pr, :, half * 512:(half + 1) * 512],
                                             tile[pr * 64:(pr + 1) * 64, half]).then_inc(qt_store[half].sem, 16)
                sp.wait_ge(gramc_done.sem, gramc_done.done(b))
                sp.dma_start(dr["gram"][ds(b, 1)], gram[:]).then_inc(gr_store.sem, 16)
            for stores in v_store:
                sp.wait_ge(stores.sem, stores.done(TILES // 4 - 1))
            for stores in qt_store:
                sp.wait_ge(stores.sem, stores.done(B - 1))
            for stores in h_store:
                sp.wait_ge(stores.sem, stores.done(B - 1))
            sp.wait_ge(top_store.sem, top_store.done(B - 1))
            sp.wait_ge(gr_store.sem, gr_store.done(B - 1))

        @block.gpsimd
        def _(pool):
            nc.gpsimd.memset(mhalf[:], -0.5).then_inc(half_ready.sem, 1)
            nc.gpsimd.memset(eps[:], EPS).then_inc(half_ready.sem, 1)
            pool.wait_ge(half_ready.sem, 2)
            with pool.Fori(0, TILES // 4) as quad:
                for t in range(4):
                    T = quad * 4 + t
                    pool.wait_ge(mv_done.sem, mv_done.done(T))
                    nc.gpsimd.tensor_tensor(veps[:, t:t + 1], mv[:, t, 1:2], eps[:], ALU.add).then_inc(ve_done.sem, 1)
                    pool.wait_ge(ve_done.sem, ve_done.done(T))
                    nc.gpsimd.tensor_tensor(rstd[:, t:t + 1], veps[:, t:t + 1], mhalf[:], ALU.pow).then_inc(rstd_done.sem, 1)

        @block.scalar
        def _(act):
            gramc_done.start(act)

            def z_t(b, t, T):
                act.wait_ge(zt_mm.sem, zt_mm.done(T))
                act.wait_ge(qkv_mm.sem, qkv_mm.freed(T, 2))
                nc.scalar.copy(z_hi[:, t % 2], ps_zt[:, :, 0:P]).then_inc(zh_done.sem, 1)

            def qk_t(b, t, T):
                act.wait_ge(qt_mm.sem, qt_mm.done(T))
                if t % 4 == 0:
                    act.wait_ge(qt_store[t // 4].sem, qt_store[t // 4].freed(b, 1))
                nc.scalar.copy(qt_hi[:, t // 4, :, t % 4 * P:(t % 4 + 1) * P], ps_qt[:]).then_inc(qth_done.sem, 1)
                if t == NT - 1:
                    act.wait_ge(gram_mm.sem, gram_mm.done(T))
                    act.wait_ge(gr_store.sem, gr_store.freed(b, 1))
                    nc.scalar.copy(gram[:], ps_gram[:, 0:4 * HD].rearrange("p (g j) -> p g j", g=4)).then_inc(gramc_done.sem, 1)

            def body(b, first, last):
                for t in range(NT):
                    if t in (0, 4) and not last:
                        act.wait_ge(tok_mm.sem, tok_mm.done(b * NT + t + 3))
                        load_patches(act, b + 1, t // 4)
                    if t < NT - 1 or not last:
                        z_t(*at(b, t + 1))
                    if t or not first:
                        qk_t(*at(b, t - 1))
                    if t == 0:
                        act.wait_ge(qk_done.sem, qk_done.done(b * NT))
                        act.wait_ge(top_store.sem, top_store.freed(b, 1))
                        nc.scalar.copy(top[:], qk[0:HD, 0, :]).then_inc(top_done.sem, 1)

            z_t(0, 0, 0)
            images(act, body)
            qk_t(*at(B, -1))

        @block.vector
        def _(dve):
            h_done.start(dve)
            qk_done.start(dve)
            v_done.start(dve)
            zl_done.start(dve)
            qtl_done.start(dve)
            dve.wait_ge(weights.sem, weights.done(0))
            for t in range(NT):
                last = nc.vector.tensor_tensor(pos_b[:, t], pos_b[:, t], tok_b[:], ALU.add)
            last.then_inc(posb_ready.sem, 1)
            dve.wait_ge(posb_ready.sem, 1)

            def weight_parts():
                nc.vector.tensor_scalar(w_hi[:], w_qkv[:], WX, None, ALU.mult).then_inc(wh_done.sem, 1)
                dve.wait_ge(wh_done.sem, 1)
                nc.vector.scalar_tensor_tensor(w_lo[:], w_qkv[:], WX, w_hi[:], ALU.mult, ALU.subtract).then_inc(wl_done.sem, 1)

            def z_low(b, t, T):
                dve.wait_ge(zh_done.sem, zh_done.done(T))
                nc.vector.tensor_tensor(z_lo[:, t % 2], ps_zt[:, :, 0:P], z_hi[:, t % 2], ALU.subtract).then_inc(zl_done.sem, 1)

            def head(b, t, T):
                k = t % 4
                dve.wait_ge(tok_mm.sem, tok_mm.done(T))
                dve.wait_ge(h_store[t].sem, h_store[t].freed(b, 1))
                nc.vector.tensor_tensor(hc[:, t, :], ps_tok[:, t % 2, 0:C], pos_b[:, t, :], ALU.add).then_inc(h_done.sem, 1)
                dve.wait_ge(h_done.sem, h_done.done(T))
                nc.vector.bn_stats(stats[:, k, :], hc[:, t, :]).then_inc(st_done.sem, 1)
                dve.wait_ge(posb_ready.sem, 1)
                dve.wait_ge(st_done.sem, st_done.done(T))
                nc.vector.bn_aggr(mv[:, k, :], stats[:, k, :]).then_inc(mv_done.sem, 1)

            def normed(b, t, T):
                k = t % 4
                dve.wait_ge(rstd_done.sem, rstd_done.done(T))
                dve.wait_ge(zt_mm.sem, zt_mm.freed(T, 2))
                nc.vector.tensor_scalar(z[:, t % 2, :], hc[:, t, :], mv[:, k, 0:1], rstd[:, k:k + 1], ALU.subtract, ALU.mult
                                        ).then_inc(z_done.sem, 1)

            def tail(b, t, T):
                dve.wait_ge(qkv_mm.sem, qkv_mm.done(T))
                dve.wait_ge(gram_mm.sem, gram_mm.freed(T, 2))
                if t == 2:
                    dve.wait_ge(top_done.sem, top_done.done(b))
                nc.vector.scalar_tensor_tensor(qk[:, t % 2, :], ps_qk[:], 1 / WX, b_qkv[:, 0:2 * C], ALU.mult, ALU.add).then_inc(qk_done.sem, 1)
                slot = v_store[t % 4]
                dve.wait_ge(slot.sem, slot.freed(b * (NT // 4) + t // 4, 1))
                nc.vector.scalar_tensor_tensor(vs[:, t % 4, :], ps_v[:, 0:C], 1 / WX, b_qkv[:, 2 * C:3 * C],
                                               ALU.mult, ALU.add).then_inc(v_done.sem, 1)

            def low_part(b, t, T):
                dve.wait_ge(qth_done.sem, qth_done.done(T))
                c = slice(t % 4 * P, (t % 4 + 1) * P)
                nc.vector.tensor_tensor(qt_lo[:, t // 4, :, c], ps_qt[:], qt_hi[:, t // 4, :, c], ALU.subtract
                                        ).then_inc(qtl_done.sem, 1)

            def body(b, first, last):
                for t in range(NT):
                    tail(*at(b, t))
                    if t < NT - 1 or not last:
                        z_low(*at(b, t + 1))
                    if t < NT - 2 or not last:
                        normed(*at(b, t + 2))
                    if t < NT - 3 or not last:
                        head(*at(b, t + 3))
                    if t or not first:
                        low_part(*at(b, t - 1))

            for t in range(3):
                head(0, t, t)
            for t in range(2):
                normed(0, t, t)
            weight_parts()
            z_low(0, 0, 0)
            images(dve, body)
            low_part(*at(B, -1))

        @block.tensor
        def _(pe):
            zt_mm.start(pe)
            qkv_mm.start(pe)
            gram_mm.start(pe)
            pe.wait_ge(weights.sem, weights.done(0))

            def tokens(b, t, T):
                if t % 4 == 0:
                    pe.wait_ge(pat_in[t // 4].sem, pat_in[t // 4].done(b))
                pe.wait_ge(h_done.sem, h_done.freed(T, 2))
                pe.matmul(ps_tok[:, t % 2, 0:C], pat[:, t * P:(t + 1) * P], tok_w[:], start=True,
                          stop=True).then_inc(tok_mm.sem, 1)

            def z_t(b, t, T):
                pe.wait_ge(z_done.sem, z_done.done(T))
                pe.wait_ge(zl_done.sem, zl_done.freed(T, 1))
                for c in range(CK):
                    last = pe.transpose(ps_zt[:, c, 0:P], z[:, t % 2, c * P:(c + 1) * P], ident[:])
                last.then_inc(zt_mm.sem, 1)

            def qkv(b, t, T):
                pe.wait_ge(zl_done.sem, zl_done.done(T))
                pe.wait_ge(v_done.sem, v_done.freed(T, 1))
                for ps, cols in ((ps_qk[:], slice(0, 2 * C)), (ps_v[:, 0:C], slice(2 * C, 3 * C))):
                    for c in range(CK):
                        for n, (z_part, w_part) in enumerate(((z_hi, w_hi), (z_hi, w_lo), (z_lo, w_hi))):
                            last = pe.matmul(ps, z_part[:, t % 2, c, :], w_part[:, c, cols], start=(c == 0 and n == 0),
                                             stop=(c == CK - 1 and n == 2))
                last.then_inc(qkv_mm.sem, 1)

            def grams(b, t, T):
                pe.wait_ge(qk_done.sem, qk_done.done(T))
                pe.wait_ge(qtl_done.sem, qtl_done.freed(T, 1))
                for g in range(4):
                    last = pe.transpose(ps_qt[:, g % 2 * 2 + g // 2, :], qk[:, t % 2, g * P:(g + 1) * P], ident[:])
                last.then_inc(qt_mm.sem, 1)
                if t == 0:
                    pe.wait_ge(gramc_done.sem, gramc_done.freed(b, 1))
                for g in range(4):
                    for j in range(4):
                        w = qk[:, t % 2, g * P + j * HD:g * P + (j + 1) * HD]
                        last = pe.matmul(ps_gram[j * HD:(j + 1) * HD, g * HD:(g + 1) * HD], w, w,
                                         start=(t == 0 and g == 0), stop=(t == NT - 1), skip_group_check=True)
                last.then_inc(gram_mm.sem, 1)

            def body(b, first, last):
                for t in range(NT):
                    qkv(*at(b, t))
                    if t < NT - 1 or not last:
                        z_t(*at(b, t + 1))
                    if t or not first:
                        grams(*at(b, t - 1))
                    if t < NT - 4 or not last:
                        tokens(*at(b, t + 4))

            for t in range(4):
                tokens(0, t, t)
            z_t(0, 0, 0)
            pe.wait_ge(wl_done.sem, 1)
            images(pe, body)
            grams(*at(B, -1))


def orthonormal_operands(nc, a, dr):
    with ExitStack() as ctx:
        m = Maker(nc, ctx, "qr")
        LAG = 2
        g = m.sb("g", [P, HD, HD])
        top = m.sb("top", [P, HD, HD])
        li = m.sb("li", [P, HD, HD])
        lt = m.sb("lt", [P, HD, HD])
        lcol = m.sb("lcol", [P, HD, HD])
        outer_g = m.sb("outer_g", [P, HD * HD])
        outer_t = m.sb("outer_t", [P, HD * HD])
        outer_z = m.sb("outer_z", [P, HD * HD])
        piv = m.sb("piv", [P, HD])
        rpiv = m.sb("rpiv", [P, HD])
        mhalf = m.sb("mhalf", [P, HD])
        rroot = m.sb("rroot", [P, HD])
        sign = m.sb("sign", [P, HD])
        rbeta = m.sb("rbeta", [P, HD])
        den = m.sb("den", [P, HD])
        rden = m.sb("rden", [P, HD])
        w = m.sb("w", [P, HD])
        rt = m.sb("rt", [P, 2, 4, P])
        rt_hi = m.sb("rt_hi", [P, 4, P], F16)
        rt_lo = m.sb("rt_lo", [P, 4, P], F16)
        qt = m.sb("qt", [P, 2, 2, 4, N], F16)
        hi = m.sb("hi", [P, 2, 4, N], F16)
        lo = m.sb("lo", [P, 2, 4, N], F16)
        ps = [m.ps(f"ps{k}", [P, 512]) for k in range(4)]

        loaded = m.count("loaded", 16 * (1 + B))
        ready = m.count("ready")
        piv_done = m.count("piv_done")
        rpiv_done = m.count("rpiv_done")
        col_done = m.count("col_done")
        og_done = m.count("og_done")
        g_done = m.count("g_done")
        rroot_done = m.count("rroot_done")
        sign_done = m.count("sign_done")
        rbeta_done = m.count("rbeta_done")
        den_done = m.count("den_done")
        rden_done = m.count("rden_done")
        w_done = m.count("w_done")
        ot_done = m.count("ot_done")
        top_done = m.count("top_done")
        z_done = m.count("z_done")
        zo_done = m.count("zo_done")
        out_done = m.count("out_done")
        stored = m.count("stored", 16)
        qt_in = [m.count(f"qt_in{s}", 16 * 4) for s in range(2)]
        rt_in = [m.count(f"rt_in{s}", 16 * 4) for s in range(2)]
        rh_done = m.count("rh_done")
        rl_done = m.count("rl_done")
        mm = m.count("mm", credit=16)
        hi_o = m.count("hi_o")
        lo_o = m.count("lo_o", credit=4)
        stores = [m.count(f"stores{s}", 16 * 4, credit=1) for s in range(2)]
        block = ctx.enter_context(nc.Block())

        @block.sync
        def _(sp):
            for s in range(2):
                stores[s].start(sp)
            sp.dma_start(g[:], dr["gram_m"]).then_inc(loaded.sem, 16)
            for b in range(B):
                sp.dma_start(top[b * 2 * H:(b + 1) * 2 * H], dr["top_m"][b]).then_inc(loaded.sem, 16)

            def load_qt(b, s):
                for part in range(2):
                    for pr in range(2):
                        sp.dma_start(qt[pr * 64:(pr + 1) * 64, s, part], dr["parts_st"][ds(b, 1), :, 0, part, pr]
                                     ).then_inc(qt_in[s].sem, 16)

            def load_rt(b, s):
                for j in range(4):
                    sp.dma_start(rt[j * HD:(j + 1) * HD, s, :, j * HD:(j + 1) * HD], dr["rt"][ds(b, 1), j]
                                 ).then_inc(rt_in[s].sem, 16)

            for s in range(2):
                load_qt(s, s)
            sp.wait_ge(out_done.sem, 1)
            sp.dma_start(dr["rt_m"], lt[:]).then_inc(stored.sem, 16)
            sp.wait_ge(ready.sem, 4)
            sp.wait_ge(stored.sem, 16)
            for s in range(2):
                load_rt(s, s)

            def load(b, s):
                sp.wait_ge(mm.sem, mm.done(8 * b - 9))
                load_qt(b, s)
                load_rt(b, s)

            def store(b, s):
                sp.wait_ge(lo_o.sem, lo_o.done(8 * b + 7))
                for part, tile in ((0, hi), (1, lo)):
                    for pr in range(2):
                        sp.dma_start(dr["parts_st"][ds(b, 1), :, 1, part, pr], tile[pr * 64:(pr + 1) * 64, s]
                                     ).then_inc(stores[s].sem, 16)

            with sp.Fori(0, B // 2 - 1) as b2:
                for s in range(2):
                    store(b2 * 2 + s, s)
                    load(b2 * 2 + (s + 2), s)
            for s in range(2):
                store(B - 2 + s, s)
            for s in range(2):
                sp.wait_ge(stores[s].sem, stores[s].done(B // 2 - 1))

        @block.gpsimd
        def _(pool):
            nc.gpsimd.memset(li[:], 0.0).then_inc(ready.sem, 1)
            pool.wait_ge(ready.sem, 1)
            for j in range(HD):
                last = nc.gpsimd.memset(li[:, j, j:j + 1], 1.0)
            last.then_inc(ready.sem, 1)
            pool.wait_ge(ready.sem, 2)
            nc.gpsimd.memset(mhalf[:], -0.5).then_inc(ready.sem, 1)
            nc.gpsimd.memset(rt[:], 0.0).then_inc(ready.sem, 1)
            pool.wait_ge(ready.sem, 4)
            for j in range(HD):
                n = HD - 1 - j
                pool.wait_ge(piv_done.sem, j + 1)
                nc.gpsimd.tensor_tensor(rroot[:, j:j + 1], piv[:, j:j + 1], mhalf[:, j:j + 1], ALU.pow).then_inc(rroot_done.sem, 1)
                if not n:
                    break
                pool.wait_ge(col_done.sem, j + 1)
                if j:
                    pool.wait_ge(z_done.sem, j)
                o = outer_z[:, 0:n * (j + 1)].rearrange("p (i k) -> p i k", i=n)
                nc.gpsimd.tensor_tensor(o, lcol[:, j, j + 1:HD].unsqueeze(2).broadcast_to([P, n, j + 1]),
                                        li[:, j:j + 1, 0:j + 1].broadcast_to([P, n, j + 1]), ALU.mult).then_inc(zo_done.sem, 1)
                pool.wait_ge(zo_done.sem, j + 1)
                nc.gpsimd.tensor_tensor(li[:, j + 1:HD, 0:j + 1], li[:, j + 1:HD, 0:j + 1], o,
                                        ALU.subtract).then_inc(z_done.sem, 1)

        @block.vector
        def _(dve):
            lo_o.start(dve)
            dve.wait_ge(loaded.sem, loaded.done(0))
            for step in range(HD + LAG):
                j, i = step, step - LAG
                n, k = HD - 1 - j, HD - 1 - i
                if n >= 0:
                    if j:
                        dve.wait_ge(g_done.sem, j)
                    nc.vector.tensor_scalar(piv[:, j:j + 1], g[:, j, j:j + 1], 1e-30, None, ALU.max).then_inc(piv_done.sem, 1)
                if i >= 0:
                    if i:
                        dve.wait_ge(top_done.sem, i)
                    nc.vector.tensor_scalar(sign[:, i:i + 1], top[:, i, i:i + 1], 0.0, -2.0, ALU.is_ge, ALU.mult
                                            ).then_inc(sign_done.sem, 1)
                if n > 0:
                    dve.wait_ge(piv_done.sem, j + 1)
                    nc.vector.reciprocal(rpiv[:, j:j + 1], piv[:, j:j + 1]).then_inc(rpiv_done.sem, 1)
                if i >= 0:
                    dve.wait_ge(rroot_done.sem, i + 1)
                    dve.wait_ge(sign_done.sem, i + 1)
                    nc.vector.tensor_scalar(rbeta[:, i:i + 1], sign[:, i:i + 1], 1.0, rroot[:, i:i + 1], ALU.add, ALU.mult
                                            ).then_inc(rbeta_done.sem, 1)
                if n > 0:
                    dve.wait_ge(rpiv_done.sem, j + 1)
                    nc.vector.tensor_scalar(lcol[:, j, j + 1:HD], g[:, j, j + 1:HD], rpiv[:, j:j + 1], None,
                                            ALU.mult).then_inc(col_done.sem, 1)
                if i >= 0 and k > 0:
                    dve.wait_ge(rbeta_done.sem, i + 1)
                    nc.vector.scalar_tensor_tensor(den[:, i:i + 1], rbeta[:, i:i + 1], piv[:, i:i + 1], top[:, i, i:i + 1],
                                                   ALU.mult, ALU.subtract).then_inc(den_done.sem, 1)
                    nc.vector.scalar_tensor_tensor(w[:, 0:k], g[:, i, i + 1:HD], rbeta[:, i:i + 1], top[:, i, i + 1:HD],
                                                   ALU.mult, ALU.subtract).then_inc(w_done.sem, 1)
                if n > 0:
                    dve.wait_ge(col_done.sem, j + 1)
                    og = outer_g[:, 0:n * n].rearrange("p (i k) -> p i k", i=n)
                    nc.vector.tensor_tensor(og, lcol[:, j, j + 1:HD].unsqueeze(2).broadcast_to([P, n, n]),
                                            g[:, j:j + 1, j + 1:HD].broadcast_to([P, n, n]), ALU.mult).then_inc(og_done.sem, 1)
                if i >= 0 and k > 0:
                    dve.wait_ge(den_done.sem, i + 1)
                    nc.vector.reciprocal(rden[:, i:i + 1], den[:, i:i + 1]).then_inc(rden_done.sem, 1)
                if n > 0:
                    dve.wait_ge(og_done.sem, j + 1)
                    nc.vector.tensor_tensor(g[:, j + 1:HD, j + 1:HD], g[:, j + 1:HD, j + 1:HD], og, ALU.subtract
                                            ).then_inc(g_done.sem, 1)
                if i >= 0 and k > 0:
                    ot = outer_t[:, 0:k * k].rearrange("p (i k) -> p i k", i=k)
                    dve.wait_ge(rden_done.sem, i + 1)
                    dve.wait_ge(w_done.sem, i + 1)
                    nc.vector.scalar_tensor_tensor(ot, top[:, i + 1:HD, i:i + 1].broadcast_to([P, k, k]), rden[:, i:i + 1],
                                                   w[:, 0:k].unsqueeze(1).broadcast_to([P, k, k]), ALU.mult, ALU.mult
                                                   ).then_inc(ot_done.sem, 1)
                    dve.wait_ge(ot_done.sem, i + 1)
                    nc.vector.tensor_tensor(top[:, i + 1:HD, i + 1:HD], top[:, i + 1:HD, i + 1:HD], ot, ALU.subtract
                                            ).then_inc(top_done.sem, 1)
            dve.wait_ge(z_done.sem, HD - 1)
            dve.wait_ge(rbeta_done.sem, HD)
            nc.vector.tensor_tensor(lt[:].rearrange("p k i -> p i k"), li[:], rbeta[:].unsqueeze(2).broadcast_to([P, HD, HD]),
                                    ALU.mult).then_inc(out_done.sem, 1)

            with dve.Fori(0, B // 2) as b2:
                for s in range(2):
                    b = b2 * 2 + s
                    dve.wait_ge(rt_in[s].sem, rt_in[s].done(b2))
                    dve.wait_ge(mm.sem, mm.done(8 * b - 1))
                    nc.vector.tensor_scalar(rt_hi[:], rt[:, s], GR, None, ALU.mult).then_inc(rh_done.sem, 1)
                    dve.wait_ge(rh_done.sem, rh_done.done(b))
                    nc.vector.scalar_tensor_tensor(rt_lo[:], rt[:, s], GR, rt_hi[:], ALU.mult, ALU.subtract
                                                   ).then_inc(rl_done.sem, 1)
                    for x in range(4):
                        for h in range(2):
                            u = b * 8 + (2 * x + h)
                            dve.wait_ge(hi_o.sem, hi_o.done(u))
                            c = slice(h * 512, (h + 1) * 512)
                            nc.vector.tensor_tensor(lo[:, s, x, c], ps[(2 * x + h) % 4][:], hi[:, s, x, c], ALU.subtract
                                                    ).then_inc(lo_o.sem, 1)

        @block.scalar
        def _(act):
            with act.Fori(0, B // 2) as b2:
                for s in range(2):
                    b = b2 * 2 + s
                    act.wait_ge(stores[s].sem, stores[s].freed(b2, 1))
                    for x in range(4):
                        for h in range(2):
                            act.wait_ge(mm.sem, mm.done(b * 8 + (2 * x + h)))
                            nc.scalar.copy(hi[:, s, x, h * 512:(h + 1) * 512], ps[(2 * x + h) % 4][:]).then_inc(hi_o.sem, 1)

        @block.tensor
        def _(pe):
            mm.start(pe)
            with pe.Fori(0, B // 2) as b2:
                for s in range(2):
                    b = b2 * 2 + s
                    pe.wait_ge(qt_in[s].sem, qt_in[s].done(b2))
                    pe.wait_ge(rl_done.sem, rl_done.done(b))
                    for x in range(4):
                        for h in range(2):
                            pe.wait_ge(lo_o.sem, lo_o.freed(b * 8 + (2 * x + h), 4))
                            c = slice(h * 512, (h + 1) * 512)
                            g = x % 2 * 2 + x // 2
                            for n, (r, part) in enumerate(((rt_hi, 0), (rt_hi, 1), (rt_lo, 0))):
                                last = pe.matmul(ps[(2 * x + h) % 4][:], r[:, g, :], qt[:, s, part, x, c], start=(n == 0), stop=(n == 2))
                            last.then_inc(mm.sem, 1)


def attention(nc, a, dr, hs):
    with ExitStack() as ctx:
        m = Maker(nc, ctx, "p3")
        NB = B * NT
        ident = m.sb("ident", [P, P])
        w_proj = m.sb("w_proj", [P, CK, C])
        b_proj = m.sb("b_proj", [P, 1, C])
        mix_w = m.sb("mix_w", [P, 3, H])
        bn = m.sb("bn", [P, 5, 3])
        mask = m.sb("mask", [P, GS])
        conv_b = m.sb("conv_b", [P, 1])
        half = m.sb("half", [P, 3])
        eps = m.sb("eps", [P, 3])
        ones = m.sb("ones", [P, 1])
        one = m.sb("one", [P, 1], F16)
        coef = m.sb("coef", [P, 4, 3])
        cw = m.sb("cw", [P, 2, 3, H])
        mixer = m.sb("mixer", [P, 3, H, GS])
        shifter = m.sb("shifter", [P, 3, H, GS])
        const = m.sb("const", [P, 1])
        keys = m.sb("keys", [P, 2, 4, N], F16)
        v = m.sb("v", [P, NT, C])
        q_in = m.sb("q_in", [P, 16, P], F16)
        q_bd = m.sb("q_bd", [P, 16, NG, 2 * GS], F16)
        mix_h = m.sb("mix_h", [P, 2, P], F16)
        mix_l = m.sb("mix_l", [P, 2, P], F16)
        const_x = m.sb("const_x", [P, 1])
        s_h = m.sb("s_h", [P, 4, 2, 512], F16)
        s_l = m.sb("s_l", [P, 4, 2, 512], F16)
        s_dd = m.sb("s_dd", [P, 2, 512])
        s_gg = m.sb("s_gg", [P, 4, 512])
        mx = m.sb("mx", [P, 2, 2])
        mxc = m.sb("mxc", [P, 2])
        bias = m.sb("bias", [P, 2])
        p = m.sb("p", [P, 2, N])
        pt = m.sb("pt", [P, NT, H, P])
        sums = m.sb("sums", [P, 2, 2])
        total = m.sb("total", [P, 2])
        rden = m.sb("rden", [P, 2])
        ot = m.sb("ot", [P, CK, P])
        delta = m.sb("delta", [P, 1, C])

        ps_d = m.ps("ps_d", [P, 2, 512])
        ps_g = m.ps("ps_g", [P, 512])
        ps_a = m.ps("ps_a", [P, 2, 512])
        ps_t = m.ps("ps_t", [P, NT, P])
        ps_m = m.ps("ps_m", [P, 1, 512])

        consts = m.count("consts", 16 * 7)
        set_up = m.count("set_up")
        pool_set = m.count("pool_set")
        fold = m.ctx.enter_context(nc.semaphore("p3_fold"))
        powed = m.count("powed")
        k_in = {(kind, mh): m.count(f"k_in_{kind}{mh}", 64) for kind in range(2) for mh in range(2)}
        v_in = m.count("v_in", 16)
        qn_in = m.count("qn_in", 64)
        qb_done = m.count("qb_done", credit=2)
        d_mm = m.count("d_mm", credit=2 * NG)
        g_mm = m.count("g_mm", credit=2 * NG)
        mix_mm = m.count("mix_mm", credit=4)
        tr_mm = m.count("tr_mm", credit=2)
        pv_mm = m.count("pv_mm", credit=2)
        pj_mm = m.count("pj_mm")
        dh_done = m.count("dh_done", 3)
        dl_done = m.count("dl_done", credit=2)
        gg_done = m.count("gg_done", credit=1)
        dd_done = m.count("dd_done", credit=2)
        mx_done = m.count("mx_done")
        mxc_done = m.count("mxc_done")
        bias_done = m.count("bias_done")
        p_done = m.count("p_done", credit=2)
        total_done = m.count("total_done")
        pt_done = m.count("pt_done", credit=1)
        rden_done = m.count("rden_done")
        pn_done = m.count("pn_done")
        otc_done = m.count("otc_done")
        delta_done = m.count("delta_done", credit=1)
        h_done = m.count("h_done")

        block = ctx.enter_context(nc.Block())

        def blocks(eng, body):
            body(0, True, False)
            with eng.Fori(1, NB - 1) as blk:
                body(blk, False, False)
            body(NB - 1, False, True)

        @block.sync
        def _(sp):
            for tile, name in ((ident, "ident"), (w_proj, "w_proj"), (b_proj, "b_proj"), (mix_w, "mix_w"), (bn, "bn"),
                               (mask, "mask"), (conv_b, "conv_b")):
                sp.dma_start(tile[:], a[name]).then_inc(consts.sem, 16)

            def queries(b, nb, blk):
                col = sp.snap(nb * P) if not isinstance(nb, int) else nb * P
                if blk is not None:
                    sp.wait_ge(qb_done.sem, qb_done.done(2 * blk - 1))
                for hp in range(2):
                    for dup in range(2):
                        r = hp * 64 + dup * HD
                        sp.dma_start(q_in[r:r + HD], dr["queries"][ds(b, 1), hp * HD:(hp + 1) * HD, :, ds(col, P)]
                                     ).then_inc(qn_in.sem, 16)

            with sp.Fori(0, B) as b:
                sp.wait_ge(qb_done.sem, qb_done.done(2 * NT * b - 1))
                queries(b, 0, None)
                for mh in range(2):
                    for kind, sem in ((0, d_mm), (1, g_mm)):
                        sp.wait_ge(sem.sem, sem.done(b * (2 * NG * NT) - 2 + mh))
                        for hp in range(2):
                            for part in range(2):
                                r = hp * 64 + part * HD
                                sp.dma_start(keys[r:r + HD, kind, :, mh * 512:(mh + 1) * 512],
                                             dr["keys"][ds(b, 1), hp * HD:(hp + 1) * HD, kind, part, :, mh * 512:(mh + 1) * 512]
                                             ).then_inc(k_in[kind, mh].sem, 16)
                sp.wait_ge(pv_mm.sem, pv_mm.done(b * NT - 1))
                sp.dma_start(v[:], dr["v"][ds(b, 1)]).then_inc(v_in.sem, 16)
                with sp.Fori(1, NT) as nb:
                    queries(b, nb, b * NT + nb)

        @block.gpsimd
        def _(pool):
            qb_done.start(pool)
            nc.gpsimd.memset(q_bd[:], 0.0).then_inc(pool_set.sem, 1)
            nc.gpsimd.memset(half[:], -0.5).then_inc(pool_set.sem, 1)
            nc.gpsimd.memset(eps[:], EPS).then_inc(pool_set.sem, 1)
            nc.gpsimd.memset(ones[:], 1.0).then_inc(pool_set.sem, 1)
            nc.gpsimd.memset(one[:], 1.0).then_inc(pool_set.sem, 1)
            pool.wait_ge(pool_set.sem, 5)
            pool.wait_ge(consts.sem, consts.done(0))
            nc.gpsimd.tensor_tensor(coef[:, 0], bn[:, 3], eps[:], ALU.add).then_inc(powed.sem, 1)
            pool.wait_ge(powed.sem, 1)
            nc.gpsimd.tensor_tensor(coef[:, 1], coef[:, 0], half[:], ALU.pow).then_inc(powed.sem, 1)
            pool.wait_ge(powed.sem, 2)
            with pool.Fori(0, NB) as blk:
                for hf in range(2):
                    pool.wait_ge(qn_in.sem, qn_in.done(blk))
                    pool.wait_ge(g_mm.sem, g_mm.freed(blk * (2 * NG) + (8 * hf + 7), 2 * NG))
                    for hp in range(2):
                        r = slice(hp * 64, hp * 64 + 64)
                        src = q_in[r, :, hf * 64:hf * 64 + 64].rearrange("p x (g n) -> p x g n", g=4)
                        last = nc.gpsimd.tensor_tensor(q_bd[r, :, 4 * hf:4 * hf + 4, hp * GS:(hp + 1) * GS], src, one[r].unsqueeze(2).unsqueeze(3).broadcast_to([64, 16, 4, GS]), ALU.mult)
                    last.then_inc(qb_done.sem, 1)

        @block.scalar
        def _(act):
            gg_done.start(act)
            p_done.start(act)

            def high_part(u, k):
                act.wait_ge(d_mm.sem, d_mm.done(u))
                act.wait_ge(mix_mm.sem, mix_mm.freed(u, 4))
                nc.scalar.copy(s_h[:, k, 0, :], ps_d[:, k % 2, :]).then_inc(dh_done.sem, 1)

            def squares(u, k):
                act.wait_ge(dd_done.sem, dd_done.freed(u, 2))
                nc.scalar.activation(s_dd[:, k % 2, :], ps_d[:, k % 2, :], ACT.Square, scale=DX).then_inc(dh_done.sem, 1)
                nc.scalar.activation(s_h[:, k, 1, :], ps_d[:, k % 2, :], ACT.Square, scale=DX).then_inc(dh_done.sem, 1)

            def grass(u, k):
                act.wait_ge(g_mm.sem, g_mm.done(u))
                act.wait_ge(mix_mm.sem, mix_mm.freed(u, 4))
                nc.scalar.activation(s_gg[:, k, :], ps_g[:], ACT.Square).then_inc(gg_done.sem, 1)

            def weights(s, g, mh):
                if mh == 0:
                    act.wait_ge(bias_done.sem, bias_done.done(s))
                    act.wait_ge(tr_mm.sem, tr_mm.freed(s, 2))
                nc.scalar.activation(p[:, g % 2, mh * 512:(mh + 1) * 512], ps_a[:, mh, :], ACT.Exp,
                                     scale=1 / MX, bias=bias[:, g % 2:g % 2 + 1], accum_out=sums[:, g % 2, mh:mh + 1]
                                     ).then_inc(p_done.sem, 1)

            def body(blk, first, last):
                for g in range(NG):
                    s = blk * NG + g
                    more = not (last and g == NG - 1)
                    k = 2 * ((g + 1) % 2)
                    if more:
                        high_part(2 * s + 2, k)
                        squares(2 * s + 2, k)
                        grass(2 * s + 2, k)
                        high_part(2 * s + 3, k + 1)
                    weights(s, g, 0)
                    weights(s, g, 1)
                    if more:
                        squares(2 * s + 3, k + 1)
                        grass(2 * s + 3, k + 1)
                    if g == 2 and not first:
                        outputs_t(blk - 1)

            def outputs_t(blk):
                act.wait_ge(pv_mm.sem, pv_mm.done(blk))
                nc.scalar.copy(ot[:].rearrange("p c n -> p (c n)"), ps_m[:, 0, 0:CK * P]).then_inc(otc_done.sem, 1)

            for u in range(2):
                high_part(u, u)
                squares(u, u)
                grass(u, u)
            blocks(act, body)
            outputs_t(NB - 1)

        @block.vector
        def _(dve):
            pt_done.start(dve)
            delta_done.start(dve)
            dl_done.start(dve)
            dd_done.start(dve)
            steps = [0]

            def link(ins):
                steps[0] += 1
                ins.then_inc(fold, 1)
                dve.wait_ge(fold, steps[0])

            dve.wait_ge(consts.sem, consts.done(0))
            dve.wait_ge(powed.sem, 2)
            link(nc.vector.tensor_tensor(coef[:, 0], bn[:, 0], coef[:, 1], ALU.mult))
            link(nc.vector.tensor_tensor(coef[:, 2], coef[:, 0], bn[:, 4], ALU.mult))
            for kind, by in enumerate((MX, MX / DX ** 2, MX / GR ** 4)):
                link(nc.vector.tensor_scalar(coef[:, 2, kind:kind + 1], coef[:, 2, kind:kind + 1], by, None, ALU.mult))
            link(nc.vector.tensor_tensor(coef[:, 3], bn[:, 2], coef[:, 0], ALU.mult))
            link(nc.vector.tensor_tensor(coef[:, 3], bn[:, 1], coef[:, 3], ALU.subtract))
            for n, w in ((2, 0), (3, 1)):
                link(nc.vector.tensor_tensor(cw[:, w], mix_w[:], coef[:, n].unsqueeze(2).broadcast_to([P, 3, H]), ALU.mult))
                for kind in range(3):
                    link(nc.vector.tensor_tensor((mixer, shifter)[w][:, kind], cw[:, w, kind].unsqueeze(2).broadcast_to([P, H, GS]),
                                                 mask[:].unsqueeze(1).broadcast_to([P, H, GS]), ALU.mult))
            link(nc.vector.tensor_copy(mix_h[:], mixer[:, 0:2].rearrange("p k o n -> p k (o n)")))
            nc.vector.tensor_tensor(mix_l[:], mixer[:, 0:2].rearrange("p k o n -> p k (o n)"), mix_h[:], ALU.subtract
                                    ).then_inc(set_up.sem, 1)
            dve.wait_ge(pv_mm.sem, 2)
            link(nc.vector.tensor_tensor(const[:], ps_m[:, 0, 0:1], conv_b[:], ALU.add))
            link(nc.vector.tensor_scalar(const_x[:], const[:], MX, None, ALU.mult))

            def low_dots(u, k):
                dve.wait_ge(dh_done.sem, dh_done.done(u))
                nc.vector.tensor_tensor(s_l[:, k, 0, :], ps_d[:, k % 2, :], s_h[:, k, 0, :], ALU.subtract).then_inc(dl_done.sem, 1)

            def low_squares(k):
                nc.vector.tensor_tensor(s_l[:, k, 1, :], s_dd[:, k % 2, :], s_h[:, k, 1, :], ALU.subtract).then_inc(dd_done.sem, 1)

            def maximum(s, g, mh):
                dve.wait_ge(mix_mm.sem, mix_mm.done(2 * s + mh))
                nc.vector.tensor_reduce(mx[:, g % 2, mh:mh + 1], ps_a[:, mh, :], AX_X, ALU.max).then_inc(mx_done.sem, 1)

            def shift(s, g):
                c = slice(g % 2, g % 2 + 1)
                dve.wait_ge(mx_done.sem, mx_done.done(2 * s + 1))
                nc.vector.tensor_scalar(mxc[:, c], mx[:, g % 2, 0:1], mx[:, g % 2, 1:2], const_x[:], ALU.max, ALU.add
                                        ).then_inc(mxc_done.sem, 1)
                dve.wait_ge(mxc_done.sem, mxc_done.done(s))
                nc.vector.tensor_scalar(bias[:, c], mxc[:, c], -1 / MX, const[:], ALU.mult, ALU.add).then_inc(bias_done.sem, 1)

            def normalised(s, g):
                c = slice(g % 2, g % 2 + 1)
                dve.wait_ge(p_done.sem, p_done.done(2 * s + 1))
                nc.vector.tensor_tensor(total[:, c], sums[:, g % 2, 0:1], sums[:, g % 2, 1:2], ALU.add).then_inc(total_done.sem, 1)
                dve.wait_ge(total_done.sem, total_done.done(s))
                nc.vector.reciprocal(rden[:, c], total[:, c]).then_inc(rden_done.sem, 1)
                dve.wait_ge(rden_done.sem, rden_done.done(s))
                nc.vector.tensor_scalar(p[:, g % 2, :], p[:, g % 2, :], rden[:, c], None, ALU.mult).then_inc(pn_done.sem, 1)

            def weights_t(s, g, blk, first):
                dve.wait_ge(tr_mm.sem, tr_mm.done(s))
                if g == 0 and not first:
                    dve.wait_ge(pv_mm.sem, pv_mm.done(blk - 1))
                nc.vector.tensor_copy(pt[:, :, :, g * GS:(g + 1) * GS], ps_t[:].rearrange("p t (o n) -> p t o n", o=H)
                                      ).then_inc(pt_done.sem, 1)

            def residual(blk):
                dve.wait_ge(pj_mm.sem, pj_mm.done(blk))
                nc.vector.tensor_tensor(delta[:], ps_m[:, :, 0:C], b_proj[:], ALU.add).then_inc(delta_done.sem, 1)
                dve.wait_ge(delta_done.sem, delta_done.done(blk))
                nc.vector.tensor_tensor(hs[:, ds(blk, 1), :], hs[:, ds(blk, 1), :], delta[:], ALU.add).then_inc(h_done.sem, 1)

            def body(blk, first, last):
                for g in range(NG):
                    s = blk * NG + g
                    more = not (last and g == NG - 1)
                    k = 2 * ((g + 1) % 2)
                    maximum(s, g, 0)
                    if g or not first:
                        normalised(s - 1, (g - 1) % NG)
                    if more:
                        low_dots(2 * s + 2, k)
                    maximum(s, g, 1)
                    shift(s, g)
                    if more:
                        low_squares(k)
                    if g or not first:
                        weights_t(s - 1, (g - 1) % NG, blk, first)
                    if more:
                        low_dots(2 * s + 3, k + 1)
                        low_squares(k + 1)
                    if g == 4 and not first:
                        residual(blk - 1)

            for u in range(2):
                low_dots(u, u)
                low_squares(u)
            blocks(dve, body)
            normalised(NB * NG - 1, NG - 1)
            weights_t(NB * NG - 1, NG - 1, NB - 1, False)
            residual(NB - 1)
            dve.wait_ge(h_done.sem, h_done.done(NB - 1))

        @block.tensor
        def _(pe):
            d_mm.start(pe)
            g_mm.start(pe)
            mix_mm.start(pe)
            tr_mm.start(pe)
            pe.sem_inc(pv_mm.sem, 1)
            pe.wait_ge(pool_set.sem, 5)
            pe.wait_ge(set_up.sem, 1)
            for kind in range(3):
                last_mm = pe.matmul(ps_m[:, 0, 0:1], shifter[:, kind].rearrange("p o n -> p (o n)"), ones[:], start=(kind == 0),
                                    stop=(kind == 2))
            last_mm.then_inc(pv_mm.sem, 1)

            def scores(blk, g, mh, kind):
                u = 2 * (blk * NG + g) + mh
                if g % 4 == 0:
                    pe.wait_ge(qb_done.sem, qb_done.done(2 * blk + g // 4))
                if g == 0:
                    pe.wait_ge(k_in[kind, mh].sem, k_in[kind, mh].done(blk // NT))
                if kind:
                    pe.wait_ge(gg_done.sem, gg_done.freed(u, 1))
                else:
                    pe.wait_ge(dl_done.sem, dl_done.freed(u, 2))
                ps = ps_g[:] if kind else ps_d[:, mh, :]
                for part in range(2):
                    for pair in range(4):
                        last_mm = pe.matmul(ps[pair * 32:(pair + 1) * 32], q_bd[:, kind * 8 + part * 4 + pair, g, :],
                                            keys[:, kind, pair, mh * 512:(mh + 1) * 512], start=(part == 0),
                                            stop=(part == 1))
                last_mm.then_inc((g_mm if kind else d_mm).sem, 1)

            def mixed(s, g, mh):
                u = 2 * s + mh
                k = 2 * (g % 2) + mh
                pe.wait_ge(p_done.sem, p_done.freed(u, 2))
                for kind, low in enumerate((dl_done, dd_done)):
                    pe.wait_ge(low.sem, low.done(u))
                    pe.matmul(ps_a[:, mh, :], mix_h[:, kind], s_h[:, k, kind, :], start=(kind == 0), stop=False)
                    pe.matmul(ps_a[:, mh, :], mix_h[:, kind], s_l[:, k, kind, :], start=False, stop=False)
                    pe.matmul(ps_a[:, mh, :], mix_l[:, kind], s_h[:, k, kind, :], start=False, stop=False)
                pe.wait_ge(gg_done.sem, gg_done.done(u))
                pe.matmul(ps_a[:, mh, :], mixer[:, 2].rearrange("p o n -> p (o n)"), s_gg[:, k, :], start=False, stop=True
                          ).then_inc(mix_mm.sem, 1)

            def transposed(s, g):
                pe.wait_ge(pn_done.sem, pn_done.done(s))
                pe.wait_ge(pt_done.sem, pt_done.freed(s, 1))
                for t in range(NT):
                    last_mm = pe.transpose(ps_t[:, t, :], p[:, g % 2, t * P:(t + 1) * P], ident[:])
                last_mm.then_inc(tr_mm.sem, 1)

            def weighted(blk):
                pe.wait_ge(pt_done.sem, pt_done.done(blk * NG + NG - 1))
                pe.wait_ge(v_in.sem, v_in.done(blk // NT))
                pe.wait_ge(delta_done.sem, delta_done.freed(blk, 1))
                for t in range(NT):
                    for c in range(CK):
                        for o in range(4 * c, 4 * c + 4):
                            r = o % 4 * HD
                            last_mm = pe.matmul(ps_m[r:r + HD, 0, c * P:(c + 1) * P], v[:, t, o * HD:(o + 1) * HD], pt[:, t, o, :],
                                                start=(t == 0 and c == 0), stop=(t == NT - 1), skip_group_check=True)
                last_mm.then_inc(pv_mm.sem, 1)

            def projected(blk):
                pe.wait_ge(otc_done.sem, otc_done.done(blk))
                for c in range(CK):
                    last_mm = pe.matmul(ps_m[:, 0, 0:C], ot[:, c, :], w_proj[:, c, :], start=(c == 0), stop=(c == CK - 1))
                last_mm.then_inc(pj_mm.sem, 1)

            def body(blk, first, last):
                for g in range(NG):
                    s = blk * NG + g
                    ahead = (blk, g + 1) if g < NG - 1 else (blk + 1, 0)
                    more = not (last and g == NG - 1)
                    mixed(s, g, 0)
                    if g == 1 and not first:
                        weighted(blk - 1)
                    if more:
                        scores(*ahead, 0, 0)
                    mixed(s, g, 1)
                    if more:
                        scores(*ahead, 0, 1)
                        scores(*ahead, 1, 0)
                    if g or not first:
                        transposed(s - 1, (g - 1) % NG)
                    if more:
                        scores(*ahead, 1, 1)
                    if g == 3 and not first:
                        projected(blk - 1)

            for mh in range(2):
                for kind in range(2):
                    scores(0, 0, mh, kind)
            blocks(pe, body)
            transposed(NB * NG - 1, NG - 1)
            weighted(NB - 1)
            projected(NB - 1)


def experts(nc, a, hs, out):
    with ExitStack() as ctx:
        m = Maker(nc, ctx, "p4")
        NB = B * N // 512
        TB = 512 // P
        HT = F // P
        ident = m.sb("ident", [P, P])
        norm = m.sb("norm", [P, 2, CK])
        w_r = m.sb("w_r", [P, CK, E])
        b_r = m.sb("b_r", [P, E])
        b1 = m.sb("b1", [P, E, HT])
        b2 = m.sb("b2", [E, C])
        iota = m.sb("iota", [P, E])
        half = m.sb("half", [P, TB])
        eps = m.sb("eps", [P, TB])
        carrier = m.sb("carrier", [P, 128])
        stage = m.sb("stage", [P, 2, 2, 1024])
        w1 = m.sb("w1", [P, 2, E, CK, F], F16)
        w2 = m.sb("w2", [P, 2, E, HT, C], F16)
        hc = m.sb("hc", [P, TB, C])
        stats = m.sb("stats", [P, TB, 6])
        mv = m.sb("mv", [P, TB, 2])
        veps = m.sb("veps", [P, TB])
        rstd = m.sb("rstd", [P, TB])
        z = m.sb("z", [P, TB, C])
        xh = m.sb("xh", [P, TB, C])
        xf = m.sb("xf", [P, CK, 512])
        x_hi = m.sb("x_hi", [P, CK, 512], F16)
        x_lo = m.sb("x_lo", [P, CK, 512], F16)
        logit = m.sb("logit", [P, TB, E])
        top = m.sb("top", [P, TB, 8])
        idx = m.sb("idx", [P, TB, 8], mybir.dt.uint32)
        idxf = m.sb("idxf", [P, TB, 2])
        gap = m.sb("gap", [P, TB])
        th = m.sb("th", [P, TB])
        wt = m.sb("wt", [P, 2, TB])
        hot = m.sb("hot", [P, 2, TB, E])
        gate_next = m.sb("gate_next", [P, TB, E])
        gate = m.sb("gate", [P, TB, E])
        gate_t = m.sb("gate_t", [E, 512])
        g32 = m.sb("g32", [P, HT, 512])
        g_hi = m.sb("g_hi", [P, 2, HT, 512], F16)
        g_lo = m.sb("g_lo", [P, 2, HT, 512], F16)
        y = m.sb("y", [P, TB, C])
        o = m.sb("o", [P, TB, C])

        ps_h = [m.ps(f"ps_h{k}", [P, 512]) for k in range(4)]
        ps_y = [m.ps(f"ps_y{k}", [P, 512]) for k in range(2)]
        ps_x = m.ps("ps_x", [P, 512])
        ps_r = m.ps("ps_r", [P, 512])

        consts = m.count("consts", 16 * 7)
        w_in = [m.count(f"w_in{k}", 32) for k in range(2)]
        wp_in = [m.count(f"wp_in{k}", 32) for k in range(2)]
        w_hi_done = m.count("w_hi_done")
        w_done = m.count("w_done")
        wp_done = m.count("wp_done")
        wp_hi_done = m.count("wp_hi_done")
        pool_set = m.count("pool_set")
        hc_in = m.count("hc_in", 16)
        st_done = m.count("st_done")
        mv_done = m.count("mv_done")
        ve_done = m.count("ve_done")
        rstd_done = m.count("rstd_done")
        z_done = m.count("z_done")
        xh_done = m.count("xh_done", credit=1)
        xt_mm = m.count("xt_mm", credit=2)
        xf_done = m.count("xf_done")
        x_hi_done = m.count("x_hi_done")
        x_lo_done = m.count("x_lo_done", credit=1)
        r_mm = m.count("r_mm")
        logit_done = m.count("logit_done")
        top_done = m.count("top_done")
        idx_done = m.count("idx_done")
        gap_done = m.count("gap_done")
        th_done = m.count("th_done")
        g_step = m.count("g_step", 1)
        gate_done = m.count("gate_done")
        gt_mm = m.count("gt_mm")
        gt_done = m.count("gt_done", credit=1)
        gate_set = m.count("gate_set", credit=1)
        h_mm = m.count("h_mm", credit=1)
        g32_done = m.count("g32_done")
        gh_done = m.count("gh_done", credit=4)
        gl_done = m.count("gl_done", credit=4)
        y_mm = m.count("y_mm", credit=8)
        acc_done = m.count("acc_done", credit=2)
        stored = m.count("stored", 16, credit=1)

        YU = TB * (E + 1)

        block = ctx.enter_context(nc.Block())

        def blocks(eng, body):
            with eng.Fori(0, NB - 1) as blk:
                body(blk, False)
            body(NB - 1, True)

        def load_weights(eng, e):
            k = (w_in if e < 2 else wp_in)[e % 2]
            eng.dma_start(stage[:, e % 2, 0], a["w1"][:, e]).then_inc(k.sem, 16)
            eng.dma_start(stage[:, e % 2, 1], a["w2"][:, e]).then_inc(k.sem, 16)

        def wait_parts(eng, e):
            k, n = (w_done, e) if e < 2 else (wp_done, e - 2)
            eng.wait_ge(k.sem, k.done(n))

        @block.sync
        def _(sp):
            stored.start(sp)
            for tile, name in ((ident, "ident"), (norm, "norm"), (w_r, "w_r"), (b_r, "b_r"), (b1, "b1"), (b2, "b2"),
                               (iota, "iota")):
                sp.dma_start(tile[:], a[name]).then_inc(consts.sem, 16)
            sp.dma_start(hc[:], hs[:, 0:TB, :]).then_inc(hc_in.sem, 16)
            for e in range(2):
                load_weights(sp, e)

            def body(blk, last):
                if not last:
                    sp.wait_ge(acc_done.sem, acc_done.done(blk * YU + (TB - 1)))
                    sp.dma_start(hc[:], hs[:, ds(blk * TB + TB, TB), :]).then_inc(hc_in.sem, 16)
                sp.wait_ge(acc_done.sem, acc_done.done(blk * YU + (YU - 1)))
                sp.dma_start(out[ds(blk * TB, TB)].rearrange("t p c -> p t c"), o[:]).then_inc(stored.sem, 16)

            blocks(sp, body)
            sp.wait_ge(stored.sem, stored.done(NB - 1))

        @block.gpsimd
        def _(pool):
            nc.gpsimd.memset(half[:], -0.5).then_inc(pool_set.sem, 1)
            nc.gpsimd.memset(eps[:], EPS).then_inc(pool_set.sem, 1)
            nc.gpsimd.memset(carrier[:], 1.0).then_inc(pool_set.sem, 1)
            pool.wait_ge(pool_set.sem, 3)

            def rstds(n):
                pool.wait_ge(mv_done.sem, mv_done.done(n))
                nc.gpsimd.tensor_tensor(veps[:], mv[:, :, 1], eps[:], ALU.add).then_inc(ve_done.sem, 1)
                pool.wait_ge(ve_done.sem, ve_done.done(n))
                nc.gpsimd.tensor_tensor(rstd[:], veps[:], half[:], ALU.pow).then_inc(rstd_done.sem, 1)

            def parts(e):
                pool.wait_ge(wp_in[e % 2].sem, wp_in[e % 2].done(e // 2 - 1))
                for k, w in enumerate((w1, w2)):
                    last = nc.gpsimd.tensor_tensor(w[:, 0, e].rearrange("p c n -> p (c n)"), stage[:, e % 2, k],
                                                   carrier[:, 0:1].broadcast_to([P, 1024]), ALU.mult)
                last.then_inc(wp_hi_done.sem, 1)
                pool.wait_ge(wp_hi_done.sem, wp_hi_done.done(e - 2))
                for k, w in enumerate((w1, w2)):
                    last = nc.gpsimd.tensor_tensor(w[:, 1, e].rearrange("p c n -> p (c n)"), stage[:, e % 2, k],
                                                   w[:, 0, e].rearrange("p c n -> p (c n)"), ALU.subtract)
                last.then_inc(wp_done.sem, 1)
                if e + 2 < E:
                    pool.wait_ge(wp_done.sem, wp_done.done(e - 2))
                    load_weights(pool, e + 2)

            rstds(0)
            rstds(1)
            for e in range(2):
                wait_parts(pool, e)
                load_weights(pool, e + 2)
            parts(2)
            parts(3)
            rstds(2)
            parts(4)
            rstds(3)
            for e in range(5, E):
                parts(e)
            with pool.Fori(4, 2 * NB) as n:
                rstds(n)

        @block.scalar
        def _(act):
            gt_done.start(act)
            gh_done.start(act)

            def scaled(blk, c):
                act.wait_ge(xt_mm.sem, xt_mm.done(2 * blk + c))
                if c == 0:
                    act.wait_ge(x_lo_done.sem, x_lo_done.freed(blk, 1))
                nc.scalar.activation(xf[:, c, :], ps_x[:], ACT.Identity, bias=norm[:, 1, c:c + 1],
                                     scale=norm[:, 0, c:c + 1]).then_inc(xf_done.sem, 1)

            def tanh(blk):
                act.wait_ge(gap_done.sem, gap_done.done(blk))
                nc.scalar.activation(th[:], gap[:], ACT.Tanh, scale=0.5).then_inc(th_done.sem, 1)

            def gates_t(blk):
                act.wait_ge(gt_mm.sem, gt_mm.done(blk))
                nc.scalar.copy(gate_t[:], ps_x[0:E, :]).then_inc(gt_done.sem, 1)

            def high_part(blk):
                act.wait_ge(xf_done.sem, xf_done.done(2 * blk + 1))
                act.wait_ge(h_mm.sem, h_mm.freed(blk * (4 * E), 1))
                nc.scalar.copy(x_hi[:], xf[:]).then_inc(x_hi_done.sem, 1)

            steps = {3: lambda blk: scaled(blk, 0), 4: lambda blk: scaled(blk, 1), 5: tanh, 7: lambda blk: (high_part(blk), gates_t(blk))}

            def hidden(blk, e):
                for t in range(HT):
                    u = blk * (4 * E) + (4 * e + t)
                    act.wait_ge(h_mm.sem, h_mm.done(u))
                    act.wait_ge(gl_done.sem, gl_done.freed(u, 4))
                    nc.scalar.activation(g32[:, t, :], ps_h[t][:], ACT.Gelu, bias=b1[:, e, t:t + 1]).then_inc(g32_done.sem, 1)
                    act.wait_ge(y_mm.sem, y_mm.done(blk * YU + (4 * e - 1 if e > 1 else 4 * e - 5)))
                    nc.scalar.activation(g_hi[:, e % 2, t, :], ps_h[t][:], ACT.Gelu, bias=b1[:, e, t:t + 1]
                                         ).then_inc(gh_done.sem, 1)

            for e in range(2):
                act.wait_ge(w_in[e].sem, w_in[e].done(0))
                nc.scalar.copy(w1[:, 0, e].rearrange("p c n -> p (c n)"), stage[:, e % 2, 0])
                nc.scalar.copy(w2[:, 0, e].rearrange("p c n -> p (c n)"), stage[:, e % 2, 1]).then_inc(w_hi_done.sem, 1)
            act.wait_ge(consts.sem, consts.done(0))
            scaled(0, 0)
            scaled(0, 1)
            high_part(0)
            tanh(0)
            gates_t(0)

            def body(blk, last):
                hidden(blk, 0)
                for e in range(E):
                    if e < E - 1:
                        hidden(blk, e + 1)
                    if not last and e in steps:
                        steps[e](blk + 1)

            blocks(act, body)

        @block.vector
        def _(dve):
            for k in (xh_done, x_lo_done, gate_set, gl_done, acc_done):
                k.start(dve)

            held = [0]

            def hold(k, value):
                dve.wait_ge(k.sem, value)
                held[0] += 1
                nc.vector.tensor_tensor(carrier[:, held[0]:held[0] + 1], carrier[:, 0:1], carrier[:, 0:1], ALU.mult)

            def moments(n, src):
                for t in range(TB):
                    last = nc.vector.bn_stats(stats[:, t, :], src[:, t, :])
                last.then_inc(st_done.sem, 1)
                hold(st_done, st_done.done(n))
                for t in range(TB):
                    last = nc.vector.bn_aggr(mv[:, t, :], stats[:, t, :])
                last.then_inc(mv_done.sem, 1)

            def centred(n, src, dst, done):
                hold(rstd_done, rstd_done.done(n))
                for t in range(TB):
                    last = nc.vector.tensor_scalar(dst[:, t, :], src[:, t, :], mv[:, t, 0:1], rstd[:, t:t + 1],
                                                   ALU.subtract, ALU.mult)
                last.then_inc(done.sem, 1)

            def first_moments(blk):
                hold(hc_in, hc_in.done(blk))
                hold(xh_done, xh_done.freed(blk, 1))
                moments(2 * blk, hc)

            def second_moments(blk):
                centred(2 * blk, hc, z, z_done)
                hold(z_done, z_done.done(blk))
                moments(2 * blk + 1, z)

            def normalised(blk):
                hold(xt_mm, xt_mm.freed(2 * blk + 1, 2))
                centred(2 * blk + 1, z, xh, xh_done)

            def best(blk):
                hold(r_mm, r_mm.done(blk))
                nc.vector.tensor_tensor(logit[:], ps_r[:, 0:TB * E].rearrange("p (t e) -> p t e", t=TB),
                                        b_r[:].unsqueeze(1).broadcast_to([P, TB, E]), ALU.add).then_inc(logit_done.sem, 1)
                hold(logit_done, logit_done.done(blk))
                for t in range(TB):
                    last = nc.vector.max(top[:, t, :], logit[:, t, :])
                last.then_inc(top_done.sem, 1)
                hold(top_done, top_done.done(blk))
                for t in range(TB):
                    last = nc.vector.max_index(idx[:, t, :], top[:, t, :], logit[:, t, :])
                last.then_inc(idx_done.sem, 1)
                nc.vector.tensor_tensor(gap[:], top[:, :, 1], top[:, :, 0], ALU.subtract).then_inc(gap_done.sem, 1)
                hold(idx_done, idx_done.done(blk))
                nc.vector.tensor_copy(idxf[:], idx[:, :, 0:2]).then_inc(g_step.sem, 1)

            def gates(blk):
                hold(th_done, th_done.done(blk))
                nc.vector.tensor_scalar(wt[:, 0], th[:], -0.5, 0.5, ALU.mult, ALU.add)
                nc.vector.tensor_scalar(wt[:, 1], th[:], 0.5, 0.5, ALU.mult, ALU.add).then_inc(g_step.sem, 1)
                hold(g_step, g_step.done(4 * blk + 1))
                for k in range(2):
                    last = nc.vector.tensor_tensor(hot[:, k], iota[:].unsqueeze(1).broadcast_to([P, TB, E]),
                                                   idxf[:, :, k:k + 1].broadcast_to([P, TB, E]), ALU.is_equal)
                last.then_inc(g_step.sem, 1)
                hold(g_step, g_step.done(4 * blk + 2))
                for k in range(2):
                    last = nc.vector.tensor_tensor(hot[:, k], hot[:, k], wt[:, k].unsqueeze(2).broadcast_to([P, TB, E]), ALU.mult)
                last.then_inc(g_step.sem, 1)
                hold(g_step, g_step.done(4 * blk + 3))
                hold(gate_set, gate_set.freed(blk, 1))
                nc.vector.tensor_tensor(gate_next[:], hot[:, 0], hot[:, 1], ALU.add).then_inc(gate_done.sem, 1)

            def low_part(blk):
                dve.wait_ge(x_hi_done.sem, x_hi_done.done(blk))
                nc.vector.tensor_tensor(x_lo[:], xf[:], x_hi[:], ALU.subtract).then_inc(x_lo_done.sem, 1)

            steps = {0: first_moments, 1: second_moments, 2: normalised, 5: best, 6: gates}

            def low(blk, e):
                for t in range(HT):
                    u = blk * (4 * E) + (4 * e + t)
                    dve.wait_ge(gh_done.sem, gh_done.done(u))
                    nc.vector.tensor_tensor(g_lo[:, e % 2, t, :], g32[:, t, :], g_hi[:, e % 2, t, :],
                                            ALU.subtract).then_inc(gl_done.sem, 1)

            def summed(blk, e):
                for t in range(TB):
                    u = blk * YU + (4 * (e + 1) + t)
                    dve.wait_ge(y_mm.sem, y_mm.done(u))
                    if e < 0:
                        nc.vector.tensor_tensor(y[:, t, :], ps_y[t % 2][:, 0:C], hc[:, t, :], ALU.add).then_inc(acc_done.sem, 1)
                        continue
                    if e == E - 1 and t == 0:
                        dve.wait_ge(stored.sem, stored.freed(blk, 1))
                    nc.vector.scalar_tensor_tensor((y, o)[e == E - 1][:, t, :], ps_y[t % 2][:, 0:C], gate[:, t, e:e + 1], y[:, t, :],
                                                   ALU.mult, ALU.add).then_inc(acc_done.sem, 1)

            dve.wait_ge(consts.sem, consts.done(0))
            dve.wait_ge(pool_set.sem, 3)
            for k in (0, 1, 2):
                steps[k](0)
            for e in range(2):
                dve.wait_ge(w_hi_done.sem, e + 1)
                nc.vector.tensor_tensor(w1[:, 1, e].rearrange("p c n -> p (c n)"), stage[:, e, 0],
                                        w1[:, 0, e].rearrange("p c n -> p (c n)"), ALU.subtract)
                nc.vector.tensor_tensor(w2[:, 1, e].rearrange("p c n -> p (c n)"), stage[:, e, 1],
                                        w2[:, 0, e].rearrange("p c n -> p (c n)"), ALU.subtract).then_inc(w_done.sem, 1)
            low_part(0)
            best(0)
            gates(0)

            def body(blk, last):
                hold(gate_done, gate_done.done(blk))
                hold(acc_done, acc_done.done(blk * YU - 1))
                nc.vector.tensor_copy(gate[:], gate_next[:]).then_inc(gate_set.sem, 1)
                hold(gate_set, gate_set.done(blk))
                summed(blk, -1)
                low(blk, 0)
                for e in range(E):
                    if e < E - 1:
                        low(blk, e + 1)
                    elif not last:
                        low_part(blk + 1)
                    summed(blk, e)
                    if not last and e in steps:
                        steps[e](blk + 1)

            blocks(dve, body)

        @block.tensor
        def _(pe):
            h_mm.start(pe)
            xt_mm.start(pe)
            y_mm.start(pe)

            def turned(blk, c):
                pe.wait_ge(xh_done.sem, xh_done.done(blk))
                if c == 0:
                    pe.wait_ge(gt_done.sem, gt_done.freed(blk, 1))
                else:
                    pe.wait_ge(xf_done.sem, xf_done.done(2 * blk))
                for t in range(TB):
                    last = pe.transpose(ps_x[:, t * P:(t + 1) * P], xh[:, t, c * P:(c + 1) * P], ident[:])
                last.then_inc(xt_mm.sem, 1)

            def routed(blk):
                pe.wait_ge(xf_done.sem, xf_done.done(2 * blk + 1))
                for t in range(TB):
                    for c in range(CK):
                        last = pe.matmul(ps_r[:, t * E:(t + 1) * E], xf[:, c, t * P:(t + 1) * P], w_r[:, c, :],
                                         start=(t == 0 and c == 0), stop=(c == CK - 1), skip_group_check=True)
                last.then_inc(r_mm.sem, 1)

            def gates_t(blk):
                pe.wait_ge(gate_done.sem, gate_done.done(blk))
                for t in range(TB):
                    last = pe.transpose(ps_x[0:E, t * P:(t + 1) * P], gate_next[:, t, :], ident[:])
                last.then_inc(gt_mm.sem, 1)

            steps = {3: lambda blk: turned(blk, 0), 4: lambda blk: turned(blk, 1), 5: routed, 7: gates_t}

            def hidden(blk, e):
                if not isinstance(blk, int) or blk == 0:
                    wait_parts(pe, e)
                for t in range(HT):
                    u = blk * (4 * E) + (4 * e + t)
                    pe.wait_ge(gh_done.sem, gh_done.freed(u, 4))
                    n = 0
                    for c in range(CK):
                        for wp, x in ((0, x_hi), (0, x_lo), (1, x_hi)):
                            last = pe.matmul(ps_h[t][:], w1[:, wp, e, c, t * P:(t + 1) * P], x[:, c, :], start=(n == 0),
                                             stop=(n == 3 * CK - 1))
                            n += 1
                    last.then_inc(h_mm.sem, 1)

            def outputs(blk, e):
                for t in range(TB):
                    u = blk * YU + (4 * (e + 1) + t)
                    pe.wait_ge(acc_done.sem, acc_done.freed(u, 2))
                    if e < 0:
                        pe.matmul(ps_y[t % 2][:, 0:C], gate_t[:, t * P:(t + 1) * P], b2[:], start=True, stop=True
                                  ).then_inc(y_mm.sem, 1)
                        continue
                    if t == 0:
                        pe.wait_ge(gl_done.sem, gl_done.done(blk * (4 * E) + (4 * e + 3)))
                    n = 0
                    for k in range(HT):
                        for g, wp in ((g_hi, 0), (g_hi, 1), (g_lo, 0)):
                            last = pe.matmul(ps_y[t % 2][:, 0:C], g[:, e % 2, k, t * P:(t + 1) * P], w2[:, wp, e, k, :],
                                             start=(n == 0), stop=(n == 3 * HT - 1))
                            n += 1
                    last.then_inc(y_mm.sem, 1)

            pe.wait_ge(consts.sem, consts.done(0))
            for k in sorted(steps):
                steps[k](0)

            def body(blk, last):
                pe.wait_ge(x_lo_done.sem, x_lo_done.done(blk))
                hidden(blk, 0)
                pe.wait_ge(gt_done.sem, gt_done.done(blk))
                outputs(blk, -1)
                for e in range(E):
                    if e < E - 1:
                        hidden(blk, e + 1)
                    outputs(blk, e)
                    if not last and e in steps:
                        steps[e](blk + 1)

            blocks(pe, body)


def program(nc, a, out):
    with ExitStack() as ctx:
        m = Maker(nc, ctx, "all")
        hs = m.sb("h", [P, TILES, C])

        def dram(name, shape, dt=F32):
            return nc.dram_tensor(name, shape, dt, kind="Internal").ap()

        v_d = dram("v_d", [B, P, NT, C])
        top_d = dram("top_d", [B, HD, 2 * C])
        gram_d = dram("gram_d", [B * 4 * P, HD])
        rt_d = dram("rt_d", [P * HD, HD])
        parts_d = dram("parts_d", [B, 2 * HD, 2, 2, 2, 4, N], F16)
        dr = {
            "v": v_d, "top": top_d,
            "gram": gram_d.rearrange("(b g p) j -> b p g j", b=B, g=4),
            "gram_m": gram_d.rearrange("(m i) j -> m i j", m=P),
            "top_m": top_d.rearrange("b n (m d) -> b m n d", d=HD),
            "rt_m": rt_d.rearrange("(m i) j -> m i j", m=P),
            "rt": rt_d.rearrange("(b g h k) i -> b h k g i", b=B, g=4, h=4),
            "parts_st": parts_d,
            "queries": parts_d.rearrange("b x k p r (g y) n -> b x y (k p r g) n", y=2)[:, :, 0],
            "keys": parts_d.rearrange("b x k p r (g y) n -> b x y k p (r g) n", y=2)[:, :, 1],
        }
        embed_and_project(nc, a, dr, hs)
        orthonormal_operands(nc, a, dr)
        attention(nc, a, dr, hs)
        experts(nc, a, hs, out.rearrange("b (t p) c -> (b t) p c", p=P))


def kernel(**inputs):
    import numpy as np
    import concourse.bacc as bacc
    from concourse.bass_utils import run_bass_kernel_spmd as run

    def rows(v, n=P):
        return np.broadcast_to(v.reshape(1, -1), (n, v.size))

    i = {k.replace("L0_", ""): np.asarray(v) for k, v in inputs.items()}
    x = i["x"].reshape(B, 32, 7, 32, 7).transpose(0, 2, 4, 1, 3).reshape(B, PD, N)
    laid = {
        "pat": x,
        "tok_w": i["tok_W"].T,
        "pos": i["tok_pos"].reshape(NT, P, C).transpose(1, 0, 2),
        "tok_b": rows(i["tok_b"]),
        "w_qkv": i["attn_w_qkv"].T.reshape(CK, P, 3 * C).transpose(1, 0, 2),
        "b_qkv": rows(i["attn_b_qkv"]),
        "ident": np.eye(P, dtype=np.float32),
    }
    heads = [g * 4 + pr * 2 + hp for pr in range(2) for g in range(2) for hp in range(2)]
    kinds = lambda v: np.repeat(v.reshape(3, H)[:, heads].T, GS, axis=0)
    laid |= {
        "w_proj": i["attn_w_proj"].T.reshape(CK, P, C).transpose(1, 0, 2),
        "b_proj": rows(i["attn_b_proj"]).reshape(P, 1, C),
        "mix_w": np.repeat(i["attn_conv_w"].reshape(H, 3, H)[:, :, heads].transpose(2, 1, 0), GS, axis=0),
        "bn": np.stack([kinds(i["attn_bn_" + k]) for k in ("gamma", "beta", "mean", "var")]
                       + [rows(np.stack([i["attn_scale"], i["attn_riem_scale"], i["attn_grassman_scale"]]))], axis=1),
        "mask": np.tile(np.eye(GS, dtype=np.float32), (H, 1)),
        "conv_b": np.repeat(i["attn_conv_b"], GS).reshape(P, 1),
    }
    laid |= {
        "norm": np.stack([i["ffn_gamma"].reshape(CK, P).T, i["ffn_beta"].reshape(CK, P).T], axis=1),
        "w_r": i["ffn_Wr"].reshape(CK, P, E).transpose(1, 0, 2),
        "b_r": rows(i["ffn_br"]),
        "b1": i["ffn_b1"].reshape(E, F // P, P).transpose(2, 0, 1),
        "b2": i["ffn_b2"],
        "iota": rows(np.arange(E, dtype=np.float32)),
        "w1": i["ffn_W1"].reshape(E, CK, P, F).transpose(2, 0, 1, 3).reshape(P, E, CK * F),
        "w2": i["ffn_W2"].reshape(E, F // P, P, C).transpose(2, 0, 1, 3).reshape(P, E, F // P * C),
    }
    nc = bacc.Bacc("TRN2", target_bir_lowering=False, num_devices=1)
    arrays, aps = {}, {}
    for name, v in laid.items():
        arrays[f"in_{name}"] = np.ascontiguousarray(v)
        aps[name] = nc.dram_tensor(f"in_{name}", v.shape, mybir.dt.from_np(v.dtype), kind="ExternalInput").ap()
    out = nc.dram_tensor("out_0", (B, N, C), F32, kind="ExternalOutput").ap()
    program(nc, aps, out)
    r = run(nc, [arrays], core_ids=[0])
    return r.results[0]["out_0"]
```
